# Optimizing a Trainium2 kernel written in Bass

```python
import numpy as np
import jax
import jax.numpy as jnp

def _softmax(x, axis=-1):
    return jax.nn.softmax(x, axis=axis)

def _gelu(x):
    return jax.nn.gelu(x, approximate=True)

def _silu(x):
    return jax.nn.silu(x)

def _sigmoid(x):
    return jax.nn.sigmoid(x)

def _layernorm(x, axis=-1, eps=1e-05):
    m = jnp.mean(x, axis=axis, keepdims=True)
    v = jnp.var(x, axis=axis, keepdims=True)
    return (x - m) / jnp.sqrt(v + eps)

def _scatter_add(tgt, idx, src, axis=0):
    return tgt.at[idx].add(src)

def _segment_sum(src, seg, n):
    return jax.ops.segment_sum(src, seg, n)
kernel_name = 'mk_cond_resid_d4_seqx_r4_86da14'

def setup_inputs(seed: int=0):
    np.random.seed(seed)
    _w = jnp.asarray

    def _rec_inputs():
        import jax
        import jax.numpy as jnp
        _rk = jax.random.key(seed)
        x = -7.109e-05 + 0.9999 * jax.random.normal(jax.random.fold_in(_rk, 1), (64, 64, 512), jnp.float32)
        _lenS = 64 - jax.random.randint(jax.random.fold_in(_rk, 7), (64,), 0, max(1, 64 // 4) + 1, jnp.int32)
        _lenS2 = 64 - jax.random.randint(jax.random.fold_in(_rk, 8), (64,), 0, max(1, 64 // 4) + 1, jnp.int32)
        itok_B_1_198 = jax.random.randint(jax.random.fold_in(_rk, 11), (64,), 1, 199, jnp.int32)
        itok_B_0_3 = jax.random.randint(jax.random.fold_in(_rk, 12), (64,), 0, 4, jnp.int32)
        itok_Bx257_0_4111 = jax.random.randint(jax.random.fold_in(_rk, 13), (64, 257), 0, 1028, jnp.int32)
        itok_B_37_3939 = jax.random.randint(jax.random.fold_in(_rk, 14), (64,), 37, 985, jnp.int32)
        itok_B_0_6 = jax.random.randint(jax.random.fold_in(_rk, 15), (64,), 0, 7, jnp.int32)
        return (x, itok_B_1_198, itok_B_0_3, itok_Bx257_0_4111, itok_B_37_3939, itok_B_0_6)
    x, itok_B_1_198, itok_B_0_3, itok_Bx257_0_4111, itok_B_37_3939, itok_B_0_6 = _rec_inputs()

    def _L0_cond_setup():
        import jax, jax.numpy as jnp
        import numpy as np
        B, C, T = (128, 64, 512)
        S, D = (200, 64)
        key = jax.random.key(seed)
        k1, k2, k3 = jax.random.split(key, 3)
        x = jax.random.normal(k1, (B, C, T), dtype=jnp.float32)
        conditions = jax.random.randint(k2, (B,), 0, S, dtype=jnp.int64)
        weights = jax.random.normal(k3, (S, C, D), dtype=jnp.float32) / jnp.sqrt(jnp.float32(C))
        return {'x': x, 'conditions': conditions, 'weights': weights}
    _L0_cond_all = _L0_cond_setup()
    _L0_cond_in = {k: v for k, v in _L0_cond_all.items() if k in ('weights',)}
    del _L0_cond_all

    def _L1_cond_setup():
        import jax, jax.numpy as jnp
        import numpy as np
        B, S, D_IN, D_OUT, R, E = (8, 512, 512, 512, 16, 4)
        key = jax.random.key(seed)
        ks = jax.random.split(key, 7)
        x = jax.random.normal(ks[0], (B, S, D_IN), dtype=jnp.float32)
        W_base = jax.random.normal(ks[1], (D_OUT, D_IN), dtype=jnp.float32) * 0.02
        Wt = jax.random.normal(ks[2], (D_IN, D_IN), dtype=jnp.float32) * 0.02
        A = jax.random.normal(ks[3], (E, R, D_IN), dtype=jnp.float32) * 0.02
        B_w = jax.random.normal(ks[4], (E, D_OUT, R), dtype=jnp.float32) * 0.02
        Wp = jax.random.normal(ks[5], (D_OUT, D_OUT), dtype=jnp.float32) * 0.02
        scaling = jnp.ones((E,), dtype=jnp.float32)
        adapter_idx = jax.random.randint(ks[6], (B,), 0, E)
        return {'x': x, 'W_base': W_base, 'Wt': Wt, 'A': A, 'B_w': B_w, 'Wp': Wp, 'scaling': scaling, 'adapter_idx': adapter_idx}
    _L1_cond_all = _L1_cond_setup()
    _L1_cond_in = {k: v for k, v in _L1_cond_all.items() if k in ('W_base', 'Wt', 'A', 'B_w', 'Wp', 'scaling')}
    del _L1_cond_all

    def _L2_cond_setup():
        import jax, jax.numpy as jnp
        import numpy as np
        H, G, HD = (8, 4, 64)
        GSZ = H // G
        BLOCK = 16
        WINDOW = 256
        SCALE = 256.0 ** (-0.5)
        EPS = 1e-06
        THETA = 10000.0
        B, T, D = (16, 4, 512)
        NBLK = 257

        def _rms(x, scale):
            var = jnp.mean(x * x, axis=-1, keepdims=True)
            return x * jax.lax.rsqrt(var + EPS) * (1.0 + scale)

        def _rope(x, pos):
            half = HD // 2
            inv = 1.0 / THETA ** (jnp.arange(half, dtype=jnp.float32) / half)
            ang = pos[:, :, None].astype(jnp.float32) * inv
            cos = jnp.cos(ang)[:, None, :, :]
            sin = jnp.sin(ang)[:, None, :, :]
            x1, x2 = (x[..., :half], x[..., half:])
            return jnp.concatenate([x1 * cos - x2 * sin, x2 * cos + x1 * sin], axis=-1)
        key = jax.random.key(seed)
        ks = jax.random.split(key, 10)
        inv_d = 1.0 / np.sqrt(D)
        return {'x': jax.random.normal(ks[0], (B, T, D), jnp.float32), 'Wq': jax.random.normal(ks[1], (H * HD, D), jnp.float32) * inv_d, 'Wk': jax.random.normal(ks[2], (G * HD, D), jnp.float32) * inv_d, 'Wv': jax.random.normal(ks[3], (G * HD, D), jnp.float32) * inv_d, 'Wo': jax.random.normal(ks[4], (D, H * HD), jnp.float32) * inv_d, 'q_norm_scale': jax.random.normal(ks[5], (HD,), jnp.float32) * 0.02, 'k_norm_scale': jax.random.normal(ks[6], (HD,), jnp.float32) * 0.02, 'k_blocks': jax.random.normal(ks[7], (B * NBLK, G, BLOCK, HD), jnp.float32), 'v_blocks': jax.random.normal(ks[8], (B * NBLK, G, BLOCK, HD), jnp.float32), 'block_tables': jnp.arange(B * NBLK, dtype=jnp.int32).reshape(B, NBLK), 'kv_lens': jax.random.randint(ks[9], (B,), 0, 1024, dtype=jnp.int32)}
    _L2_cond_all = _L2_cond_setup()
    _L2_cond_in = {k: v for k, v in _L2_cond_all.items() if k in ('Wq', 'Wk', 'Wv', 'Wo', 'q_norm_scale', 'k_norm_scale', 'k_blocks', 'v_blocks')}
    del _L2_cond_all

    def _L3_cond_setup():
        import jax, jax.numpy as jnp
        import numpy as np
        B, T, D_IN, D_OUT = (16, 512, 512, 512)
        N_ADAPTERS, RANK = (8, 16)
        key = jax.random.key(seed)
        k_x, k_w, k_a, k_b, k_s, k_idx = jax.random.split(key, 6)
        x = jax.random.normal(k_x, (B, T, D_IN), dtype=jnp.float32)
        W = jax.random.normal(k_w, (D_OUT, D_IN), dtype=jnp.float32) * (1.0 / np.sqrt(D_IN))
        A = jax.random.normal(k_a, (N_ADAPTERS, RANK, D_IN), dtype=jnp.float32) * 0.02
        Bm = jax.random.normal(k_b, (N_ADAPTERS, D_OUT, RANK), dtype=jnp.float32) * 0.02
        scalings = jnp.ones((N_ADAPTERS,), dtype=jnp.float32)
        adapter_idx = jax.random.randint(k_idx, (B,), 0, N_ADAPTERS, dtype=jnp.int32)
        return {'x': x, 'W': W, 'A': A, 'Bm': Bm, 'scalings': scalings, 'adapter_idx': adapter_idx}
    _L3_cond_all = _L3_cond_setup()
    _L3_cond_in = {k: v for k, v in _L3_cond_all.items() if k in ('W', 'A', 'Bm', 'scalings')}
    del _L3_cond_all
    return {'x': x, 'itok_B_1_198': itok_B_1_198, 'itok_B_0_3': itok_B_0_3, 'itok_Bx257_0_4111': itok_Bx257_0_4111, 'itok_B_37_3939': itok_B_37_3939, 'itok_B_0_6': itok_B_0_6, 'L0_cond_weights': _L0_cond_in['weights'], 'L1_cond_W_base': _L1_cond_in['W_base'], 'L1_cond_Wt': _L1_cond_in['Wt'], 'L1_cond_A': _L1_cond_in['A'], 'L1_cond_B_w': _L1_cond_in['B_w'], 'L1_cond_Wp': _L1_cond_in['Wp'], 'L1_cond_scaling': _L1_cond_in['scaling'], 'L2_cond_Wq': _L2_cond_in['Wq'], 'L2_cond_Wk': _L2_cond_in['Wk'], 'L2_cond_Wv': _L2_cond_in['Wv'], 'L2_cond_Wo': _L2_cond_in['Wo'], 'L2_cond_q_norm_scale': _L2_cond_in['q_norm_scale'], 'L2_cond_k_norm_scale': _L2_cond_in['k_norm_scale'], 'L2_cond_k_blocks': _L2_cond_in['k_blocks'], 'L2_cond_v_blocks': _L2_cond_in['v_blocks'], 'L3_cond_W': _L3_cond_in['W'], 'L3_cond_A': _L3_cond_in['A'], 'L3_cond_Bm': _L3_cond_in['Bm'], 'L3_cond_scalings': _L3_cond_in['scalings']}

def reference(x, itok_B_1_198, itok_B_0_3, itok_Bx257_0_4111, itok_B_37_3939, itok_B_0_6, L0_cond_weights, L1_cond_W_base, L1_cond_Wt, L1_cond_A, L1_cond_B_w, L1_cond_Wp, L1_cond_scaling, L2_cond_Wq, L2_cond_Wk, L2_cond_Wv, L2_cond_Wo, L2_cond_q_norm_scale, L2_cond_k_norm_scale, L2_cond_k_blocks, L2_cond_v_blocks, L3_cond_W, L3_cond_A, L3_cond_Bm, L3_cond_scalings):
    import jax
    import jax.numpy as jnp

    def _L0_cond_ref(x, conditions, weights):
        import jax, jax.numpy as jnp
        import numpy as np
        B, C, T = (128, 64, 512)
        S, D = (200, 64)
        w = weights[conditions]
        return jnp.einsum('bct,bcd->bdt', x, w)

    def _L1_cond_ref(x, W_base, Wt, A, B_w, Wp, scaling, adapter_idx):
        import jax, jax.numpy as jnp
        import numpy as np
        B, S, D_IN, D_OUT, R, E = (8, 512, 512, 512, 16, 4)
        base = jnp.einsum('bsi,oi->bso', x, W_base)
        h = jnp.einsum('bsi,ji->bsj', x, Wt)
        Ab = A[adapter_idx]
        Bb = B_w[adapter_idx]
        sc = scaling[adapter_idx]
        z = jnp.einsum('bsj,brj->bsr', h, Ab)
        l = jnp.einsum('bsr,bor->bso', z, Bb)
        lora_out = jnp.einsum('bso,po->bsp', l, Wp) * sc[:, None, None]
        return base + lora_out

    def _L2_cond_ref(x, Wq, Wk, Wv, Wo, q_norm_scale, k_norm_scale, k_blocks, v_blocks, block_tables, kv_lens):
        import jax, jax.numpy as jnp
        import numpy as np
        H, G, HD = (8, 4, 64)
        GSZ = H // G
        BLOCK = 16
        WINDOW = 256
        SCALE = 256.0 ** (-0.5)
        EPS = 1e-06
        THETA = 10000.0
        B, T, D = (16, 4, 512)
        NBLK = 257

        def _rms(x, scale):
            var = jnp.mean(x * x, axis=-1, keepdims=True)
            return x * jax.lax.rsqrt(var + EPS) * (1.0 + scale)

        def _rope(x, pos):
            half = HD // 2
            inv = 1.0 / THETA ** (jnp.arange(half, dtype=jnp.float32) / half)
            ang = pos[:, :, None].astype(jnp.float32) * inv
            cos = jnp.cos(ang)[:, None, :, :]
            sin = jnp.sin(ang)[:, None, :, :]
            x1, x2 = (x[..., :half], x[..., half:])
            return jnp.concatenate([x1 * cos - x2 * sin, x2 * cos + x1 * sin], axis=-1)
        Bx, Tx, _ = x.shape
        q = jnp.einsum('btd,od->bto', x, Wq).reshape(Bx, Tx, H, HD).transpose(0, 2, 1, 3)
        k = jnp.einsum('btd,od->bto', x, Wk).reshape(Bx, Tx, G, HD).transpose(0, 2, 1, 3)
        v = jnp.einsum('btd,od->bto', x, Wv).reshape(Bx, Tx, G, HD).transpose(0, 2, 1, 3)
        q = _rms(q, q_norm_scale)
        k = _rms(k, k_norm_scale)
        pos = kv_lens[:, None] + jnp.arange(Tx, dtype=jnp.int32)
        q = _rope(q, pos)
        k = _rope(k, pos)
        slot = pos // BLOCK
        off = pos % BLOCK
        blk = jnp.take_along_axis(block_tables, slot, axis=1)
        k_blocks = k_blocks.at[blk, :, off, :].set(k.transpose(0, 2, 1, 3))
        v_blocks = v_blocks.at[blk, :, off, :].set(v.transpose(0, 2, 1, 3))
        k_all = k_blocks[block_tables].transpose(0, 2, 1, 3, 4).reshape(Bx, G, -1, HD)
        v_all = v_blocks[block_tables].transpose(0, 2, 1, 3, 4).reshape(Bx, G, -1, HD)
        S = k_all.shape[2]
        qg = q.reshape(Bx, G, GSZ, Tx, HD)
        scores = jnp.einsum('bghtd,bgsd->bghts', qg, k_all) * SCALE
        kpos = jnp.arange(S, dtype=jnp.int32)
        allowed = (kpos[None, None, :] <= pos[:, :, None]) & (kpos[None, None, :] > pos[:, :, None] - WINDOW)
        scores = jnp.where(allowed[:, None, None, :, :], scores, -jnp.inf)
        p = jax.nn.softmax(scores, axis=-1)
        o = jnp.einsum('bghts,bgsd->bghtd', p, v_all).reshape(Bx, H, Tx, HD)
        o = o.transpose(0, 2, 1, 3).reshape(Bx, Tx, H * HD)
        return jnp.einsum('bto,do->btd', o, Wo)

    def _L3_cond_ref(x, W, A, Bm, scalings, adapter_idx):
        import jax, jax.numpy as jnp
        import numpy as np
        B, T, D_IN, D_OUT = (16, 512, 512, 512)
        N_ADAPTERS, RANK = (8, 16)
        H = jnp.einsum('btd,od->bto', x, W)
        A_b = A[adapter_idx]
        B_b = Bm[adapter_idx]
        s_b = scalings[adapter_idx]
        xa = jnp.einsum('btd,brd->btr', x, A_b)
        delta = jnp.einsum('btr,bor->bto', xa, B_b)
        delta = jax.lax.stop_gradient(delta * s_b[:, None, None])
        return H + delta
    x = x + _L0_cond_ref(x, itok_B_1_198, L0_cond_weights)
    x = x + _L1_cond_ref(x, L1_cond_W_base, L1_cond_Wt, L1_cond_A, L1_cond_B_w, L1_cond_Wp, L1_cond_scaling, itok_B_0_3)
    x = x + _L2_cond_ref(x, L2_cond_Wq, L2_cond_Wk, L2_cond_Wv, L2_cond_Wo, L2_cond_q_norm_scale, L2_cond_k_norm_scale, L2_cond_k_blocks, L2_cond_v_blocks, itok_Bx257_0_4111, itok_B_37_3939)
    x = x + _L3_cond_ref(x, L3_cond_W, L3_cond_A, L3_cond_Bm, L3_cond_scalings, itok_B_0_6)
    return x

_drawn_inputs = setup_inputs


def setup_inputs(seed=0):
    import zlib

    import numpy as np

    out = dict(_drawn_inputs(seed))
    spreads = {'L1_cond_scaling': (1.0, 0.6), 'L3_cond_scalings': (1.0, 0.6)}
    factors = {'L1_cond_Wt': 8.0,
     'L1_cond_A': 8.0,
     'L1_cond_B_w': 8.0,
     'L1_cond_Wp': 8.0,
     'L2_cond_Wk': 12.185,
     'L2_cond_q_norm_scale': 64.0,
     'L2_cond_k_norm_scale': 64.0,
     'L2_cond_k_blocks': 26.228,
     'L1_cond_W_base': 4.405,
     'L2_cond_Wq': 3.835,
     'L2_cond_Wv': 2.919,
     'L2_cond_Wo': 2.811,
     'L2_cond_v_blocks': 8.0}
    for name, (base, spread) in spreads.items():
        noise = np.random.default_rng([zlib.crc32(name.encode()), seed]).standard_normal(out[name].shape)
        drawn = base * np.exp(spread * noise) if base else spread * noise
        out[name] = jnp.asarray(drawn.astype(out[name].dtype))
    for name, factor in factors.items():
        out[name] = (out[name] * factor).astype(out[name].dtype)
    return out
```

```python
from contextlib import ExitStack

import numpy as np
import concourse.bass as bass
from concourse import mybir

F32, F32R, I32 = mybir.dt.float32, mybir.dt.float32r, mybir.dt.int32
ALU, ACT, AX = mybir.AluOpType, mybir.ActivationFunctionType, mybir.AxisListType

B, T, D = 64, 64, 512
PAIRS = B // 2
KC = D // 128
H, G, HD = 8, 4, 64
NBLK, BLOCK, WINDOW = 257, 16, 256
NCACHE = 16 * NBLK
MAXPOS = NBLK * BLOCK
CONDS = 200
R = 16
E1, E3 = 4, 8
WR = T // BLOCK + 1
RD = 21
NE = WR * B
RPAD = 32
JQ = RD * 4
NPOS = RD * BLOCK
SKIP = float(1 << 20)
MASKED = 1e30
KEY = 1024
EPS = 1e-6
SCALE = 256.0 ** -0.5
NIDX = 2 + 2 * G


def program(nc, t):
    with ExitStack() as whole:
        pk = nc.dram_tensor("patched_k", (NE * G, BLOCK * HD), F32).ap()
        pv = nc.dram_tensor("patched_v", (NE * G, BLOCK * HD), F32).ap()
        q_dram = nc.dram_tensor("q_rows", (PAIRS, 128, H * HD), F32).ap()
        x2_dram = nc.dram_tensor("x2_t", (PAIRS, 128, KC * 128), F32).ap()

        def keep(name, shape, dt=F32):
            return whole.enter_context(nc.sbuf_tensor(name, shape, dt))

        s = {
            "ident": keep("ident", [128, 128]),
            "wo": keep("wo", [128, KC, D]),
            "w3h": keep("w3h", [128, KC, D], F32R), "w3l": keep("w3l", [128, KC, D], F32R),
            "a3": keep("a3", [128, KC, E3 * R]),
            "b3": keep("b3", [128, D]),
            "mask1": keep("mask1", [128, B]), "mask3": keep("mask3", [128, B]),
            "pair_idx": keep("pair_idx", [128, PAIRS, 2 + G], I32),
            "row_idx": keep("row_idx", [128, B, NIDX], I32),
            "centre": keep("minus_centre", [128, B]), "half": keep("half", [128, B]),
            "pcol": keep("pcol", [128, NPOS]),
        }
        with ExitStack() as early:
            def early_t(name, shape, dt=F32):
                return early.enter_context(nc.sbuf_tensor(name, shape, dt))
            w = {
                "wbh": early_t("wbh", [128, KC, D], F32R), "wbl": early_t("wbl", [128, KC, D], F32R),
                "wqh": early_t("wqh", [128, KC, D], F32R), "wql": early_t("wql", [128, KC, D], F32R),
                "wkvh": early_t("wkvh", [128, KC, D], F32R), "wkvl": early_t("wkvl", [128, KC, D], F32R),
                "awh": early_t("awh", [128, KC, 128], F32R), "awl": early_t("awl", [128, KC, 128], F32R),
                "pbh": early_t("pbh", [128, D], F32R), "pbl": early_t("pbl", [128, D], F32R),
                "normscale": early_t("normscale", [128, 2, 2, HD]),
            }
            with ExitStack() as c:
                prepare(nc, c, t, s, w, pk, pv)
            with ExitStack() as c:
                project(nc, c, t, s, w, pk, pv, q_dram, x2_dram)
        with ExitStack() as c:
            attend(nc, c, t, s, pk, pv, q_dram, x2_dram)


def prepare(nc, ctx, t, s, w, pk, pv):
    def sb(name, shape, dt=F32):
        return ctx.enter_context(nc.sbuf_tensor(f"prep_{name}", shape, dt))

    def sem(name):
        return ctx.enter_context(nc.semaphore(f"prep_{name}"))

    stage = [sb(f"stage{i}", [128, KC, D]) for i in range(2)]
    wt, wpt = sb("wt", [128, KC, D]), sb("wpt", [128, KC, D])
    at, bt = sb("at", [128, KC, E1 * R]), sb("bt", [128, KC, E1 * R])
    sc1, sc3 = sb("sc1", [128, 1]), sb("sc3", [128, 1])
    cols = sb("cols", [128, 4])
    rows = sb("rows", [128, 512])
    later = sb("later", [B, WR, NE])
    qrow = sb("qrow", [128, JQ])
    kv_col, table = sb("kv_col", [128, 1], I32), sb("table", [128, NBLK], I32)
    ints = sb("ints", [128, 4, B], I32)
    k_it, w_it = sb("k_it", [128, 4], I32), sb("w_it", [128, 3, B], I32)
    fcol = sb("fcol", [128, 4])
    frow = sb("frow", [128, 8, B])
    tablef, picked = sb("tablef", [128, NBLK]), sb("picked", [128, NBLK])
    slots, blocks = sb("slots", [128, RD + WR]), sb("blocks", [128, RD + WR])
    diag, ones = sb("diag", [B, WR, B]), sb("ones", [B, 128])
    xrow, key = sb("xrow", [128, NE]), sb("key", [128, NE])
    keyed = sb("keyed", [128, RD + WR])
    dist = sb("dist", [128, RD + WR, NE])
    first = sb("first", [128, RD + WR])
    found, cached, patched = sb("found", [128, RD]), sb("cached", [128, RD]), sb("patched", [128, RD])
    kidx = sb("kidx", [B, 2, G, RPAD])
    vidx = sb("vidx", [B, 2, JQ])
    over = sb("over", [B, WR, NE])
    valid = sb("valid", [B, WR, BLOCK])
    dest = sb("dest", [B, WR * BLOCK])
    onehot = sb("onehot", [B, BLOCK])
    move = sb("move", [B, 2, T])
    init_idx = sb("init_idx", [128, WR, 2], I32)
    initf = sb("initf", [128, WR, 2])
    blkbuf = [sb(f"blkbuf{i}", [128, BLOCK * HD]) for i in range(4)]
    ps = [ctx.enter_context(nc.psum_tensor(f"prep_ps{i}", [128, 512], F32)) for i in range(4)]

    small_in, later_in, lora_in, keep_in = sem("small_in"), sem("later_in"), sem("lora_in"), sem("keep_in")
    stage_in = [sem(f"stage_in{i}") for i in range(2)]
    stage_free, wsplit_h = sem("stage_free"), sem("wsplit_h")
    step, pe_step, dist_ready = sem("step"), sem("pe_step"), sem("dist_ready")
    blk_in = [sem(f"blk_in{i}") for i in range(4)]
    blk_out = [sem(f"blk_out{i}") for i in range(4)]
    split_w = [("wbt", "wbh", "wbl", True), ("wqt", "wqh", "wql", False),
               ("wkvt", "wkvh", "wkvl", False), ("w3t", "w3h", "w3l", True)]
    smalls = [(cols, "cols"), (rows, "rows"), (qrow, "qrow"), (kv_col, "kv_col"), (table, "table"),
              (sc1, "sc1"), (sc3, "sc3"), (ints, "ints"), (s["ident"], "ident"), (s["pcol"], "pcol")]
    marks = {}
    with nc.Block() as block:

        @block.vector
        def _(dve):
            n = [0]

            def link(ins, mark=None):
                n[0] += 1
                ins.then_inc(step, 1)
                dve.wait_ge(step, n[0])
                if mark:
                    marks[mark] = n[0]

            v = nc.vector
            dve.wait_ge(small_in, 16 * len(smalls))
            link(v.tensor_scalar(k_it[:, 0:1], kv_col[:], 4, None, ALU.arith_shift_right))
            link(v.tensor_scalar(k_it[:, 1:2], kv_col[:], 15, None, ALU.bitwise_and))
            link(v.tensor_scalar(k_it[:, 3:4], kv_col[:], float(WINDOW - 1), None, ALU.subtract))
            link(v.tensor_scalar(k_it[:, 2:3], k_it[:, 3:4], 4, None, ALU.arith_shift_right))
            link(v.tensor_copy(fcol[:, 0:3], k_it[:, 0:3]))
            link(v.tensor_copy(tablef[:], table[:]))
            link(v.tensor_scalar(slots[:, 0:RD], rows[:, 0:RD], fcol[:, 2:3], 0.0, ALU.add, ALU.max))
            link(v.tensor_scalar(slots[:, RD:], rows[:, 0:WR], fcol[:, 0:1], 0.0, ALU.add, ALU.max))
            link(v.tensor_scalar(slots[:], slots[:], float(NBLK - 1), None, ALU.min))
            for j in range(RD + WR):
                link(v.scalar_tensor_tensor(picked[:], rows[:, 0:NBLK], slots[:, j:j + 1], tablef[:],
                                            ALU.is_equal, ALU.mult, accum_out=blocks[:, j:j + 1]))
            for half in range(2):
                link(v.tensor_scalar(initf[:, :, half], blocks[:, RD:], 4.0, 2.0 * half, ALU.mult, ALU.add))
            link(v.tensor_scalar(initf[:], initf[:], cols[:, 3:4], None, ALU.add))
            link(v.tensor_copy(init_idx[:], initf[:]), "init_idx")
            link(v.memset(ones[:], 1.0))
            for j in range(WR):
                link(v.tensor_scalar(diag[:, j, :], s["ident"][0:B, 0:B], blocks[0:B, RD + j:RD + j + 1], None,
                                     ALU.mult), "diag" if j == WR - 1 else None)
            dve.wait_ge(pe_step, 3)
            link(v.tensor_copy(xrow[:], ps[2][:, 0:NE]))
            link(v.scalar_tensor_tensor(key[:], xrow[:], float(KEY), rows[:, 0:NE], ALU.mult, ALU.add))
            link(v.tensor_scalar(keyed[:], blocks[:], -float(KEY), None, ALU.mult), "keyed")
            dve.wait_ge(dist_ready, RD + WR)
            link(v.tensor_reduce(first[:], dist[:], AX.X, ALU.min))
            dve.wait_ge(later_in, 16)
            for j in range(WR):
                link(v.scalar_tensor_tensor(over[:, j, :], xrow[0:B, :], blocks[0:B, RD + j:RD + j + 1],
                                            later[:, j, :], ALU.is_equal, ALU.mult))
            link(v.memset(valid[:], 1.0))
            link(v.tensor_scalar(valid[:, 0, :], rows[0:B, 0:BLOCK], fcol[0:B, 1:2], None, ALU.is_ge))
            link(v.tensor_scalar(valid[:, WR - 1, :], rows[0:B, 0:BLOCK], fcol[0:B, 1:2], None, ALU.is_lt), "over")
            link(v.tensor_scalar(found[:], first[:, 0:RD], NE - 0.5, SKIP, ALU.is_lt, ALU.mult))
            link(v.tensor_tensor(cached[:], blocks[:, 0:RD], found[:], ALU.add))
            link(v.tensor_scalar(found[:], first[:, 0:RD], NE - 0.5, SKIP, ALU.is_gt, ALU.mult))
            link(v.tensor_scalar(patched[:], first[:, 0:RD], float(NE), None, ALU.min))
            link(v.tensor_tensor(patched[:], patched[:], found[:], ALU.add))
            link(v.memset(kidx[:], SKIP))
            for c, src in enumerate((cached, patched)):
                for g in range(G):
                    link(v.tensor_scalar(kidx[:, c, g, 0:RD], src[0:B, :], 4.0, float(g), ALU.mult, ALU.add))
                for q in range(4):
                    link(v.tensor_scalar(vidx[:, c, :].rearrange("b (j q) -> b j q", q=4)[:, :, q], src[0:B, :],
                                         16.0, float(q), ALU.mult, ALU.add),
                         "vidx" if (c, q) == (1, 3) else None)
            dve.wait_ge(pe_step, 4)
            d3 = dest[:].rearrange("b (j o) -> b j o", j=WR)
            link(v.tensor_scalar(dest[:], ps[3][0:B, 0:WR * BLOCK], 0.5, SKIP, ALU.is_gt, ALU.mult))
            for j in range(WR):
                link(v.scalar_tensor_tensor(d3[:, j, :], rows[0:B, 0:BLOCK], 1.0, d3[:, j, :], ALU.mult, ALU.add))
                link(v.tensor_scalar(keyed[0:B, j:j + 1], first[0:B, RD + j:RD + j + 1], 64.0, None, ALU.mult))
                link(v.tensor_scalar(d3[:, j, :], d3[:, j, :], keyed[0:B, j:j + 1], None, ALU.add))
            link(v.tensor_scalar(onehot[:], rows[0:B, 0:BLOCK], fcol[0:B, 1:2], None, ALU.is_equal))
            link(v.tensor_scalar(move[:, 0, :], dest[:, 0:T], onehot[:, 0:1], None, ALU.mult))
            for o in range(1, BLOCK):
                link(v.scalar_tensor_tensor(move[:, 0, :], dest[:, o:o + T], onehot[:, o:o + 1], move[:, 0, :],
                                            ALU.mult, ALU.add))
            link(v.tensor_copy(move[:, 1, :], move[:, 0, :]), "move")
            link(v.memset(s["row_idx"][:], 0))
            dve.wait_ge(pe_step, 5)
            for c in range(2):
                link(v.tensor_copy(s["row_idx"][:, :, c], ps[2][:, c * B:c * B + B]))
                for g in range(G):
                    link(v.tensor_scalar(s["row_idx"][0:JQ, :, 2 + c * G + g], ps[2][0:JQ, 128 + c * B:128 + c * B + B],
                                         4.0 * g, None, ALU.add))
            link(v.tensor_copy(frow[:, 0:4, :], ints[:]))
            p2 = frow[:].rearrange("p k (i two) -> p k i two", two=2)
            for half, rng in ((0, slice(0, 64)), (1, slice(64, 128))):
                link(v.tensor_scalar(frow[rng, 4, 0:PAIRS], p2[rng, 1, :, half], 64.0, cols[rng, 0:1],
                                     ALU.mult, ALU.add))
                link(v.tensor_scalar(frow[rng, 4, PAIRS:B], p2[rng, 0, :, half], cols[rng, 0:1], float(MAXPOS - 1),
                                     ALU.add, ALU.min))
            link(v.tensor_copy(s["pair_idx"][:, :, 0], frow[:, 4, 0:PAIRS]))
            link(v.tensor_copy(s["pair_idx"][:, :, 1], frow[:, 4, PAIRS:B]))
            dve.wait_ge(pe_step, 6)
            m2 = ps[3][:, 128:128 + B].rearrange("p (i two) -> p i two", two=2)
            for g in range(G):
                for half, rng in ((0, slice(0, 64)), (1, slice(64, 128))):
                    link(v.tensor_scalar(s["pair_idx"][rng, :, 2 + g], m2[rng, :, half], 16.0 * g, None, ALU.add))
            link(v.tensor_scalar(w_it[:, 0, :], ints[:, 0, :], 1.0, None, ALU.add))
            link(v.tensor_scalar(w_it[:, 0, :], w_it[:, 0, :], 15, None, ALU.bitwise_and))
            link(v.tensor_scalar(w_it[:, 1, :], ints[:, 0, :], float(WINDOW - 1), None, ALU.subtract))
            link(v.tensor_scalar(w_it[:, 2, :], w_it[:, 1, :], 4, None, ALU.arith_shift_right))
            link(v.tensor_copy(frow[:, 5, :], w_it[:, 0, :]))
            link(v.tensor_copy(frow[:, 6, :], w_it[:, 2, :]))
            link(v.tensor_scalar(frow[:, 5, :], frow[:, 5, :], cols[:, 0:1], None, ALU.add))
            link(v.tensor_scalar(frow[:, 6, :], frow[:, 6, :], -16.0, 0.0, ALU.mult, ALU.max))
            link(v.tensor_tensor(frow[:, 6, :], frow[:, 6, :], frow[:, 5, :], ALU.max))
            link(v.tensor_scalar(frow[:, 5, :], frow[:, 5, :], float(WINDOW - 1), 0.5, ALU.add, ALU.mult))
            link(v.scalar_tensor_tensor(s["centre"][:], frow[:, 6, :], 0.5, frow[:, 5, :], ALU.mult, ALU.add))
            link(v.tensor_scalar(s["centre"][:], s["centre"][:], -1.0, None, ALU.mult))
            link(v.scalar_tensor_tensor(frow[:, 7, :], frow[:, 6, :], -0.5, frow[:, 5, :], ALU.mult, ALU.add))
            link(v.tensor_scalar(s["half"][:], frow[:, 7, :], 0.25, None, ALU.add))
            link(v.tensor_scalar(s["mask1"][:], frow[:, 2, :], cols[:, 1:2], sc1[:, 0:1], ALU.is_equal, ALU.mult))
            link(v.tensor_scalar(s["mask3"][:], frow[:, 3, :], cols[:, 2:3], sc3[:, 0:1], ALU.is_equal, ALU.mult))
            dve.wait_ge(keep_in, 64)
            dve.wait_ge(pe_step, 2)
            aw = ps[0][:, 0:KC * 64].rearrange("p (k m) -> p k m", k=KC)
            for d in range(2):
                link(v.tensor_copy(w["awh"][:, :, 64 * d:64 * d + 64], aw))
                link(v.tensor_tensor(w["awl"][:, :, 64 * d:64 * d + 64], aw,
                                     w["awh"][:, :, 64 * d:64 * d + 64].bitcast(F32), ALU.subtract))
            link(v.tensor_copy(w["pbh"][:], ps[1][:]))
            link(v.tensor_tensor(w["pbl"][:], ps[1][:], w["pbh"][:].bitcast(F32), ALU.subtract))
            link(v.tensor_scalar(w["normscale"][:], w["normscale"][:], 1.0, None, ALU.add))
            minus = w["normscale"][:, :, 1, 0:HD // 2]
            link(v.tensor_scalar(minus, minus, -1.0, None, ALU.mult))
            link(v.tensor_scalar(w["normscale"][:, 0], w["normscale"][:, 0], -SCALE, None, ALU.mult))
            both = {**s, **w}
            for i, (_, h, lo, eye) in enumerate(split_w):
                dve.wait_ge(stage_in[i % 2], 16 * (i // 2) + 16)
                for k in range(KC if eye else 0):
                    link(v.tensor_tensor(stage[i % 2][:, k, k * 128:k * 128 + 128],
                                         stage[i % 2][:, k, k * 128:k * 128 + 128], s["ident"][:], ALU.add))
                link(v.tensor_copy(both[h][:], stage[i % 2][:]))
                link(v.tensor_tensor(both[lo][:], stage[i % 2][:], both[h][:].bitcast(F32), ALU.subtract))
                dve.sem_inc(stage_free, 1)

        @block.sync
        def _(sp):
            for dst, name in smalls:
                sp.dma_start(dst[:], t[name]).then_inc(small_in, 16)
            sp.dma_start(later[:], t["later"]).then_inc(later_in, 16)
            for dst, name in ((wt, "wt"), (at, "at"), (bt, "bt"), (wpt, "wpt")):
                sp.dma_start(dst[:], t[name]).then_inc(lora_in, 16)
            for dst, name in ((s["wo"], "wot"), (s["a3"], "a3t"), (s["b3"], "b3"), (w["normscale"], "normscale")):
                sp.dma_start(dst[:], t[name]).then_inc(keep_in, 16)
            sp.wait_ge(keep_in, 64)
            for n in range(2 * WR * 2):
                table_out = (pk, pv)[n % 2].rearrange("(j b g) f -> j g b f", j=WR, g=G)
                j, half = divmod(n // 2, 2)
                sp.wait_ge(blk_in[n % 4], 16 * (n // 4) + 16)
                for g2 in range(2):
                    sp.dma_start(table_out[j, 2 * half + g2], blkbuf[n % 4][64 * g2:64 * g2 + 64, :])\
                        .then_inc(blk_out[n % 4], 16)
            for i in range(4):
                sp.wait_ge(blk_out[i], 32 * 5)

        @block.scalar
        def _(act):
            for n, (name, h, _, _) in enumerate(split_w[0:2]):
                act.dma_start(stage[n][:], t[name]).then_inc(stage_in[n], 16)
            act.wait_ge(step, marks["keyed"])
            for j in range(RD + WR):
                nc.scalar.activation(dist[:, j, :], key[:], ACT.Abs, bias=keyed[:, j:j + 1]).then_inc(dist_ready, 1)
            for n, (name, h, _, _) in enumerate(split_w):
                if n < 2:
                    continue
                act.wait_ge(stage_free, n - 1)
                act.dma_start(stage[n % 2][:], t[name]).then_inc(stage_in[n % 2], 16)

        @block.gpsimd
        def _(pool):
            pool.wait_ge(step, marks["init_idx"])
            for n in range(2 * WR * 2):
                j, half = divmod(n // 2, 2)
                if n >= 4:
                    pool.wait_ge(blk_out[n % 4], 32 * (n // 4))
                src = t["k_rows"] if n % 2 == 0 else t["v_rows"]
                pool.indirect_dma_start(blkbuf[n % 4][:], None, src,
                                        bass.IndirectOffsetOnAxis(ap=init_idx[:, j, half:half + 1], axis=0),
                                        bounds_check=NCACHE * G - 1, oob_is_err=False).then_inc(blk_in[n % 4], 16)

        @block.tensor
        def _(pe):
            pe.wait_ge(lora_in, 64)
            for m in range(KC):
                for k in range(KC):
                    mm = pe.matmul(ps[0][:, m * 64:m * 64 + 64], wt[:, k, m * 128:m * 128 + 128], at[:, k, :],
                                   start=(k == 0), stop=(k == KC - 1))
            mm.then_inc(pe_step, 1)
            for d in range(2):
                for k in range(KC):
                    mm = pe.matmul(ps[1][64 * d:64 * d + 64, :], bt[:, k, :], wpt[:, k, :],
                                   start=(k == 0), stop=(k == KC - 1))
            mm.then_inc(pe_step, 1)
            pe.wait_ge(step, marks["diag"])
            for j in range(WR):
                mm = pe.matmul(ps[2][:, j * B:j * B + B], ones[:, :], diag[:, j, :], start=True, stop=True)
            mm.then_inc(pe_step, 1)
            pe.wait_ge(step, marks["over"])
            for j in range(WR):
                for j2 in range(WR):
                    mm = pe.matmul(ps[3][0:B, j * BLOCK:j * BLOCK + BLOCK], over[:, j2, j * B:j * B + B],
                                   valid[:, j2, :], start=(j2 == 0), stop=(j2 == WR - 1))
            mm.then_inc(pe_step, 1)
            pe.wait_ge(step, marks["vidx"])
            for c in range(2):
                pe.transpose(ps[2][:, c * B:c * B + B], kidx[:, c].rearrange("b g j -> b (g j)"), s["ident"][0:B, 0:B])
                mm = pe.transpose(ps[2][0:JQ, 128 + c * B:128 + c * B + B], vidx[:, c, :], s["ident"][0:B, 0:B])
            mm.then_inc(pe_step, 1)
            pe.wait_ge(step, marks["move"])
            pe.transpose(ps[3][:, 128:128 + B], move[:].rearrange("b a t -> b (a t)"),
                         s["ident"][0:B, 0:B]).then_inc(pe_step, 1)


def project(nc, ctx, t, s, w, pk, pv, q_dram, x2_dram):
    GP = 4
    TURNS = PAIRS // GP
    N = GP * 128

    def sb(name, shape, dt=F32):
        return ctx.enter_context(nc.sbuf_tensor(f"proj_{name}", shape, dt))

    def sem(name):
        return ctx.enter_context(nc.semaphore(f"proj_{name}"))

    xn = [sb(f"xn{p}", [128, D]) for p in range(GP)]
    cw = [sb(f"cw{p}", [128, T]) for p in range(GP)]
    mix = [sb(f"mix{p}", [128, 128]) for p in range(GP)]
    cw_idx = [sb(f"cw_idx{p}", [128, 1], I32) for p in range(GP)]
    idx = [sb(f"idx{p}", [128, 1 + G], I32) for p in range(GP)]
    rope = [sb(f"rope{p}", [128, 2, HD]) for p in range(GP)]
    turn = sb("turn", [128, 2, 2, HD])
    x1h, x1l = sb("x1h", [128, KC, N], F32R), sb("x1l", [128, KC, N], F32R)
    zm, zs = sb("zm", [128, N]), sb("zs", [128, N], F32R)
    x2r, x2h, x2l = sb("x2r", [128, KC, N]), sb("x2h", [128, KC, N], F32R), sb("x2l", [128, KC, N], F32R)
    NH = H + G
    sq, y, t1, t2 = (sb(n, [128, NH, HD]) for n in ("sq", "y", "t1", "t2"))
    ss, ms, rs = (sb(n, [128, NH]) for n in ("ss", "ms", "rs"))
    q_out = [sb(f"q_out{i}", [128, H, HD]) for i in range(2)]
    kv_out = [sb(f"kv_out{i}", [128, 2, G, HD]) for i in range(2)]

    x1_ps = [ctx.enter_context(nc.psum_tensor(f"x1_ps{i}", [128, KC, 128], F32)) for i in range(2)]
    x2_ps = [ctx.enter_context(nc.psum_tensor(f"x2_ps{i}", [128, N], F32)) for i in range(3)]
    z_ps = ctx.enter_context(nc.psum_tensor("z_ps", [128, N], F32))
    q_ps = ctx.enter_context(nc.psum_tensor("q_ps", [128, H, HD], F32))
    kv_ps = ctx.enter_context(nc.psum_tensor("kv_ps", [128, 2, G, HD], F32))

    x_in = [sem(f"x_in{p}") for p in range(GP)]
    cw_in, rope_in = [sem(f"cw_in{p}") for p in range(GP)], [sem(f"rope_in{p}") for p in range(GP)]
    begun = sem("begun")
    cw_idx_ready, idx_ready, mix_zero, mix_ready = sem("cw_idx_ready"), sem("idx_ready"), sem("mix_zero"), sem("mix_ready")
    x1_mm, x1_high, x1_low = sem("x1_mm"), sem("x1_high"), sem("x1_low")
    z_mm, z_masked, z_high, z_low = sem("z_mm"), sem("z_masked"), sem("z_high"), sem("z_low")
    x2_mm, x2_raw, x2_high, x2_low = sem("x2_mm"), sem("x2_raw"), sem("x2_high"), sem("x2_low")
    x2_stored = sem("x2_stored")
    qkv_mm, squared = sem("qkv_mm"), sem("squared")
    averaged, rooted = sem("averaged"), sem("rooted")
    turn_ready, chain, scaled, turned = sem("turn_ready"), sem("chain"), sem("scaled"), sem("turned")
    q_stored = [sem(f"q_stored{i}") for i in range(2)]
    kv_scattered = [sem(f"kv_scattered{i}") for i in range(2)]
    pk16 = pk.rearrange("r (o d) -> (r o) d", d=HD)
    pv16 = pv.rearrange("r (o d) -> (r o) d", d=HD)

    def turns(engine, body):
        body(0, False)
        with engine.Fori(1, TURNS - 1) as i:
            body(i, False)
        body(TURNS - 1, True)

    def wait(engine, semaphore, value):
        if not isinstance(value, int) or value > 0:
            engine.wait_ge(semaphore, value)

    def some(x, n=1):
        return slice(x, x + n) if isinstance(x, int) else bass.ds(x, n)

    with nc.Block() as block:

        @block.sync
        def _(sp):
            def load(n, p, before):
                wait(sp, x1_mm, before)
                sp.dma_start(xn[p][:], t["x_pairs"][some(n)].rearrange("a p n -> p (a n)")).then_inc(x_in[p], 16)

            def body(i, last):
                if not last:
                    for p in range(GP):
                        load(GP * i + GP + p, p, GP * i + p + 1)
                sp.wait_ge(x2_raw, KC * i + KC)
                for p in range(GP):
                    sp.dma_start(x2_dram[some(GP * i + p)].rearrange("a p (k n) -> p (a k) n", k=KC),
                                 x2r[:, :, p * 128:p * 128 + 128]).then_inc(x2_stored, 16)
                for p in range(GP):
                    sp.wait_ge(turned, GP * i + p + 1)
                    sp.dma_start(q_dram[some(GP * i + p)].rearrange("a p n -> p (a n)"),
                                 q_out[p % 2][:].rearrange("p h d -> p (h d)")).then_inc(q_stored[p % 2], 16)

            for p in range(GP):
                load(p, p, 0)
            turns(sp, body)
            sp.wait_ge(x2_stored, 16 * PAIRS)
            for i in range(2):
                sp.wait_ge(q_stored[i], 16 * PAIRS // 2)

        @block.gpsimd
        def _(pool):
            def weights(i, n, p):
                wait(pool, cw_in[p], 16 * i)
                wait(pool, mix_ready, n - GP + 1)
                pool.sem_inc(begun, 1)
                pool.tensor_copy(cw_idx[p][:], s["pair_idx"][:, some(n), 0]).then_inc(cw_idx_ready, 1)
                pool.wait_ge(cw_idx_ready, n + 1)
                pool.sem_inc(begun, 1)
                pool.indirect_dma_start(cw[p][:], None, t["l0w"],
                                        bass.IndirectOffsetOnAxis(ap=cw_idx[p][:, 0:1], axis=0),
                                        bounds_check=CONDS * T - 1, oob_is_err=False).then_inc(cw_in[p], 16)

            def angles(i, n, p):
                if p < 2:
                    wait(pool, kv_scattered[p], 32 * G * 2 * i)
                wait(pool, turn_ready, n - GP + 1)
                pool.sem_inc(begun, 1)
                pool.tensor_copy(idx[p][:], s["pair_idx"][:, some(n), 1:2 + G].rearrange("p a k -> p (a k)"))\
                    .then_inc(idx_ready, 1)
                pool.wait_ge(idx_ready, n + 1)
                pool.sem_inc(begun, 1)
                pool.indirect_dma_start(rope[p][:].rearrange("p a d -> p (a d)"), None, t["rope"],
                                        bass.IndirectOffsetOnAxis(ap=idx[p][:, 0:1], axis=0),
                                        bounds_check=MAXPOS - 1, oob_is_err=False).then_inc(rope_in[p], 16)

            def body(i, last):
                for p in range(GP):
                    angles(i, GP * i + p, p)
                if not last:
                    for p in range(GP):
                        weights(i + 1, GP * i + GP + p, p)
                for p in range(GP):
                    pool.wait_ge(turned, GP * i + p + 1)
                    pool.wait_ge(squared, GP * i + p + 1)
                    pool.sem_inc(begun, 1)
                    for kv, dst in enumerate((pk16, pv16)):
                        for g in range(G):
                            pool.indirect_dma_start(dst, bass.IndirectOffsetOnAxis(ap=idx[p][:, 1 + g:2 + g], axis=0),
                                                    kv_out[p % 2][:, kv, g, :], None,
                                                    bounds_check=NE * G * BLOCK - 1, oob_is_err=False)\
                                .then_inc(kv_scattered[p % 2], 16)

            for p in range(GP):
                pool.memset(mix[p][:], 0.0).then_inc(mix_zero, 1)
            for p in range(GP):
                weights(0, p, p)
            turns(pool, body)
            for i in range(2):
                pool.wait_ge(kv_scattered[i], 32 * G * PAIRS // 2)

        @block.tensor
        def _(pe):
            def mix_tokens(i, n, p):
                pe.wait_ge(x_in[p], 16 * i + 16)
                pe.wait_ge(mix_ready, n + 1)
                wait(pe, x1_low, n - 1)
                for k in range(KC):
                    mm = pe.matmul(x1_ps[p % 2][:, k, :], xn[p][:, k * 128:k * 128 + 128], mix[p][:],
                                   start=True, stop=True)
                mm.then_inc(x1_mm, 1)

            def base(i, o):
                oc = slice(o * 128, o * 128 + 128)
                wait(pe, x2_high, KC * i + (0, -2, -1, 1)[o])
                for k in range(KC):
                    for m, (wa, xa) in enumerate((("wbh", x1h), ("wbh", x1l), ("wbl", x1h))):
                        pe.matmul(x2_ps[o % 3][:], w[wa][:, k, oc], xa[:, k, :],
                                  start=(k == 0 and m == 0), stop=False)

            def lora(o):
                oc = slice(o * 128, o * 128 + 128)
                pe.matmul(x2_ps[o % 3][:], w["pbh"][:, oc], zs[:], start=False, stop=False)
                pe.matmul(x2_ps[o % 3][:], w["pbl"][:, oc], zs[:], start=False, stop=True).then_inc(x2_mm, 1)

            def body(i, last):
                pe.wait_ge(x1_low, GP * i + GP)
                wait(pe, z_masked, i)
                for k in range(KC):
                    for m, (wa, xa) in enumerate((("awh", x1h), ("awh", x1l), ("awl", x1h))):
                        mm = pe.matmul(z_ps[:], w[wa][:, k, :], xa[:, k, :],
                                       start=(k == 0 and m == 0), stop=(k == KC - 1 and m == 2))
                mm.then_inc(z_mm, 1)
                base(i, 0)
                base(i, 1)
                pe.wait_ge(z_low, i + 1)
                lora(0)
                base(i, 2)
                lora(1)
                base(i, 3)
                lora(2)
                lora(3)
                for p in range(GP):
                    if not last:
                        mix_tokens(i + 1, GP * i + GP + p, p)
                    if p == 0:
                        pe.wait_ge(x2_low, KC * i + KC)
                    wait(pe, scaled, GP * i + p)
                    wait(pe, squared, GP * i + p)
                    tok = slice(p * 128, p * 128 + 128)
                    for out, wh, wl in ((q_ps[:].rearrange("p a b -> p (a b)"), "wqh", "wql"),
                                        (kv_ps[:].rearrange("p a b c -> p (a b c)"), "wkvh", "wkvl")):
                        for k in range(KC):
                            for m, (xa, wa) in enumerate(((x2h, wh), (x2l, wh), (x2h, wl))):
                                mm = pe.matmul(out, xa[:, k, tok], w[wa][:, k, :],
                                               start=(k == 0 and m == 0), stop=(k == KC - 1 and m == 2))
                    mm.then_inc(qkv_mm, 1)

            for p in range(GP):
                mix_tokens(0, p, p)
            turns(pe, body)

        @block.scalar
        def _(act):
            sc = nc.scalar

            def x1_part(n, p):
                act.wait_ge(x1_mm, n + 1)
                sc.copy(x1h[:, :, p * 128:p * 128 + 128], x1_ps[p % 2][:]).then_inc(x1_high, 1)

            def body(i, last):
                act.wait_ge(z_masked, i + 1)
                sc.copy(zs[:], zm[:]).then_inc(z_high, 1)
                for o in range(KC):
                    act.wait_ge(x2_mm, KC * i + o + 1)
                    if o == 0:
                        wait(act, x2_stored, 16 * GP * i)
                    sc.copy(x2r[:, o, :], x2_ps[o % 3][:]).then_inc(x2_raw, 1)
                    sc.copy(x2h[:, o, :], x2_ps[o % 3][:]).then_inc(x2_high, 1)
                for p in range(GP):
                    if not last:
                        x1_part(GP * i + GP + p, p)
                    act.wait_ge(qkv_mm, GP * i + p + 1)
                    wait(act, scaled, GP * i + p)
                    sc.activation(sq[:, 0:H, :], q_ps[:], ACT.Square)
                    sc.activation(sq[:, H:NH, :], kv_ps[:, 0], ACT.Square)
                    wait(act, kv_scattered[p % 2], 32 * G * (2 * i + p // 2))
                    sc.copy(kv_out[p % 2][:, 1], kv_ps[:, 1]).then_inc(squared, 1)
                    act.wait_ge(averaged, GP * i + p + 1)
                    sc.activation(rs[:], ms[:], ACT.Sqrt).then_inc(rooted, 1)

            for p in range(GP):
                x1_part(p, p)
            turns(act, body)

        @block.vector
        def _(dve):
            v = nc.vector

            def mixer(i, n, p):
                dve.wait_ge(cw_in[p], 16 * i + 16)
                wait(dve, x1_mm, n - GP + 1)
                for r in (slice(0, 64), slice(64, 128)):
                    ins = v.tensor_tensor(mix[p][r, r], cw[p][r, :], s["ident"][r, r], ALU.add)
                ins.then_inc(mix_ready, 1)

            def x1_rest(n, p):
                dve.wait_ge(x1_high, n + 1)
                tok = slice(p * 128, p * 128 + 128)
                v.tensor_tensor(x1l[:, :, tok], x1_ps[p % 2][:], x1h[:, :, tok].bitcast(F32), ALU.subtract)\
                    .then_inc(x1_low, 1)

            def norm_and_turn(i, n, p):
                dve.wait_ge(rope_in[p], 16 * i + 16)
                v.tensor_tensor(turn[:], rope[p][:].unsqueeze(1).broadcast_to([128, 2, 2, HD]),
                                w["normscale"][:], ALU.mult).then_inc(turn_ready, 1)
                dve.wait_ge(squared, n + 1)
                v.tensor_reduce(ss[:], sq[:], AX.X, ALU.add).then_inc(chain, 1)
                dve.wait_ge(chain, 3 * n + 1)
                v.tensor_scalar(ms[:], ss[:], 1.0 / HD, EPS, ALU.mult, ALU.add).then_inc(averaged, 1)
                dve.wait_ge(rooted, n + 1)
                v.reciprocal(ss[:], rs[:]).then_inc(chain, 1)
                dve.wait_ge(chain, 3 * n + 2)
                v.tensor_tensor(y[:, 0:H, :], q_ps[:], ss[:, 0:H].unsqueeze(2).broadcast_to([128, H, HD]), ALU.mult)
                v.tensor_tensor(y[:, H:NH, :], kv_ps[:, 0], ss[:, H:NH].unsqueeze(2).broadcast_to([128, G, HD]),
                                ALU.mult).then_inc(scaled, 1)
                dve.wait_ge(scaled, n + 1)
                dve.wait_ge(turn_ready, n + 1)
                hh = HD // 2
                for k, (a, b) in enumerate(((0, H), (H, NH))):
                    m = b - a
                    v.tensor_tensor(t1[:, a:b, :], y[:, a:b, :],
                                    turn[:, k, 0, :].unsqueeze(1).broadcast_to([128, m, HD]), ALU.mult)
                    for u in range(2):
                        ins = v.tensor_tensor(t2[:, a:b, u * hh:u * hh + hh], y[:, a:b, hh - u * hh:HD - u * hh],
                                              turn[:, k, 1, u * hh:u * hh + hh].unsqueeze(1)
                                              .broadcast_to([128, m, hh]), ALU.mult)
                ins.then_inc(chain, 1)
                dve.wait_ge(chain, 3 * n + 3)
                wait(dve, q_stored[p % 2], 16 * (2 * i + p // 2))
                v.tensor_tensor(q_out[p % 2][:], t1[:, 0:H, :], t2[:, 0:H, :], ALU.add)
                wait(dve, kv_scattered[p % 2], 32 * G * (2 * i + p // 2))
                v.tensor_tensor(kv_out[p % 2][:, 0], t1[:, H:NH, :], t2[:, H:NH, :], ALU.add).then_inc(turned, 1)

            def body(i, last):
                dve.wait_ge(z_mm, i + 1)
                v.tensor_tensor(zm[:].rearrange("p (b t) -> p b t", t=T), z_ps[:].rearrange("p (b t) -> p b t", t=T),
                                s["mask1"][:, some(2 * GP * i, 2 * GP)].unsqueeze(2).broadcast_to([128, 2 * GP, T]),
                                ALU.mult).then_inc(z_masked, 1)
                dve.wait_ge(z_high, i + 1)
                v.tensor_tensor(zs[64:128, :], zm[64:128, :], zs[64:128, :].bitcast(F32), ALU.subtract)\
                    .then_inc(z_low, 1)
                if not last:
                    for p in range(GP):
                        mixer(i + 1, GP * i + GP + p, p)
                for o in range(KC):
                    dve.wait_ge(x2_high, KC * i + o + 1)
                    v.tensor_tensor(x2l[:, o, :], x2r[:, o, :], x2h[:, o, :].bitcast(F32), ALU.subtract)\
                        .then_inc(x2_low, 1)
                for p in range(GP):
                    if not last:
                        x1_rest(GP * i + GP + p, p)
                    norm_and_turn(i, GP * i + p, p)

            dve.wait_ge(mix_zero, GP)
            for p in range(GP):
                mixer(0, p, p)
            for p in range(GP):
                x1_rest(p, p)
            turns(dve, body)


def attend(nc, ctx, t, s, pk, pv, q_dram, x2_dram):
    QUAD = 4

    def sb(name, shape, dt=F32):
        return ctx.enter_context(nc.sbuf_tensor(f"attn_{name}", shape, dt))

    def sem(name):
        return ctx.enter_context(nc.semaphore(f"attn_{name}"))

    ridx = [sb(f"ridx{i}", [128, NIDX], I32) for i in range(QUAD)]
    kt = [sb(f"kt{i}", [128, BLOCK * HD]) for i in range(2)]
    vt = [sb(f"vt{i}", [JQ, G, 4 * HD]) for i in range(QUAD)]
    kd = sb("kd", [128, BLOCK, 2, HD], F32R)
    ks = [sb(f"ks{i}", [128, G, NPOS], F32R) for i in range(2)]
    qn = [sb(f"qn{i}", [128, H * HD]) for i in range(2)]
    qd = sb("qd", [128, H, 3, HD], F32R)
    qs = [sb(f"qs{i}", [128, 2, 2, H, T], F32R) for i in range(2)]
    mask = [sb(f"mask{i}", [128, NPOS]) for i in range(2)]
    prob = [sb(f"prob{i}", [128, G, NPOS]) for i in range(2)]
    low, rsum, rinv = (sb(n, [128, 2, G]) for n in ("low", "rsum", "rinv"))
    pt = [sb(f"pt{g}", [JQ, 4, 128]) for g in range(G)]
    x2 = [sb(f"x2_{i}", [128, KC, 128]) for i in range(2)]
    ot = sb("ot", [128, 2, KC, T])
    x3, x3h, x3l = sb("x3", [128, KC, 128]), sb("x3h", [128, KC, 128], F32R), sb("x3l", [128, KC, 128], F32R)
    z3 = sb("z3", [128, 128])
    outs = [sb(f"outs{i}", [128, D]) for i in range(2)]

    def pb(name):
        return ctx.enter_context(nc.psum_tensor(name, [128, 512], F32))

    kt_ps, s_ps, pt_ps = ([pb(f"{n}{i}") for i in range(2)] for n in ("kt_ps", "s_ps", "pt_ps"))
    o_ps, m_ps = pb("o_ps"), pb("m_ps")

    begun = sem("begun")
    idx_ready, zeroed = sem("idx_ready"), sem("zeroed")
    k_base, k_in = [sem(f"k_base{i}") for i in range(2)], [sem(f"k_in{i}") for i in range(2)]
    v_base, v_in = [sem(f"v_base{i}") for i in range(QUAD)], [sem(f"v_in{i}") for i in range(QUAD)]
    q_in, x2_in = [sem(f"q_in{i}") for i in range(2)], [sem(f"x2_in{i}") for i in range(2)]
    keys_high, keys_split, keys_mm, keys_out = (sem(n) for n in ("keys_high", "keys_split", "keys_mm", "keys_out"))
    q_high, q_split, q_mm, q_out = (sem(n) for n in ("q_high", "q_split", "q_mm", "q_out"))
    scores_mm, masked, exped, summed, normed, mask_step = (sem(n) for n in (
        "scores_mm", "masked", "exped", "summed", "normed", "mask_step"))
    distances = sem("distances")
    probs_mm, probs_out = sem("probs_mm"), [sem(f"probs_out{i}") for i in range(2)]
    values_mm, o_out = sem("values_mm"), sem("o_out")
    wo_mm, x3_sum, x3_high, x3_low = sem("wo_mm"), sem("x3_sum"), sem("x3_high"), sem("x3_low")
    z3_mm, z3_out, l3_mm, out_ready = sem("z3_mm"), sem("z3_out"), sem("l3_mm"), sem("out_ready")
    out_stored = [sem(f"out_stored{i}") for i in range(2)]
    QUADS = B // QUAD

    def quads(engine, body):
        body(0, True, False)
        with engine.Fori(1, QUADS - 1) as i:
            body(i, False, False)
        body(QUADS - 1, False, True)

    def wait(engine, semaphore, value):
        if not isinstance(value, int) or value > 0:
            engine.wait_ge(semaphore, value)

    def one(x):
        return slice(x, x + 1) if isinstance(x, int) else bass.ds(x, 1)

    def keys_at(buf, o):
        return buf[:].rearrange("p g (o j q) -> p o q g j", o=4, q=4)[:, o]

    def turned_keys(ps):
        return ps[:].rearrange("p (q g j) -> p q g j", q=4, g=G)[:, :, :, 0:RD]

    with nc.Block() as block:

        @block.sync
        def _(sp):
            def load_q(pair, u, uses):
                wait(sp, q_split, uses)
                sp.dma_start(qn[u][:], q_dram[one(pair)].rearrange("a p n -> p (a n)")).then_inc(q_in[u], 16)

            def store(pair, u):
                sp.wait_ge(out_ready, pair + 1)
                sp.dma_start(t["out_pairs"][one(pair)].rearrange("a p n -> p (a n)"), outs[u][:])\
                    .then_inc(out_stored[u], 16)

            def body(i, first, last):
                for u in range(2):
                    pair = 2 * i + u
                    if not (last and u == 1):
                        load_q(pair + 1, (u + 1) % 2, pair)
                    wait(sp, x3_sum, pair - 1)
                    sp.dma_start(x2[u][:].rearrange("p k n -> p (k n)"),
                                 x2_dram[one(pair)].rearrange("a p n -> p (a n)")).then_inc(x2_in[u], 16)
                    if not first:
                        store(pair - 2, u)

            load_q(0, 0, 0)
            quads(sp, body)
            for u in range(2):
                store(PAIRS - 2 + u, u)
            for u in range(2):
                sp.wait_ge(out_stored[u], 16 * PAIRS // 2)

        @block.gpsimd
        def _(pool):
            def gather(dst, table, col, bound, done):
                pool.sem_inc(begun, 1)
                pool.indirect_dma_start(dst, None, table, bass.IndirectOffsetOnAxis(ap=col, axis=0),
                                        bounds_check=bound, oob_is_err=False).then_inc(done, 16)

            def columns(row, r, turns):
                wait(pool, v_in[r], 16 * G * turns)
                pool.sem_inc(begun, 1)
                pool.tensor_copy(ridx[r][:], s["row_idx"][:, one(row), :].rearrange("p a k -> p (a k)"))\
                    .then_inc(idx_ready, 1)
                pool.wait_ge(idx_ready, row + 1)

            def keys(row, r):
                wait(pool, keys_split, G * (row - 1))
                gather(kt[r % 2][:], t["k_rows"], ridx[r][:, 0:1], NCACHE * G - 1, k_base[r % 2])

            def keys_written(row, r, uses):
                pool.wait_ge(k_base[r % 2], 16 * uses)
                gather(kt[r % 2][:], pk, ridx[r][:, 1:2], NE * G - 1, k_in[r % 2])

            def values(row, r):
                wait(pool, values_mm, 2 * (row - 3))
                for g in range(G):
                    gather(vt[r][:, g, :], t["v_quarters"], ridx[r][0:JQ, 2 + g:3 + g], NCACHE * 16 - 1, v_base[r])

            def values_written(r, turns):
                pool.wait_ge(v_base[r], 16 * G * turns)
                for g in range(G):
                    gather(vt[r][:, g, :], pv16, ridx[r][0:JQ, 2 + G + g:3 + G + g], NE * 16 - 1, v_in[r])

            def body(i, first, last):
                for r in range(QUAD):
                    b = QUAD * i + r
                    n, m = (r + 1) % QUAD, (r + 2) % QUAD
                    if not (last and r >= QUAD - 2):
                        columns(b + 2, m, i + (r + 2) // QUAD)
                        keys(b + 2, m)
                    if not (last and r == QUAD - 1):
                        values(b + 1, n)
                    if not (last and r >= QUAD - 2):
                        keys_written(b + 2, m, 2 * i + (r + 2) // 2 + 1)
                    if not (last and r == QUAD - 1):
                        values_written(n, i + 1 + (r + 1) // QUAD)

            pv16 = pv.rearrange("r (q f) -> (r q) f", q=4)
            for i in range(2):
                pool.memset(kt[i][:], 0.0).then_inc(zeroed, 1)
            pool.wait_ge(zeroed, 2)
            for r in range(2):
                columns(r, r, 0)
                keys(r, r)
                keys_written(r, r, 1)
            values(0, 0)
            values_written(0, 1)
            quads(pool, body)

        @block.tensor
        def _(pe):
            def turn_probs(b, r, g):
                pe.wait_ge(normed, G * (b - 1) + g + 1)
                wait(pe, probs_out[g % 2], 2 * (b - 1) + g // 2)
                for o in range(4):
                    mm = pe.transpose(pt_ps[g % 2][0:JQ, o * 128:o * 128 + 128],
                                      prob[(r - 1) % 2][:, g, o * JQ:o * JQ + JQ], s["ident"][:])
                mm.then_inc(probs_mm, 1)

            def scores(b, r, g, pair):
                if g == 0:
                    pe.wait_ge(keys_out, G * (b + 1))
                    if r % 2 == 0:
                        pe.wait_ge(q_out, 4 * pair + 4)
                wait(pe, masked, G * b + g - 1)
                for m in range(2):
                    mm = pe.matmul(s_ps[g % 2][:, 0:NPOS],
                                   qs[r // 2][:, m, r % 2, 2 * g:2 * g + 2, :].rearrange("p h t -> p (h t)"),
                                   ks[r % 2][:, g, :], start=(m == 0), stop=(m == 1))
                mm.then_inc(scores_mm, 1)

            def turn_keys(n, o):
                pe.wait_ge(keys_split, G * n + o + 1)
                wait(pe, keys_out, G * n + o - 1)
                for q in range(4):
                    mm = pe.transpose(kt_ps[o % 2][:, q * 128:q * 128 + 128],
                                      kd[:, 4 * q + o].rearrange("p a d -> p (a d)").bitcast(F32), s["ident"][:])
                mm.then_inc(keys_mm, 1)

            def turn_q(pair, u, step):
                if step == 0:
                    pe.wait_ge(q_split, pair + 1)
                elif step == 3:
                    wait(pe, out_ready, pair - 1)
                wait(pe, q_out, 4 * pair + step)
                for hh in range(4):
                    window = qd[:, 4 * (step // 2) + hh].rearrange("p a d -> p (a d)")
                    at = HD * (step % 2)
                    mm = pe.transpose(m_ps[:, hh * 128:hh * 128 + 128], window[:, at:at + 128].bitcast(F32),
                                      s["ident"][:])
                mm.then_inc(q_mm, 1)

            def values(b, r, i, c, pair):
                for j in range(2):
                    pe.wait_ge(probs_out[j], 2 * (b - 1) + c + 1)
                if c == 0:
                    pe.wait_ge(v_in[(r - 1) % QUAD], 16 * G * (i + (r > 0)))
                    if r % 2 == 1:
                        wait(pe, o_out, pair)
                at = ((r - 1) % 2) * 256 + c * 128
                for o in range(4):
                    for g2 in range(2):
                        mm = pe.matmul(o_ps[64 * g2:64 * g2 + 64, at:at + 128],
                                       vt[(r - 1) % QUAD][:, 2 * c + g2, o * HD:o * HD + HD],
                                       pt[2 * c + g2][:, o, :], start=(o == 0), stop=(o == 3))
                mm.then_inc(values_mm, 1)

            def wo(pair):
                pe.wait_ge(o_out, pair)
                wait(pe, out_ready, pair - 1)
                pe.wait_ge(q_out, min(4 * pair + 7, 4 * PAIRS) if isinstance(pair, int) else 4 * pair + 7)
                for m in range(KC):
                    for k in range(KC):
                        mm = pe.matmul(m_ps[:, m * 128:m * 128 + 128], s["wo"][:, k, m * 128:m * 128 + 128],
                                       ot[:, :, k, :], start=(k == 0), stop=(k == KC - 1))
                mm.then_inc(wo_mm, 1)

            def lora3(pair):
                pe.wait_ge(x3_sum, pair)
                for k in range(KC):
                    mm = pe.matmul(m_ps[:, 0:128], s["a3"][:, k, :], x3[:, k, :], start=(k == 0), stop=(k == KC - 1))
                mm.then_inc(z3_mm, 1)

            def out3(pair):
                pe.wait_ge(z3_out, pair)
                pe.wait_ge(x3_low, pair)
                for k in range(KC):
                    for m, (xa, wa) in enumerate(((x3h, "w3h"), (x3l, "w3h"), (x3h, "w3l"))):
                        pe.matmul(m_ps[:], xa[:, k, :], s[wa][:, k, :], start=(k == 0 and m == 0), stop=False)
                pe.matmul(m_ps[:], z3[:], s["b3"][:], start=False, stop=True).then_inc(l3_mm, 1)

            def body(i, first, last):
                for r in range(QUAD):
                    b, pair, u = QUAD * i + r, 2 * i + r // 2, r // 2
                    before, after = not (first and r == 0), not (last and r == QUAD - 1)
                    for g in range(G):
                        if before:
                            turn_probs(b, r, g)
                        scores(b, r, g, pair)
                        if after:
                            turn_keys(b + 1, g)
                        if not (last and u == 1) and (r % 2 == 0 and g > 0 or r % 2 == 1 and g == 3):
                            turn_q(pair + 1, (u + 1) % 2, g - 1 if r % 2 == 0 else 3)
                        if r % 2 == 1 and not (first and u == 0) and g < 3:
                            (wo, lora3, out3)[g](pair)
                        if before and g >= 2:
                            values(b, r, i, g - 2, pair)

            for o in range(4):
                turn_keys(0, o)
            for step in range(4):
                turn_q(0, 0, step)
            quads(pe, body)
            for g in range(G):
                turn_probs(B, 0, g)
                if g >= 2:
                    values(B, 0, QUADS, g - 2, PAIRS)
            wo(PAIRS)
            lora3(PAIRS)
            out3(PAIRS)

        @block.scalar
        def _(act):
            sc = nc.scalar

            def probs_copy(b, g):
                act.wait_ge(probs_mm, G * (b - 1) + g + 1)
                wait(act, values_mm, 2 * (b - 1))
                sc.copy(pt[g][:].rearrange("p o c -> p (o c)"), pt_ps[1][0:JQ, :]).then_inc(probs_out[1], 1)

            def mask_distance(row, r):
                wait(act, masked, G * (row - 1))
                sc.activation(mask[r % 2][:], s["pcol"][:], ACT.Abs, bias=s["centre"][:, one(row)])\
                    .then_inc(distances, 1)

            def exponents(b, r, g):
                act.wait_ge(masked, G * b + g + 1)
                p = prob[r % 2][:, g, :]
                sc.activation(p, p, ACT.Exp, bias=low[:, r % 2, g:g + 1], scale=-1.0,
                              accum_out=rsum[:, r % 2, g:g + 1]).then_inc(exped, 1)

            def keys_part(n, rn, o, uses):
                if o == 0:
                    act.wait_ge(k_in[rn % 2], 16 * uses)
                wait(act, keys_mm, G * (n - 1) + o + 1)
                sc.copy(kd[:].rearrange("p (q o) a d -> p o q a d", o=4)[:, o, :, 0],
                        kt[rn % 2][:].rearrange("p (q o d) -> p o q d", q=4, o=4)[:, o]).then_inc(keys_high, 1)

            def keys_copy(n, rn, o):
                act.wait_ge(keys_mm, G * n + o + 1)
                sc.copy(keys_at(ks[rn % 2], o), turned_keys(kt_ps[o % 2])).then_inc(keys_out, 1)

            def q_part(pair, u, uses):
                act.wait_ge(q_in[u], 16 * uses)
                wait(act, q_mm, 4 * pair)
                sc.copy(qd[:, :, 0:3:2, :].rearrange("p h a d -> p a h d"),
                        qn[u][:].rearrange("p (h d) -> p h d", h=H).unsqueeze(1).broadcast_to([128, 2, H, HD]))\
                    .then_inc(q_high, 1)

            def o_copy(pair):
                act.wait_ge(values_mm, 4 * pair)
                wait(act, wo_mm, pair - 1)
                sc.copy(ot[:].rearrange("p b k t -> p (b k t)"), o_ps[:]).then_inc(o_out, 1)

            def x3_copy(pair):
                act.wait_ge(x3_sum, pair)
                wait(act, l3_mm, pair - 1)
                sc.copy(x3h[:], x3[:]).then_inc(x3_high, 1)

            def out_copy(pair, u, uses):
                act.wait_ge(l3_mm, pair)
                wait(act, out_stored[u], 16 * uses)
                sc.copy(outs[u][:], m_ps[:]).then_inc(out_ready, 1)

            def body(i, first, last):
                for r in range(QUAD):
                    b, pair, u = QUAD * i + r, 2 * i + r // 2, r // 2
                    before, after = not (first and r == 0), not (last and r == QUAD - 1)
                    tail = r % 2 == 1 and not (first and u == 0)
                    for g in range(G):
                        if tail and g == 0:
                            o_copy(pair)
                        if before and g % 2 == 1:
                            probs_copy(b, g)
                        exponents(b, r, g)
                        if after:
                            keys_copy(b + 1, r + 1, g)
                        if g < 3 and after:
                            keys_part(b + 1, r + 1, g + 1, 0)
                        elif g == 3 and not (last and r >= QUAD - 2):
                            keys_part(b + 2, r + 2, 0, 2 * i + (r + 2) // 2 + 1)
                        if r % 2 == 0 and g == 0 and not (last and u == 1):
                            q_part(pair + 1, (u + 1) % 2, i + 1 + u)
                        if tail and g == 0:
                            x3_copy(pair)
                        if after and g == 1:
                            mask_distance(b + 1, r + 1)
                        if tail and g == 2:
                            out_copy(pair, (u + 1) % 2, i + u - 1)

            mask_distance(0, 0)
            for o in range(4):
                keys_part(0, 0, o, 1)
            q_part(0, 0, 1)
            for o in range(4):
                keys_copy(0, 0, o)
            keys_part(1, 1, 0, 1)
            quads(act, body)
            for g in (1, 3):
                probs_copy(B, g)
            o_copy(PAIRS)
            x3_copy(PAIRS)
            out_copy(PAIRS, 1, QUADS - 1)

        @block.vector
        def _(dve):
            v = nc.vector

            def mask_far(row, r):
                dve.wait_ge(distances, row + 1)
                v.tensor_scalar(mask[r % 2][:], mask[r % 2][:], s["half"][:, one(row)], MASKED,
                                ALU.is_gt, ALU.mult).then_inc(mask_step, 1)

            def probs_copy(b, g):
                dve.wait_ge(probs_mm, G * (b - 1) + g + 1)
                wait(dve, values_mm, 2 * (b - 1))
                v.tensor_copy(pt[g][:].rearrange("p o c -> p (o c)"), pt_ps[0][0:JQ, :]).then_inc(probs_out[0], 1)

            def inverse(n, r, g):
                dve.wait_ge(exped, n)
                v.reciprocal(rinv[:, r % 2, g:g + 1], rsum[:, r % 2, g:g + 1]).then_inc(summed, 1)

            def lowest(r, g):
                v.tensor_tensor_reduce(prob[r % 2][:, g, :], s_ps[g % 2][:, 0:NPOS], mask[r % 2][:], 1.0, 3e38,
                                       ALU.add, ALU.min, low[:, r % 2, g:g + 1]).then_inc(masked, 1)

            def normalise(n, r, g):
                dve.wait_ge(summed, n)
                p = prob[r % 2][:, g, :]
                v.tensor_scalar(p, p, rinv[:, r % 2, g:g + 1], None, ALU.mult).then_inc(normed, 1)

            def keys_rest(n, rn, o):
                dve.wait_ge(keys_high, G * n + o + 1)
                parts = kd[:].rearrange("p (q o) a d -> p o q a d", o=4)[:, o]
                v.tensor_tensor(parts[:, :, 1], kt[rn % 2][:].rearrange("p (q o d) -> p o q d", q=4, o=4)[:, o],
                                parts[:, :, 0].bitcast(F32), ALU.subtract).then_inc(keys_split, 1)

            def q_rest(pair, u):
                dve.wait_ge(q_high, pair + 1)
                v.tensor_tensor(qd[:, :, 1, :], qn[u][:].rearrange("p (h d) -> p h d", h=H),
                                qd[:, :, 0, :].bitcast(F32), ALU.subtract).then_inc(q_split, 1)

            def q_copy(pair, u, step):
                dve.wait_ge(q_mm, 4 * pair + step + 1)
                h = 4 * (step // 2)
                v.tensor_copy(qs[u][:, step % 2, :, h:h + 4, :],
                              m_ps[:].rearrange("p (h b t) -> p b h t", h=4, b=2)).then_inc(q_out, 1)

            def x3_add(pair, u, uses):
                dve.wait_ge(wo_mm, pair)
                dve.wait_ge(x2_in[u], 16 * uses)
                v.tensor_tensor(x3[:], m_ps[:].rearrange("p (k n) -> p k n", k=KC), x2[u][:], ALU.add)\
                    .then_inc(x3_sum, 1)

            def x3_rest(pair):
                dve.wait_ge(x3_high, pair)
                v.tensor_tensor(x3l[:], x3[:], x3h[:].bitcast(F32), ALU.subtract).then_inc(x3_low, 1)

            def z3_mask(pair):
                dve.wait_ge(z3_mm, pair)
                cols = slice(2 * pair - 2, 2 * pair) if isinstance(pair, int) else bass.ds(2 * pair - 2, 2)
                v.tensor_tensor(z3[:].rearrange("p (b t) -> p b t", b=2),
                                m_ps[:, 0:128].rearrange("p (b t) -> p b t", b=2),
                                s["mask3"][:, cols].unsqueeze(2).broadcast_to([128, 2, T]), ALU.mult)\
                    .then_inc(z3_out, 1)

            def body(i, first, last):
                for r in range(QUAD):
                    b, pair, u = QUAD * i + r, 2 * i + r // 2, r // 2
                    before, after = not (first and r == 0), not (last and r == QUAD - 1)
                    tail = r % 2 == 1 and not (first and u == 0)
                    for g in range(G):
                        if before and g % 2 == 0:
                            probs_copy(b, g)
                        prev = (G * b + g, r, g - 1) if g > 0 else (G * b, r - 1, G - 1)
                        dve.wait_ge(scores_mm, G * b + g + 1)
                        if g == 0:
                            dve.wait_ge(mask_step, b + 1)
                        if g > 0 or before:
                            inverse(*prev)
                        lowest(r, g)
                        if g > 0 or before:
                            normalise(*prev)
                        if g < 3 and after:
                            keys_rest(b + 1, r + 1, g + 1)
                        elif g == 3 and not (last and r >= QUAD - 2):
                            keys_rest(b + 2, r + 2, 0)
                        if not (last and u == 1):
                            if r % 2 == 0 and g == 0:
                                q_rest(pair + 1, (u + 1) % 2)
                            elif r % 2 == 0 or g == 3:
                                q_copy(pair + 1, (u + 1) % 2, g - 1 if r % 2 == 0 else 3)
                        if tail and g == 0:
                            x3_add(pair, (u + 1) % 2, i + u)
                        if tail and g == 1:
                            x3_rest(pair)
                            z3_mask(pair)
                        if after and g == 3:
                            mask_far(b + 1, r + 1)

            mask_far(0, 0)
            for o in range(4):
                keys_rest(0, 0, o)
            q_rest(0, 0)
            keys_rest(1, 1, 0)
            for step in range(4):
                q_copy(0, 0, step)
            quads(dve, body)
            inverse(G * B, QUAD - 1, G - 1)
            normalise(G * B, QUAD - 1, G - 1)
            for g in (0, 2):
                probs_copy(B, g)
            x3_add(PAIRS, 1, QUADS)
            x3_rest(PAIRS)
            z3_mask(PAIRS)


def kernel(**inputs):
    import concourse.bacc as bacc
    from concourse.bass_utils import run_bass_kernel_spmd

    a = {k: np.asarray(v) for k, v in inputs.items()}

    def chunks(m):
        return m.reshape(KC, 128, m.shape[1]).transpose(1, 0, 2)

    def rows(m):
        return np.broadcast_to(m, (128,) + m.shape)

    conds, kv = (a["itok_B_1_198"], a["itok_B_0_3"], a["itok_B_0_6"]), a["itok_B_37_3939"]
    qk = [a["L2_cond_q_norm_scale"], a["L2_cond_k_norm_scale"]]
    hh = HD // 2
    p = np.arange(128)
    entry = np.arange(NE)
    order = (entry % B) * WR + entry // B
    inv = (np.float32(1) / np.float32(10000.0) ** (np.arange(hh, dtype=np.float32) / np.float32(hh))).astype(np.float32)
    ang = np.arange(MAXPOS, dtype=np.float32)[:, None] * inv
    cos, sin = np.cos(ang), np.sin(ang)
    o4, j, q = np.meshgrid(np.arange(4), np.arange(RD), np.arange(4), indexing="ij")
    laid = {
        "x_pairs": a["x"].reshape(PAIRS, 128, D),
        "l0w": a["L0_cond_weights"].reshape(CONDS * T, T),
        "wbt": chunks(a["L1_cond_W_base"].T), "wt": chunks(a["L1_cond_Wt"]), "wpt": chunks(a["L1_cond_Wp"].T),
        "at": chunks(a["L1_cond_A"].reshape(E1 * R, D).T),
        "bt": chunks(a["L1_cond_B_w"].transpose(1, 0, 2).reshape(D, E1 * R)),
        "wqt": chunks(a["L2_cond_Wq"].T),
        "wkvt": chunks(np.concatenate([a["L2_cond_Wk"].T, a["L2_cond_Wv"].T], axis=1)),
        "wot": a["L2_cond_Wo"].T.reshape(2, 2, 2, HD, D).transpose(1, 3, 0, 2, 4).reshape(128, KC, D),
        "w3t": chunks(a["L3_cond_W"].T),
        "a3t": chunks(a["L3_cond_A"].reshape(E3 * R, D).T),
        "b3": a["L3_cond_Bm"].transpose(0, 2, 1).reshape(E3 * R, D),
        "normscale": rows(np.stack([np.stack([m, np.concatenate([m[hh:], m[:hh]])]) for m in qk])),
        "k_rows": a["L2_cond_k_blocks"].reshape(NCACHE * G, BLOCK * HD),
        "v_quarters": a["L2_cond_v_blocks"].reshape(NCACHE * G * 4, 4 * HD),
        "kv_col": np.concatenate([kv, kv])[:, None],
        "table": np.concatenate([a["itok_Bx257_0_4111"]] * 2),
        "ints": rows(np.stack([kv, *conds])),
        "sc1": np.tile(np.repeat(a["L1_cond_scaling"], R), 2)[:, None],
        "sc3": np.repeat(a["L3_cond_scalings"], R)[:, None],
        "cols": np.stack([p % B, p % (E1 * R) // R, p // R, p // B], 1).astype(np.float32),
        "rows": rows(np.arange(512, dtype=np.float32)),
        "qrow": rows((np.arange(JQ) % 4).astype(np.float32)),
        "later": (np.arange(B)[:, None, None] * WR + np.arange(WR)[None, :, None] > order).astype(np.float32),
        "ident": np.eye(128, dtype=np.float32),
        "pcol": rows((16 * j + 4 * q + o4).reshape(-1).astype(np.float32)),
        "rope": np.concatenate([cos, cos, sin, sin], axis=1).astype(np.float32),
    }
    nc = bacc.Bacc("TRN2", target_bir_lowering=False, num_devices=1)
    arrays, t = {}, {}
    for name, m in laid.items():
        arrays[f"in_{name}"] = np.ascontiguousarray(m)
        t[name] = nc.dram_tensor(f"in_{name}", m.shape, mybir.dt.from_np(m.dtype), kind="ExternalInput").ap()
    t["v_rows"] = t["v_quarters"].rearrange("(r q) f -> r (q f)", q=4)
    t["out_pairs"] = nc.dram_tensor("out", (PAIRS, 128, D), F32, kind="ExternalOutput").ap()
    program(nc, t)
    r = run_bass_kernel_spmd(nc, [arrays], core_ids=[0])
    return r.results[0]["out"].reshape(B, T, D)
```

```python
from contextlib import ExitStack

import numpy as np
import concourse.bass as bass
from concourse import mybir

F32, F32R, I32 = mybir.dt.float32, mybir.dt.float32r, mybir.dt.int32
ALU, ACT, AX = mybir.AluOpType, mybir.ActivationFunctionType, mybir.AxisListType

B, T, D = 64, 64, 512
PAIRS = B // 2
KC = D // 128
H, G, HD = 8, 4, 64
NBLK, BLOCK, WINDOW = 257, 16, 256
NCACHE = 16 * NBLK
MAXPOS = NBLK * BLOCK
CONDS = 200
R = 16
E1, E3 = 4, 8
WR = T // BLOCK + 1
RD = 21
NE = WR * B
JQ = RD * 4
OQ = BLOCK // 4
ROW = OQ * G * HD
NPOS = RD * BLOCK
SKIP = float(1 << 20)
MASKED = 1e30
KEY = 1024
EPS = 1e-6
SCALE = 256.0 ** -0.5


def program(nc, t):
    with ExitStack() as whole:
        pk = nc.dram_tensor("patched_k", (NE * 4, ROW), F32).ap()
        pv = nc.dram_tensor("patched_v", (NE * 4, ROW), F32).ap()
        q_dram = nc.dram_tensor("q_rows", (PAIRS, 128, H * HD), F32).ap()
        x2_dram = nc.dram_tensor("x2_t", (PAIRS, 128, KC * 128), F32).ap()

        def keep(name, shape, dt=F32):
            return whole.enter_context(nc.sbuf_tensor(name, shape, dt))

        s = {
            "ident": keep("ident", [128, 128]),
            "wo": keep("wo", [128, KC, D]),
            "w3h": keep("w3h", [128, KC, D], F32R), "w3l": keep("w3l", [128, KC, D], F32R),
            "a3": keep("a3", [128, KC, E3 * R]),
            "b3": keep("b3", [128, D]),
            "mask1": keep("mask1", [128, B]), "mask3": keep("mask3", [128, B]),
            "pair_idx": keep("pair_idx", [128, PAIRS, 3], I32),
            "row_idx": keep("row_idx", [JQ, B, 2], I32),
            "centre": keep("minus_centre", [128, B]), "half": keep("half", [128, B]),
            "pcol": keep("pcol", [128, NPOS]),
        }
        with ExitStack() as early:
            def early_t(name, shape, dt=F32):
                return early.enter_context(nc.sbuf_tensor(name, shape, dt))
            w = {
                "wbh": early_t("wbh", [128, KC, D], F32R), "wbl": early_t("wbl", [128, KC, D], F32R),
                "wqh": early_t("wqh", [128, KC, D], F32R), "wql": early_t("wql", [128, KC, D], F32R),
                "wkvh": early_t("wkvh", [128, KC, D], F32R), "wkvl": early_t("wkvl", [128, KC, D], F32R),
                "awh": early_t("awh", [128, KC, 128], F32R), "awl": early_t("awl", [128, KC, 128], F32R),
                "pbh": early_t("pbh", [128, D], F32R), "pbl": early_t("pbl", [128, D], F32R),
                "normscale": early_t("normscale", [128, 2, 2, HD]),
            }
            with ExitStack() as c:
                prepare(nc, c, t, s, w, pk, pv)
            with ExitStack() as c:
                project(nc, c, t, s, w, pk, pv, q_dram, x2_dram)
        with ExitStack() as c:
            attend(nc, c, t, s, pk, pv, q_dram, x2_dram)


def prepare(nc, ctx, t, s, w, pk, pv):
    def sb(name, shape, dt=F32):
        return ctx.enter_context(nc.sbuf_tensor(f"prep_{name}", shape, dt))

    def sem(name):
        return ctx.enter_context(nc.semaphore(f"prep_{name}"))

    stage = [sb(f"stage{i}", [128, KC, D]) for i in range(2)]
    wt, wpt = sb("wt", [128, KC, D]), sb("wpt", [128, KC, D])
    at, bt = sb("at", [128, KC, E1 * R]), sb("bt", [128, KC, E1 * R])
    sc1, sc3 = sb("sc1", [128, 1]), sb("sc3", [128, 1])
    cols = sb("cols", [128, 4])
    rows = sb("rows", [128, 512])
    later = sb("later", [B, WR, NE])
    kv_col, table = sb("kv_col", [128, 1], I32), sb("table", [128, NBLK], I32)
    ints = sb("ints", [128, 4, B], I32)
    k_it, w_it = sb("k_it", [128, 4], I32), sb("w_it", [128, 3, B], I32)
    fcol = sb("fcol", [128, 4])
    frow = sb("frow", [128, 8, B])
    tablef, picked = sb("tablef", [128, NBLK]), sb("picked", [128, NBLK])
    slots, blocks = sb("slots", [128, RD + WR]), sb("blocks", [128, RD + WR])
    diag, ones = sb("diag", [B, WR, B]), sb("ones", [B, 128])
    xrow, key = sb("xrow", [128, NE]), sb("key", [128, NE])
    keyed = sb("keyed", [128, RD + WR])
    dist = sb("dist", [128, RD + WR, NE])
    first = sb("first", [128, RD + WR])
    found, cached, patched = sb("found", [128, RD]), sb("cached", [128, RD]), sb("patched", [128, RD])
    quarter = sb("quarter", [B, 2, JQ])
    over = sb("over", [B, WR, NE])
    valid = sb("valid", [B, WR, BLOCK])
    dest = sb("dest", [B, WR * BLOCK])
    onehot = sb("onehot", [B, BLOCK])
    move = sb("move", [B, 2, T])
    init_idx = sb("init_idx", [128, WR, 2], I32)
    initf = sb("initf", [128, WR, 2])
    blkbuf = [sb(f"blkbuf{i}", [128, ROW]) for i in range(4)]
    ps = [ctx.enter_context(nc.psum_tensor(f"prep_ps{i}", [128, 512], F32)) for i in range(4)]

    small_in, later_in, lora_in, keep_in = sem("small_in"), sem("later_in"), sem("lora_in"), sem("keep_in")
    stage_in = [sem(f"stage_in{i}") for i in range(2)]
    stage_free, wsplit_h = sem("stage_free"), sem("wsplit_h")
    step, pe_step, dist_ready = sem("step"), sem("pe_step"), sem("dist_ready")
    blk_in = [sem(f"blk_in{i}") for i in range(4)]
    blk_out = [sem(f"blk_out{i}") for i in range(4)]
    split_w = [("wbt", "wbh", "wbl", True), ("wqt", "wqh", "wql", False),
               ("wkvt", "wkvh", "wkvl", False), ("w3t", "w3h", "w3l", True)]
    smalls = [(cols, "cols"), (rows, "rows"), (kv_col, "kv_col"), (table, "table"),
              (sc1, "sc1"), (sc3, "sc3"), (ints, "ints"), (s["ident"], "ident"), (s["pcol"], "pcol")]
    marks = {}
    with nc.Block() as block:

        @block.vector
        def _(dve):
            n = [0]

            def link(ins, mark=None):
                n[0] += 1
                ins.then_inc(step, 1)
                dve.wait_ge(step, n[0])
                if mark:
                    marks[mark] = n[0]

            v = nc.vector
            dve.wait_ge(small_in, 16 * len(smalls))
            link(v.tensor_scalar(k_it[:, 0:1], kv_col[:], 4, None, ALU.arith_shift_right))
            link(v.tensor_scalar(k_it[:, 1:2], kv_col[:], 15, None, ALU.bitwise_and))
            link(v.tensor_scalar(k_it[:, 3:4], kv_col[:], float(WINDOW - 1), None, ALU.subtract))
            link(v.tensor_scalar(k_it[:, 2:3], k_it[:, 3:4], 4, None, ALU.arith_shift_right))
            link(v.tensor_copy(fcol[:, 0:3], k_it[:, 0:3]))
            link(v.tensor_copy(tablef[:], table[:]))
            link(v.tensor_scalar(slots[:, 0:RD], rows[:, 0:RD], fcol[:, 2:3], 0.0, ALU.add, ALU.max))
            link(v.tensor_scalar(slots[:, RD:], rows[:, 0:WR], fcol[:, 0:1], 0.0, ALU.add, ALU.max))
            link(v.tensor_scalar(slots[:], slots[:], float(NBLK - 1), None, ALU.min))
            for j in range(RD + WR):
                link(v.scalar_tensor_tensor(picked[:], rows[:, 0:NBLK], slots[:, j:j + 1], tablef[:],
                                            ALU.is_equal, ALU.mult, accum_out=blocks[:, j:j + 1]))
            for half in range(2):
                link(v.tensor_scalar(initf[:, :, half], blocks[:, RD:], 4.0, 2.0 * half, ALU.mult, ALU.add))
            link(v.tensor_scalar(initf[:], initf[:], cols[:, 3:4], None, ALU.add))
            link(v.tensor_copy(init_idx[:], initf[:]), "init_idx")
            link(v.memset(ones[:], 1.0))
            for j in range(WR):
                link(v.tensor_scalar(diag[:, j, :], s["ident"][0:B, 0:B], blocks[0:B, RD + j:RD + j + 1], None,
                                     ALU.mult), "diag" if j == WR - 1 else None)
            dve.wait_ge(pe_step, 3)
            link(v.tensor_copy(xrow[:], ps[2][:, 0:NE]))
            link(v.scalar_tensor_tensor(key[:], xrow[:], float(KEY), rows[:, 0:NE], ALU.mult, ALU.add))
            link(v.tensor_scalar(keyed[:], blocks[:], -float(KEY), None, ALU.mult), "keyed")
            dve.wait_ge(dist_ready, RD + WR)
            link(v.tensor_reduce(first[:], dist[:], AX.X, ALU.min))
            dve.wait_ge(later_in, 16)
            for j in range(WR):
                link(v.scalar_tensor_tensor(over[:, j, :], xrow[0:B, :], blocks[0:B, RD + j:RD + j + 1],
                                            later[:, j, :], ALU.is_equal, ALU.mult))
            link(v.memset(valid[:], 1.0))
            link(v.tensor_scalar(valid[:, 0, :], rows[0:B, 0:BLOCK], fcol[0:B, 1:2], None, ALU.is_ge))
            link(v.tensor_scalar(valid[:, WR - 1, :], rows[0:B, 0:BLOCK], fcol[0:B, 1:2], None, ALU.is_lt), "over")
            link(v.tensor_scalar(found[:], first[:, 0:RD], NE - 0.5, SKIP, ALU.is_lt, ALU.mult))
            link(v.tensor_tensor(cached[:], blocks[:, 0:RD], found[:], ALU.add))
            link(v.tensor_scalar(found[:], first[:, 0:RD], NE - 0.5, SKIP, ALU.is_gt, ALU.mult))
            link(v.tensor_scalar(patched[:], first[:, 0:RD], float(NE), None, ALU.min))
            link(v.tensor_tensor(patched[:], patched[:], found[:], ALU.add))
            for c, src in enumerate((cached, patched)):
                for q in range(4):
                    link(v.tensor_scalar(quarter[:, c, :].rearrange("b (j q) -> b j q", q=4)[:, :, q], src[0:B, :],
                                         4.0, float(q), ALU.mult, ALU.add),
                         "quarter" if (c, q) == (1, 3) else None)
            dve.wait_ge(pe_step, 4)
            d3 = dest[:].rearrange("b (j o) -> b j o", j=WR)
            link(v.tensor_scalar(dest[:], ps[3][0:B, 0:WR * BLOCK], 0.5, SKIP, ALU.is_gt, ALU.mult))
            for j in range(WR):
                link(v.scalar_tensor_tensor(d3[:, j, :], rows[0:B, 0:BLOCK], 1.0, d3[:, j, :], ALU.mult, ALU.add))
                link(v.tensor_scalar(keyed[0:B, j:j + 1], first[0:B, RD + j:RD + j + 1], float(BLOCK), None, ALU.mult))
                link(v.tensor_scalar(d3[:, j, :], d3[:, j, :], keyed[0:B, j:j + 1], None, ALU.add))
            link(v.tensor_scalar(onehot[:], rows[0:B, 0:BLOCK], fcol[0:B, 1:2], None, ALU.is_equal))
            link(v.tensor_scalar(move[:, 0, :], dest[:, 0:T], onehot[:, 0:1], None, ALU.mult))
            for o in range(1, BLOCK):
                link(v.scalar_tensor_tensor(move[:, 0, :], dest[:, o:o + T], onehot[:, o:o + 1], move[:, 0, :],
                                            ALU.mult, ALU.add))
            link(v.tensor_copy(move[:, 1, :], move[:, 0, :]), "move")
            dve.wait_ge(pe_step, 5)
            for c in range(2):
                link(v.tensor_copy(s["row_idx"][:, :, c], ps[2][0:JQ, c * B:c * B + B]))
            link(v.tensor_copy(frow[:, 0:4, :], ints[:]))
            p2 = frow[:].rearrange("p k (i two) -> p k i two", two=2)
            for half, rng in ((0, slice(0, 64)), (1, slice(64, 128))):
                link(v.tensor_scalar(frow[rng, 4, 0:PAIRS], p2[rng, 1, :, half], 64.0, cols[rng, 0:1],
                                     ALU.mult, ALU.add))
                link(v.tensor_scalar(frow[rng, 4, PAIRS:B], p2[rng, 0, :, half], cols[rng, 0:1], float(MAXPOS - 1),
                                     ALU.add, ALU.min))
            link(v.tensor_copy(s["pair_idx"][:, :, 0], frow[:, 4, 0:PAIRS]))
            link(v.tensor_copy(s["pair_idx"][:, :, 1], frow[:, 4, PAIRS:B]))
            dve.wait_ge(pe_step, 6)
            m2 = ps[3][:, 128:128 + B].rearrange("p (i two) -> p i two", two=2)
            for half, rng in ((0, slice(0, 64)), (1, slice(64, 128))):
                link(v.tensor_copy(s["pair_idx"][rng, :, 2], m2[rng, :, half]))
            link(v.tensor_scalar(w_it[:, 0, :], ints[:, 0, :], 1.0, None, ALU.add))
            link(v.tensor_scalar(w_it[:, 0, :], w_it[:, 0, :], 15, None, ALU.bitwise_and))
            link(v.tensor_scalar(w_it[:, 1, :], ints[:, 0, :], float(WINDOW - 1), None, ALU.subtract))
            link(v.tensor_scalar(w_it[:, 2, :], w_it[:, 1, :], 4, None, ALU.arith_shift_right))
            link(v.tensor_copy(frow[:, 5, :], w_it[:, 0, :]))
            link(v.tensor_copy(frow[:, 6, :], w_it[:, 2, :]))
            link(v.tensor_scalar(frow[:, 5, :], frow[:, 5, :], cols[:, 0:1], None, ALU.add))
            link(v.tensor_scalar(frow[:, 6, :], frow[:, 6, :], -16.0, 0.0, ALU.mult, ALU.max))
            link(v.tensor_tensor(frow[:, 6, :], frow[:, 6, :], frow[:, 5, :], ALU.max))
            link(v.tensor_scalar(frow[:, 5, :], frow[:, 5, :], float(WINDOW - 1), 0.5, ALU.add, ALU.mult))
            link(v.scalar_tensor_tensor(s["centre"][:], frow[:, 6, :], 0.5, frow[:, 5, :], ALU.mult, ALU.add))
            link(v.tensor_scalar(s["centre"][:], s["centre"][:], -1.0, None, ALU.mult))
            link(v.scalar_tensor_tensor(frow[:, 7, :], frow[:, 6, :], -0.5, frow[:, 5, :], ALU.mult, ALU.add))
            link(v.tensor_scalar(s["half"][:], frow[:, 7, :], 0.25, None, ALU.add))
            link(v.tensor_scalar(s["mask1"][:], frow[:, 2, :], cols[:, 1:2], sc1[:, 0:1], ALU.is_equal, ALU.mult))
            link(v.tensor_scalar(s["mask3"][:], frow[:, 3, :], cols[:, 2:3], sc3[:, 0:1], ALU.is_equal, ALU.mult))
            dve.wait_ge(keep_in, 64)
            dve.wait_ge(pe_step, 2)
            aw = ps[0][:, 0:KC * 64].rearrange("p (k m) -> p k m", k=KC)
            for d in range(2):
                link(v.tensor_copy(w["awh"][:, :, 64 * d:64 * d + 64], aw))
                link(v.tensor_tensor(w["awl"][:, :, 64 * d:64 * d + 64], aw,
                                     w["awh"][:, :, 64 * d:64 * d + 64].bitcast(F32), ALU.subtract))
            link(v.tensor_copy(w["pbh"][:], ps[1][:]))
            link(v.tensor_tensor(w["pbl"][:], ps[1][:], w["pbh"][:].bitcast(F32), ALU.subtract))
            link(v.tensor_scalar(w["normscale"][:], w["normscale"][:], 1.0, None, ALU.add))
            minus = w["normscale"][:, :, 1, 0:HD // 2]
            link(v.tensor_scalar(minus, minus, -1.0, None, ALU.mult))
            link(v.tensor_scalar(w["normscale"][:, 0], w["normscale"][:, 0], -SCALE, None, ALU.mult))
            both = {**s, **w}
            for i, (_, h, lo, eye) in enumerate(split_w):
                dve.wait_ge(stage_in[i % 2], 16 * (i // 2) + 16)
                for k in range(KC if eye else 0):
                    link(v.tensor_tensor(stage[i % 2][:, k, k * 128:k * 128 + 128],
                                         stage[i % 2][:, k, k * 128:k * 128 + 128], s["ident"][:], ALU.add))
                link(v.tensor_copy(both[h][:], stage[i % 2][:]))
                link(v.tensor_tensor(both[lo][:], stage[i % 2][:], both[h][:].bitcast(F32), ALU.subtract))
                dve.sem_inc(stage_free, 1)

        @block.sync
        def _(sp):
            for dst, name in smalls:
                sp.dma_start(dst[:], t[name]).then_inc(small_in, 16)
            sp.dma_start(later[:], t["later"]).then_inc(later_in, 16)
            for dst, name in ((wt, "wt"), (at, "at"), (bt, "bt"), (wpt, "wpt")):
                sp.dma_start(dst[:], t[name]).then_inc(lora_in, 16)
            for dst, name in ((s["wo"], "wot"), (s["a3"], "a3t"), (s["b3"], "b3"), (w["normscale"], "normscale")):
                sp.dma_start(dst[:], t[name]).then_inc(keep_in, 16)
            sp.wait_ge(keep_in, 64)
            for n in range(2 * WR * 2):
                table_out = (pk, pv)[n % 2].rearrange("(j b q) f -> j q b f", j=WR, q=4)
                j, half = divmod(n // 2, 2)
                sp.wait_ge(blk_in[n % 4], 16 * (n // 4) + 16)
                for q2 in range(2):
                    sp.dma_start(table_out[j, 2 * half + q2], blkbuf[n % 4][64 * q2:64 * q2 + 64, :])\
                        .then_inc(blk_out[n % 4], 16)
            for i in range(4):
                sp.wait_ge(blk_out[i], 32 * 5)

        @block.scalar
        def _(act):
            for n, (name, h, _, _) in enumerate(split_w[0:2]):
                act.dma_start(stage[n][:], t[name]).then_inc(stage_in[n], 16)
            act.wait_ge(step, marks["keyed"])
            for j in range(RD + WR):
                nc.scalar.activation(dist[:, j, :], key[:], ACT.Abs, bias=keyed[:, j:j + 1]).then_inc(dist_ready, 1)
            for n, (name, h, _, _) in enumerate(split_w):
                if n < 2:
                    continue
                act.wait_ge(stage_free, n - 1)
                act.dma_start(stage[n % 2][:], t[name]).then_inc(stage_in[n % 2], 16)

        @block.gpsimd
        def _(pool):
            pool.wait_ge(step, marks["init_idx"])
            for n in range(2 * WR * 2):
                j, half = divmod(n // 2, 2)
                if n >= 4:
                    pool.wait_ge(blk_out[n % 4], 32 * (n // 4))
                src = t["k_rows"] if n % 2 == 0 else t["v_rows"]
                pool.indirect_dma_start(blkbuf[n % 4][:], None, src,
                                        bass.IndirectOffsetOnAxis(ap=init_idx[:, j, half:half + 1], axis=0),
                                        bounds_check=NCACHE * 4 - 1, oob_is_err=False).then_inc(blk_in[n % 4], 16)

        @block.tensor
        def _(pe):
            pe.wait_ge(lora_in, 64)
            for m in range(KC):
                for k in range(KC):
                    mm = pe.matmul(ps[0][:, m * 64:m * 64 + 64], wt[:, k, m * 128:m * 128 + 128], at[:, k, :],
                                   start=(k == 0), stop=(k == KC - 1))
            mm.then_inc(pe_step, 1)
            for d in range(2):
                for k in range(KC):
                    mm = pe.matmul(ps[1][64 * d:64 * d + 64, :], bt[:, k, :], wpt[:, k, :],
                                   start=(k == 0), stop=(k == KC - 1))
            mm.then_inc(pe_step, 1)
            pe.wait_ge(step, marks["diag"])
            for j in range(WR):
                mm = pe.matmul(ps[2][:, j * B:j * B + B], ones[:, :], diag[:, j, :], start=True, stop=True)
            mm.then_inc(pe_step, 1)
            pe.wait_ge(step, marks["over"])
            for j in range(WR):
                for j2 in range(WR):
                    mm = pe.matmul(ps[3][0:B, j * BLOCK:j * BLOCK + BLOCK], over[:, j2, j * B:j * B + B],
                                   valid[:, j2, :], start=(j2 == 0), stop=(j2 == WR - 1))
            mm.then_inc(pe_step, 1)
            pe.wait_ge(step, marks["quarter"])
            for c in range(2):
                mm = pe.transpose(ps[2][0:JQ, c * B:c * B + B], quarter[:, c, :], s["ident"][0:B, 0:B])
            mm.then_inc(pe_step, 1)
            pe.wait_ge(step, marks["move"])
            pe.transpose(ps[3][:, 128:128 + B], move[:].rearrange("b a t -> b (a t)"),
                         s["ident"][0:B, 0:B]).then_inc(pe_step, 1)


def project(nc, ctx, t, s, w, pk, pv, q_dram, x2_dram):
    GP = 4
    TURNS = PAIRS // GP
    N = GP * 128

    def sb(name, shape, dt=F32):
        return ctx.enter_context(nc.sbuf_tensor(f"proj_{name}", shape, dt))

    def sem(name):
        return ctx.enter_context(nc.semaphore(f"proj_{name}"))

    xn = [sb(f"xn{p}", [128, D]) for p in range(GP)]
    cw = [sb(f"cw{p}", [128, T]) for p in range(GP)]
    mix = [sb(f"mix{p}", [128, 128]) for p in range(GP)]
    idx = [sb(f"idx{c}", [128, GP], I32) for c in range(3)]
    rope = [sb(f"rope{p}", [128, 2, HD]) for p in range(GP)]
    turn = sb("turn", [128, 2, 2, HD])
    x1h, x1l = sb("x1h", [128, KC, N], F32R), sb("x1l", [128, KC, N], F32R)
    zm, zs = sb("zm", [128, N]), sb("zs", [128, N], F32R)
    x2r, x2h, x2l = sb("x2r", [128, KC, N]), sb("x2h", [128, KC, N], F32R), sb("x2l", [128, KC, N], F32R)
    NH = H + G
    sq, y, t1, t2 = (sb(n, [128, NH, HD]) for n in ("sq", "y", "t1", "t2"))
    ss, ms, rs = (sb(n, [128, NH]) for n in ("ss", "ms", "rs"))
    q_out = [sb(f"q_out{i}", [128, H, HD]) for i in range(2)]
    kv_out = [sb(f"kv_out{p}", [128, 2, G, HD]) for p in range(GP)]

    x1_ps = [ctx.enter_context(nc.psum_tensor(f"x1_ps{i}", [128, KC, 128], F32)) for i in range(2)]
    x2_ps = [ctx.enter_context(nc.psum_tensor(f"x2_ps{i}", [128, N], F32)) for i in range(3)]
    z_ps = ctx.enter_context(nc.psum_tensor("z_ps", [128, N], F32))
    q_bank = ctx.enter_context(nc.psum_tensor("q_bank", [128, N], F32))
    kv_bank = ctx.enter_context(nc.psum_tensor("kv_bank", [128, N], F32))
    x2_at = x2_ps + [q_bank]
    q_ps = [m[:].rearrange("p (h d) -> p h d", h=H) for m in (q_bank, x2_ps[1])]
    kv_ps = [m[:].rearrange("p (v g d) -> p v g d", v=2, g=G) for m in (kv_bank, x2_ps[2])]

    x_in = [sem(f"x_in{p}") for p in range(GP)]
    cw_in, rope_in = [sem(f"cw_in{p}") for p in range(GP)], [sem(f"rope_in{p}") for p in range(GP)]
    begun = sem("begun")
    idx_ready, mix_zero, mix_ready = [sem(f"idx_ready{c}") for c in range(3)], sem("mix_zero"), sem("mix_ready")
    x1_mm, x1_high, x1_low = sem("x1_mm"), sem("x1_high"), sem("x1_low")
    z_mm, z_masked, z_high, z_low = sem("z_mm"), sem("z_masked"), sem("z_high"), sem("z_low")
    x2_mm, x2_raw, x2_high, x2_low = sem("x2_mm"), sem("x2_raw"), sem("x2_high"), sem("x2_low")
    x2_stored = sem("x2_stored")
    qkv_mm, squared = sem("qkv_mm"), sem("squared")
    averaged, rooted = sem("averaged"), sem("rooted")
    turn_ready, chain, scaled, turned = sem("turn_ready"), sem("chain"), sem("scaled"), sem("turned")
    q_stored = [sem(f"q_stored{i}") for i in range(2)]
    kv_scattered = [sem(f"kv_scattered{p}") for p in range(GP)]
    positions = [m.rearrange("r (o f) -> (r o) f", o=OQ) for m in (pk, pv)]

    def turns(engine, body):
        body(0, 2)
        with engine.Fori(1, TURNS - 2) as i:
            body(i, 2)
        body(TURNS - 2, 1)
        body(TURNS - 1, 0)

    def wait(engine, semaphore, value):
        if not isinstance(value, int) or value > 0:
            engine.wait_ge(semaphore, value)

    def some(x, n=1):
        return slice(x, x + n) if isinstance(x, int) else bass.ds(x, n)

    with nc.Block() as block:

        @block.sync
        def _(sp):
            def load(n, p, before):
                wait(sp, x1_mm, before)
                sp.dma_start(xn[p][:], t["x_pairs"][some(n)].rearrange("a p n -> p (a n)")).then_inc(x_in[p], 16)

            def body(i, follow):
                if follow:
                    for p in range(GP):
                        load(GP * i + GP + p, p, GP * i + p + 1)
                sp.wait_ge(x2_raw, KC * i + KC)
                for p in range(GP):
                    sp.dma_start(x2_dram[some(GP * i + p)].rearrange("a p (k n) -> p (a k) n", k=KC),
                                 x2r[:, :, p * 128:p * 128 + 128]).then_inc(x2_stored, 16)
                for p in range(GP):
                    sp.wait_ge(turned, GP * i + p + 1)
                    sp.dma_start(q_dram[some(GP * i + p)].rearrange("a p n -> p (a n)"),
                                 q_out[p % 2][:].rearrange("p h d -> p (h d)")).then_inc(q_stored[p % 2], 16)

            for p in range(GP):
                load(p, p, 0)
            turns(sp, body)
            sp.wait_ge(x2_stored, 16 * PAIRS)
            for i in range(2):
                sp.wait_ge(q_stored[i], 16 * PAIRS // 2)

        @block.gpsimd
        def _(pool):
            def columns(c, i):
                for p in range(GP):
                    wait(pool, (cw_in, rope_in, kv_scattered)[c][p], (32 if c == 2 else 16) * i)
                pool.sem_inc(begun, 1)
                pool.tensor_copy(idx[c][:], s["pair_idx"][:, some(GP * i, GP), c]).then_inc(idx_ready[c], 1)
                pool.wait_ge(idx_ready[c], i + 1)

            def weights(n, p):
                wait(pool, mix_ready, n - GP + 1)
                pool.sem_inc(begun, 1)
                pool.indirect_dma_start(cw[p][:], None, t["l0w"],
                                        bass.IndirectOffsetOnAxis(ap=idx[0][:, p:p + 1], axis=0),
                                        bounds_check=CONDS * T - 1, oob_is_err=False).then_inc(cw_in[p], 16)

            def angles(n, p):
                wait(pool, turn_ready, n - GP + 1)
                pool.sem_inc(begun, 1)
                pool.indirect_dma_start(rope[p][:].rearrange("p a d -> p (a d)"), None, t["rope"],
                                        bass.IndirectOffsetOnAxis(ap=idx[1][:, p:p + 1], axis=0),
                                        bounds_check=MAXPOS - 1, oob_is_err=False).then_inc(rope_in[p], 16)

            def body(i, follow):
                columns(2, i)
                if follow > 0:
                    columns(1, i + 1)
                if follow > 1:
                    columns(0, i + 2)
                for p in range(GP):
                    n = GP * i + p
                    pool.wait_ge(turned, n + 1)
                    pool.wait_ge(squared, n + 1)
                    pool.sem_inc(begun, 1)
                    for kv in range(2):
                        pool.indirect_dma_start(positions[kv],
                                                bass.IndirectOffsetOnAxis(ap=idx[2][:, p:p + 1], axis=0),
                                                kv_out[p][:, kv].rearrange("p g d -> p (g d)"), None,
                                                bounds_check=NE * BLOCK - 1, oob_is_err=False)\
                            .then_inc(kv_scattered[p], 16)
                    if follow > 0:
                        angles(n + GP, p)
                    if follow > 1:
                        weights(n + 2 * GP, p)

            for p in range(GP):
                pool.memset(mix[p][:], 0.0).then_inc(mix_zero, 1)
            columns(0, 0)
            for p in range(GP):
                weights(p, p)
            columns(1, 0)
            for p in range(GP):
                angles(p, p)
            columns(0, 1)
            for p in range(GP):
                weights(GP + p, p)
            turns(pool, body)
            for p in range(GP):
                pool.wait_ge(kv_scattered[p], 32 * TURNS)

        @block.tensor
        def _(pe):
            def mix_tokens(i, n, p):
                pe.wait_ge(x_in[p], 16 * i + 16)
                pe.wait_ge(mix_ready, n + 1)
                wait(pe, x1_low, n - 1)
                for k in range(KC):
                    mm = pe.matmul(x1_ps[p % 2][:, k, :], xn[p][:, k * 128:k * 128 + 128], mix[p][:],
                                   start=True, stop=True)
                mm.then_inc(x1_mm, 1)

            def base(i, o):
                oc = slice(o * 128, o * 128 + 128)
                if o == 0:
                    wait(pe, x2_high, KC * i)
                elif o == 1:
                    wait(pe, scaled, GP * i)
                    wait(pe, squared, GP * i)
                for k in range(KC):
                    for m, (wa, xa) in enumerate((("wbh", x1h), ("wbh", x1l), ("wbl", x1h))):
                        pe.matmul(x2_at[o][:], w[wa][:, k, oc], xa[:, k, :],
                                  start=(k == 0 and m == 0), stop=False)

            def lora(o):
                oc = slice(o * 128, o * 128 + 128)
                pe.matmul(x2_at[o][:], w["pbh"][:, oc], zs[:], start=False, stop=False)
                pe.matmul(x2_at[o][:], w["pbl"][:, oc], zs[:], start=False, stop=True).then_inc(x2_mm, 1)

            def body(i, follow):
                pe.wait_ge(x1_low, GP * i + GP)
                wait(pe, z_masked, i)
                for k in range(KC):
                    for m, (wa, xa) in enumerate((("awh", x1h), ("awh", x1l), ("awl", x1h))):
                        mm = pe.matmul(z_ps[:], w[wa][:, k, :], xa[:, k, :],
                                       start=(k == 0 and m == 0), stop=(k == KC - 1 and m == 2))
                mm.then_inc(z_mm, 1)
                base(i, 0)
                base(i, 1)
                base(i, 2)
                pe.wait_ge(z_low, i + 1)
                lora(0)
                lora(1)
                base(i, 3)
                lora(2)
                lora(3)
                if follow:
                    mix_tokens(i + 1, GP * i + GP, 0)
                for p in range(GP):
                    n = GP * i + p
                    if follow and p < GP - 1:
                        mix_tokens(i + 1, n + GP + 1, p + 1)
                    if p == 0:
                        pe.wait_ge(x2_low, KC * i + KC)
                    wait(pe, scaled, n - 1)
                    wait(pe, squared, n - 1)
                    tok = slice(p * 128, p * 128 + 128)
                    for out, wh, wl in ((q_ps[p % 2].rearrange("p a b -> p (a b)"), "wqh", "wql"),
                                        (kv_ps[p % 2].rearrange("p a b c -> p (a b c)"), "wkvh", "wkvl")):
                        for k in range(KC):
                            for m, (xa, wa) in enumerate(((x2h, wh), (x2l, wh), (x2h, wl))):
                                mm = pe.matmul(out, xa[:, k, tok], w[wa][:, k, :],
                                               start=(k == 0 and m == 0), stop=(k == KC - 1 and m == 2))
                    mm.then_inc(qkv_mm, 1)

            for p in range(GP):
                mix_tokens(0, p, p)
            turns(pe, body)

        @block.scalar
        def _(act):
            sc = nc.scalar

            def x1_part(n, p):
                act.wait_ge(x1_mm, n + 1)
                sc.copy(x1h[:, :, p * 128:p * 128 + 128], x1_ps[p % 2][:]).then_inc(x1_high, 1)

            def body(i, follow):
                act.wait_ge(z_masked, i + 1)
                sc.copy(zs[:], zm[:]).then_inc(z_high, 1)
                for o in range(KC):
                    act.wait_ge(x2_mm, KC * i + o + 1)
                    if o == 0:
                        wait(act, x2_stored, 16 * GP * i)
                    sc.copy(x2r[:, o, :], x2_at[o][:]).then_inc(x2_raw, 1)
                    sc.copy(x2h[:, o, :], x2_at[o][:]).then_inc(x2_high, 1)
                if follow:
                    x1_part(GP * i + GP, 0)
                for p in range(GP):
                    if follow and p < GP - 1:
                        x1_part(GP * i + GP + p + 1, p + 1)
                    act.wait_ge(qkv_mm, GP * i + p + 1)
                    wait(act, scaled, GP * i + p)
                    sc.activation(sq[:, 0:H, :], q_ps[p % 2], ACT.Square)
                    sc.activation(sq[:, H:NH, :], kv_ps[p % 2][:, 0], ACT.Square)
                    wait(act, kv_scattered[p], 32 * i)
                    sc.copy(kv_out[p][:, 1], kv_ps[p % 2][:, 1]).then_inc(squared, 1)
                    act.wait_ge(averaged, GP * i + p + 1)
                    sc.activation(rs[:], ms[:], ACT.Sqrt).then_inc(rooted, 1)

            for p in range(GP):
                x1_part(p, p)
            turns(act, body)

        @block.vector
        def _(dve):
            v = nc.vector

            def mixer(i, n, p):
                dve.wait_ge(cw_in[p], 16 * i + 16)
                wait(dve, x1_mm, n - GP + 1)
                for r in (slice(0, 64), slice(64, 128)):
                    ins = v.tensor_tensor(mix[p][r, r], cw[p][r, :], s["ident"][r, r], ALU.add)
                ins.then_inc(mix_ready, 1)

            def x1_rest(n, p):
                dve.wait_ge(x1_high, n + 1)
                tok = slice(p * 128, p * 128 + 128)
                v.tensor_tensor(x1l[:, :, tok], x1_ps[p % 2][:], x1h[:, :, tok].bitcast(F32), ALU.subtract)\
                    .then_inc(x1_low, 1)

            def norm_and_turn(i, n, p):
                dve.wait_ge(rope_in[p], 16 * i + 16)
                v.tensor_tensor(turn[:], rope[p][:].unsqueeze(1).broadcast_to([128, 2, 2, HD]),
                                w["normscale"][:], ALU.mult).then_inc(turn_ready, 1)
                dve.wait_ge(squared, n + 1)
                v.tensor_reduce(ss[:], sq[:], AX.X, ALU.add).then_inc(chain, 1)
                dve.wait_ge(chain, 3 * n + 1)
                v.tensor_scalar(ms[:], ss[:], 1.0 / HD, EPS, ALU.mult, ALU.add).then_inc(averaged, 1)
                dve.wait_ge(rooted, n + 1)
                v.reciprocal(ss[:], rs[:]).then_inc(chain, 1)
                dve.wait_ge(chain, 3 * n + 2)
                v.tensor_tensor(y[:, 0:H, :], q_ps[p % 2], ss[:, 0:H].unsqueeze(2).broadcast_to([128, H, HD]), ALU.mult)
                v.tensor_tensor(y[:, H:NH, :], kv_ps[p % 2][:, 0], ss[:, H:NH].unsqueeze(2).broadcast_to([128, G, HD]),
                                ALU.mult).then_inc(scaled, 1)
                dve.wait_ge(scaled, n + 1)
                dve.wait_ge(turn_ready, n + 1)
                hh = HD // 2
                for k, (a, b) in enumerate(((0, H), (H, NH))):
                    m = b - a
                    v.tensor_tensor(t1[:, a:b, :], y[:, a:b, :],
                                    turn[:, k, 0, :].unsqueeze(1).broadcast_to([128, m, HD]), ALU.mult)
                    for u in range(2):
                        ins = v.tensor_tensor(t2[:, a:b, u * hh:u * hh + hh], y[:, a:b, hh - u * hh:HD - u * hh],
                                              turn[:, k, 1, u * hh:u * hh + hh].unsqueeze(1)
                                              .broadcast_to([128, m, hh]), ALU.mult)
                ins.then_inc(chain, 1)
                dve.wait_ge(chain, 3 * n + 3)
                wait(dve, q_stored[p % 2], 16 * (2 * i + p // 2))
                v.tensor_tensor(q_out[p % 2][:], t1[:, 0:H, :], t2[:, 0:H, :], ALU.add)
                wait(dve, kv_scattered[p], 32 * i)
                v.tensor_tensor(kv_out[p][:, 0], t1[:, H:NH, :], t2[:, H:NH, :], ALU.add).then_inc(turned, 1)

            def body(i, follow):
                dve.wait_ge(z_mm, i + 1)
                v.tensor_tensor(zm[:].rearrange("p (b t) -> p b t", t=T), z_ps[:].rearrange("p (b t) -> p b t", t=T),
                                s["mask1"][:, some(2 * GP * i, 2 * GP)].unsqueeze(2).broadcast_to([128, 2 * GP, T]),
                                ALU.mult).then_inc(z_masked, 1)
                dve.wait_ge(z_high, i + 1)
                v.tensor_tensor(zs[64:128, :], zm[64:128, :], zs[64:128, :].bitcast(F32), ALU.subtract)\
                    .then_inc(z_low, 1)
                if follow:
                    for p in range(GP):
                        mixer(i + 1, GP * i + GP + p, p)
                for o in range(KC):
                    dve.wait_ge(x2_high, KC * i + o + 1)
                    v.tensor_tensor(x2l[:, o, :], x2r[:, o, :], x2h[:, o, :].bitcast(F32), ALU.subtract)\
                        .then_inc(x2_low, 1)
                if follow:
                    x1_rest(GP * i + GP, 0)
                for p in range(GP):
                    if follow and p < GP - 1:
                        x1_rest(GP * i + GP + p + 1, p + 1)
                    norm_and_turn(i, GP * i + p, p)

            dve.wait_ge(mix_zero, GP)
            for p in range(GP):
                mixer(0, p, p)
            for p in range(GP):
                x1_rest(p, p)
            turns(dve, body)


def attend(nc, ctx, t, s, pk, pv, q_dram, x2_dram):
    QUAD = 4

    def sb(name, shape, dt=F32):
        return ctx.enter_context(nc.sbuf_tensor(f"attn_{name}", shape, dt))

    def sem(name):
        return ctx.enter_context(nc.semaphore(f"attn_{name}"))

    ridx = [sb(f"ridx{i}", [JQ, 2], I32) for i in range(QUAD)]
    kt = [sb(f"kt{i}", [JQ, OQ, G, HD]) for i in range(2)]
    vt = [sb(f"vt{i}", [JQ, OQ, G, HD]) for i in range(QUAD)]
    kd = sb("kd", [JQ, G, OQ, 2, HD], F32R)
    ks = [sb(f"ks{i}", [128, G, NPOS], F32R) for i in range(2)]
    qn = [sb(f"qn{i}", [128, H * HD]) for i in range(2)]
    qd = sb("qd", [128, H, 3, HD], F32R)
    qs = [sb(f"qs{i}", [128, 2, 2, H, T], F32R) for i in range(2)]
    mask = [sb(f"mask{i}", [128, NPOS]) for i in range(2)]
    prob = [sb(f"prob{i}", [128, G, NPOS]) for i in range(2)]
    low, rsum, rinv = (sb(n, [128, 2, G]) for n in ("low", "rsum", "rinv"))
    pt = [sb(f"pt{g}", [JQ, 4, 128]) for g in range(G)]
    x2 = [sb(f"x2_{i}", [128, KC, 128]) for i in range(2)]
    ot = sb("ot", [128, 2, KC, T])
    x3, x3h, x3l = sb("x3", [128, KC, 128]), sb("x3h", [128, KC, 128], F32R), sb("x3l", [128, KC, 128], F32R)
    z3 = sb("z3", [128, 128])
    outs = [sb(f"outs{i}", [128, D]) for i in range(2)]

    def pb(name):
        return ctx.enter_context(nc.psum_tensor(name, [128, 512], F32))

    kt_ps, s_ps, pt_ps = ([pb(f"{n}{i}") for i in range(2)] for n in ("kt_ps", "s_ps", "pt_ps"))
    o_ps, m_ps = pb("o_ps"), pb("m_ps")
    z_ps = kt_ps[1][:, 384:512]

    begun = sem("begun")
    idx_ready = sem("idx_ready")
    k_base, k_in = [sem(f"k_base{i}") for i in range(2)], [sem(f"k_in{i}") for i in range(2)]
    v_base, v_in = [sem(f"v_base{i}") for i in range(QUAD)], [sem(f"v_in{i}") for i in range(QUAD)]
    q_in, x2_in = [sem(f"q_in{i}") for i in range(2)], [sem(f"x2_in{i}") for i in range(2)]
    keys_high, keys_split, keys_mm, keys_out = (sem(n) for n in ("keys_high", "keys_split", "keys_mm", "keys_out"))
    q_high, q_split, q_mm, q_out = (sem(n) for n in ("q_high", "q_split", "q_mm", "q_out"))
    scores_mm, masked, exped, summed, normed, mask_step = (sem(n) for n in (
        "scores_mm", "masked", "exped", "summed", "normed", "mask_step"))
    distances = sem("distances")
    probs_mm, probs_out = sem("probs_mm"), [sem(f"probs_out{i}") for i in range(2)]
    values_mm, o_out = sem("values_mm"), sem("o_out")
    wo_mm, x3_sum, x3_high, x3_low = sem("wo_mm"), sem("x3_sum"), sem("x3_high"), sem("x3_low")
    z3_mm, z3_out, l3_mm, out_ready = sem("z3_mm"), sem("z3_out"), sem("l3_mm"), sem("out_ready")
    out_stored = [sem(f"out_stored{i}") for i in range(2)]
    QUADS = B // QUAD

    def quads(engine, body):
        body(0, True, False)
        with engine.Fori(1, QUADS - 1) as i:
            body(i, False, False)
        body(QUADS - 1, False, True)

    def wait(engine, semaphore, value):
        if not isinstance(value, int) or value > 0:
            engine.wait_ge(semaphore, value)

    def one(x):
        return slice(x, x + 1) if isinstance(x, int) else bass.ds(x, 1)

    with nc.Block() as block:

        @block.sync
        def _(sp):
            def load_q(pair, u, uses):
                wait(sp, q_split, uses)
                sp.dma_start(qn[u][:], q_dram[one(pair)].rearrange("a p n -> p (a n)")).then_inc(q_in[u], 16)

            def store(pair, u):
                sp.wait_ge(out_ready, pair + 1)
                sp.dma_start(t["out_pairs"][one(pair)].rearrange("a p n -> p (a n)"), outs[u][:])\
                    .then_inc(out_stored[u], 16)

            def body(i, first, last):
                for u in range(2):
                    pair = 2 * i + u
                    if not (last and u == 1):
                        load_q(pair + 1, (u + 1) % 2, pair)
                    wait(sp, x3_sum, pair - 1)
                    sp.dma_start(x2[u][:].rearrange("p k n -> p (k n)"),
                                 x2_dram[one(pair)].rearrange("a p n -> p (a n)")).then_inc(x2_in[u], 16)
                    if not first:
                        store(pair - 2, u)

            load_q(0, 0, 0)
            quads(sp, body)
            for u in range(2):
                store(PAIRS - 2 + u, u)
            for u in range(2):
                sp.wait_ge(out_stored[u], 16 * PAIRS // 2 + 16)

        @block.gpsimd
        def _(pool):
            def gather(dst, table, col, bound, done):
                pool.sem_inc(begun, 1)
                pool.indirect_dma_start(dst[:].rearrange("p o g d -> p (o g d)"), None, table, bass.IndirectOffsetOnAxis(ap=col, axis=0),
                                        bounds_check=bound, oob_is_err=False).then_inc(done, 16)

            def columns(row, r, turns):
                wait(pool, v_in[r], 16 * turns)
                pool.sem_inc(begun, 1)
                pool.tensor_copy(ridx[r][:], s["row_idx"][:, one(row), :].rearrange("p a k -> p (a k)"))\
                    .then_inc(idx_ready, 1)
                pool.wait_ge(idx_ready, row + 1)

            def keys(row, r):
                wait(pool, keys_split, G * (row - 1))
                gather(kt[r % 2], t["k_rows"], ridx[r][:, 0:1], NCACHE * 4 - 1, k_base[r % 2])

            def keys_written(row, r, uses):
                pool.wait_ge(k_base[r % 2], 16 * uses)
                gather(kt[r % 2], pk, ridx[r][:, 1:2], NE * 4 - 1, k_in[r % 2])

            def values(row, r):
                wait(pool, values_mm, 2 * (row - 3))
                gather(vt[r], t["v_rows"], ridx[r][:, 0:1], NCACHE * 4 - 1, v_base[r])

            def values_written(r, turns):
                pool.wait_ge(v_base[r], 16 * turns)
                gather(vt[r], pv, ridx[r][:, 1:2], NE * 4 - 1, v_in[r])

            def body(i, first, last):
                for r in range(QUAD):
                    b = QUAD * i + r
                    n, m = (r + 1) % QUAD, (r + 2) % QUAD
                    if not (last and r >= QUAD - 2):
                        columns(b + 2, m, i + (r + 2) // QUAD)
                        keys(b + 2, m)
                    if not (last and r == QUAD - 1):
                        values(b + 1, n)
                    if not (last and r >= QUAD - 2):
                        keys_written(b + 2, m, 2 * i + (r + 2) // 2 + 1)
                    if not (last and r == QUAD - 1):
                        values_written(n, i + 1 + (r + 1) // QUAD)

            for r in range(2):
                columns(r, r, 0)
                keys(r, r)
                keys_written(r, r, 1)
            values(0, 0)
            values_written(0, 1)
            quads(pool, body)

        @block.tensor
        def _(pe):
            def turn_probs(b, r, g):
                pe.wait_ge(normed, G * (b - 1) + g + 1)
                wait(pe, probs_out[g % 2], 2 * (b - 1) + g // 2)
                for o in range(4):
                    mm = pe.transpose(pt_ps[g % 2][0:JQ, o * 128:o * 128 + 128],
                                      prob[(r - 1) % 2][:, g, o * JQ:o * JQ + JQ], s["ident"][:])
                mm.then_inc(probs_mm, 1)

            def scores(b, r, g, pair):
                pe.wait_ge(keys_out, G * b + g + 1)
                if g == 0 and r % 2 == 0:
                    pe.wait_ge(q_out, 4 * pair + 4)
                wait(pe, masked, G * b + g - 1)
                for m in range(2):
                    mm = pe.matmul(s_ps[g % 2][:, 0:NPOS],
                                   qs[r // 2][:, m, r % 2, 2 * g:2 * g + 2, :].rearrange("p h t -> p (h t)"),
                                   ks[r % 2][:, g, :], start=(m == 0), stop=(m == 1))
                mm.then_inc(scores_mm, 1)

            def turn_keys(n, g):
                pe.wait_ge(keys_split, G * n + g + 1)
                wait(pe, keys_out, G * n + g - 1)
                for o in range(OQ):
                    mm = pe.transpose(kt_ps[g % 2][:, o * JQ:o * JQ + JQ],
                                      kd[:, g, o].rearrange("p a d -> p (a d)").bitcast(F32), s["ident"][0:JQ, 0:JQ])
                mm.then_inc(keys_mm, 1)

            def turn_q(pair, u, step):
                if step == 0:
                    pe.wait_ge(q_split, pair + 1)
                    wait(pe, out_ready, pair - 2)
                elif step == 2:
                    wait(pe, x3_sum, pair - 1)
                wait(pe, q_out, 4 * pair + step)
                for hh in range(4):
                    window = qd[:, 4 * (step // 2) + hh].rearrange("p a d -> p (a d)")
                    at = HD * (step % 2)
                    mm = pe.transpose(m_ps[:, hh * 128:hh * 128 + 128], window[:, at:at + 128].bitcast(F32),
                                      s["ident"][:])
                mm.then_inc(q_mm, 1)

            def values(b, r, i, c, pair):
                for j in range(2):
                    pe.wait_ge(probs_out[j], 2 * (b - 1) + c + 1)
                if c == 0:
                    pe.wait_ge(v_in[(r - 1) % QUAD], 16 * (i + (r > 0)))
                    if r % 2 == 1:
                        wait(pe, o_out, pair)
                at = ((r - 1) % 2) * 256 + c * 128
                for o in range(4):
                    for g2 in range(2):
                        mm = pe.matmul(o_ps[64 * g2:64 * g2 + 64, at:at + 128],
                                       vt[(r - 1) % QUAD][:, o, 2 * c + g2, :],
                                       pt[2 * c + g2][:, o, :], start=(o == 0), stop=(o == 3))
                mm.then_inc(values_mm, 1)

            def wo(pair, half):
                if half == 0:
                    pe.wait_ge(o_out, pair)
                    wait(pe, out_ready, pair - 1)
                    pe.wait_ge(q_out, min(4 * pair + 6, 4 * PAIRS) if isinstance(pair, int) else 4 * pair + 6)
                for m in (2 * half, 2 * half + 1):
                    for k in range(KC):
                        mm = pe.matmul(m_ps[:, m * 128:m * 128 + 128], s["wo"][:, k, m * 128:m * 128 + 128],
                                       ot[:, :, k, :], start=(k == 0), stop=(k == KC - 1))
                if half == 1:
                    mm.then_inc(wo_mm, 1)

            def lora3(pair):
                pe.wait_ge(x3_sum, pair)
                pe.wait_ge(keys_out, min(8 * pair + 10, G * B) if isinstance(pair, int) else 8 * pair + 10)
                wait(pe, z3_out, pair - 1)
                for k in range(KC):
                    mm = pe.matmul(z_ps, s["a3"][:, k, :], x3[:, k, :], start=(k == 0), stop=(k == KC - 1))
                mm.then_inc(z3_mm, 1)

            def out3(pair, half):
                if half == 0:
                    pe.wait_ge(x3_low, pair)
                    pe.wait_ge(x3_sum, pair)
                    pe.wait_ge(q_out, min(4 * pair + 8, 4 * PAIRS) if isinstance(pair, int) else 4 * pair + 8)
                for k in (2 * half, 2 * half + 1):
                    for m, (xa, wa) in enumerate(((x3h, "w3h"), (x3l, "w3h"), (x3h, "w3l"))):
                        pe.matmul(m_ps[:], xa[:, k, :], s[wa][:, k, :], start=(k == 0 and m == 0), stop=False)
                if half == 1:
                    pe.wait_ge(z3_out, pair)
                    pe.matmul(m_ps[:], z3[:], s["b3"][:], start=False, stop=True).then_inc(l3_mm, 1)

            def body(i, first, last):
                for r in range(QUAD):
                    b, pair, u = QUAD * i + r, 2 * i + r // 2, r // 2
                    before, after = not (first and r == 0), not (last and r == QUAD - 1)
                    tail = r % 2 == 1 and not (first and u == 0)
                    for g in range(G):
                        scores(b, r, g, pair)
                        if before:
                            turn_probs(b, r, g)
                        if tail and g == 3:
                            lora3(pair)
                        if after:
                            turn_keys(b + 1, g)
                        if r % 2 == 0 and not first and g < 2:
                            out3(pair - 1, g)
                        if tail and g < 2:
                            wo(pair, g)
                        if g >= 2 and not (last and u == 1):
                            turn_q(pair + 1, (u + 1) % 2, 2 * (r % 2) + g - 2)
                        if before and g >= 2:
                            values(b, r, i, g - 2, pair)

            for g in range(G):
                turn_keys(0, g)
            for step in range(4):
                turn_q(0, 0, step)
            quads(pe, body)
            for g in range(G):
                turn_probs(B, 0, g)
                if g < 2:
                    out3(PAIRS - 1, g)
                else:
                    values(B, 0, QUADS, g - 2, PAIRS)
            for half in range(2):
                wo(PAIRS, half)
            lora3(PAIRS)
            for half in range(2):
                out3(PAIRS, half)

        @block.scalar
        def _(act):
            sc = nc.scalar

            def probs_copy(b, g):
                act.wait_ge(probs_mm, G * (b - 1) + g + 1)
                wait(act, values_mm, 2 * (b - 1))
                sc.copy(pt[g][:].rearrange("p o c -> p (o c)"), pt_ps[1][0:JQ, :]).then_inc(probs_out[1], 1)

            def mask_distance(row, r):
                wait(act, masked, G * (row - 1))
                sc.activation(mask[r % 2][:], s["pcol"][:], ACT.Abs, bias=s["centre"][:, one(row)])\
                    .then_inc(distances, 1)

            def exponents(b, r, g):
                act.wait_ge(masked, G * b + g + 1)
                p = prob[r % 2][:, g, :]
                sc.activation(p, p, ACT.Exp, bias=low[:, r % 2, g:g + 1], scale=-1.0,
                              accum_out=rsum[:, r % 2, g:g + 1]).then_inc(exped, 1)

            def keys_part(n, rn, g, uses):
                if g == 0:
                    act.wait_ge(k_in[rn % 2], 16 * uses)
                wait(act, keys_mm, G * (n - 1) + g + 1)
                sc.copy(kd[:, g, :, 0], kt[rn % 2][:, :, g]).then_inc(keys_high, 1)

            def keys_copy(n, rn, g):
                act.wait_ge(keys_mm, G * n + g + 1)
                sc.copy(ks[rn % 2][:, g, :], kt_ps[g % 2][:, 0:NPOS]).then_inc(keys_out, 1)

            def q_part(pair, u, uses):
                act.wait_ge(q_in[u], 16 * uses)
                wait(act, q_mm, 4 * pair)
                sc.copy(qd[:, :, 0:3:2, :].rearrange("p h a d -> p a h d"),
                        qn[u][:].rearrange("p (h d) -> p h d", h=H).unsqueeze(1).broadcast_to([128, 2, H, HD]))\
                    .then_inc(q_high, 1)

            def o_copy(pair):
                act.wait_ge(values_mm, 4 * pair)
                wait(act, wo_mm, pair - 1)
                sc.copy(ot[:].rearrange("p b k t -> p (b k t)"), o_ps[:]).then_inc(o_out, 1)

            def x3_copy(pair):
                act.wait_ge(x3_sum, pair)
                wait(act, l3_mm, pair - 1)
                sc.copy(x3h[:], x3[:]).then_inc(x3_high, 1)

            def z3_mask(pair):
                act.wait_ge(z3_mm, pair)
                act.wait_ge(keys_mm, min(8 * pair + 12, G * B) if isinstance(pair, int) else 8 * pair + 12)
                for u in range(2):
                    col = 2 * pair - 2 + u
                    ins = sc.mul(z3[:, T * u:T * u + T], z_ps[:, T * u:T * u + T], s["mask3"][:, one(col)])
                ins.then_inc(z3_out, 1)

            def out_copy(pair, u, uses):
                act.wait_ge(l3_mm, pair)
                act.wait_ge(out_stored[u], 16 * uses + 16)
                sc.copy(outs[u][:], m_ps[:]).then_inc(out_ready, 1)

            def body(i, first, last):
                for r in range(QUAD):
                    b, pair, u = QUAD * i + r, 2 * i + r // 2, r // 2
                    before, after = not (first and r == 0), not (last and r == QUAD - 1)
                    tail = r % 2 == 1 and not (first and u == 0)
                    for g in range(G):
                        if tail and g == 0:
                            o_copy(pair)
                        if r % 2 == 0 and not first and g == 2:
                            out_copy(pair - 1, u, i - 1)
                        exponents(b, r, g)
                        if before and g % 2 == 1:
                            probs_copy(b, g)
                        if tail and g == 3:
                            z3_mask(pair)
                        if after:
                            keys_copy(b + 1, r + 1, g)
                        if g == 0 and after:
                            keys_part(b + 1, r + 1, 3, 0)
                        elif g > 0 and not (last and r >= QUAD - 2):
                            keys_part(b + 2, r + 2, g - 1, 2 * i + (r + 2) // 2 + 1)
                        if r % 2 == 0 and g == 0 and not (last and u == 1):
                            q_part(pair + 1, (u + 1) % 2, i + 1 + u)
                        if after and g == 1:
                            mask_distance(b + 1, r + 1)
                        if tail and g == 2:
                            x3_copy(pair)

            for i in range(2):
                act.sem_inc(out_stored[i], 16)
            mask_distance(0, 0)
            for g in range(G):
                keys_part(0, 0, g, 1)
            q_part(0, 0, 1)
            for g in range(G):
                keys_copy(0, 0, g)
            for g in range(3):
                keys_part(1, 1, g, 1)
            quads(act, body)
            probs_copy(B, 1)
            out_copy(PAIRS - 1, 0, QUADS - 1)
            probs_copy(B, 3)
            o_copy(PAIRS)
            x3_copy(PAIRS)
            z3_mask(PAIRS)
            out_copy(PAIRS, 1, QUADS - 1)

        @block.vector
        def _(dve):
            v = nc.vector

            def mask_far(row, r):
                dve.wait_ge(distances, row + 1)
                v.tensor_scalar(mask[r % 2][:], mask[r % 2][:], s["half"][:, one(row)], MASKED,
                                ALU.is_gt, ALU.mult).then_inc(mask_step, 1)

            def probs_copy(b, g):
                dve.wait_ge(probs_mm, G * (b - 1) + g + 1)
                wait(dve, values_mm, 2 * (b - 1))
                v.tensor_copy(pt[g][:].rearrange("p o c -> p (o c)"), pt_ps[0][0:JQ, :]).then_inc(probs_out[0], 1)

            def inverse(n, r, g):
                dve.wait_ge(exped, n)
                v.reciprocal(rinv[:, r % 2, g:g + 1], rsum[:, r % 2, g:g + 1]).then_inc(summed, 1)

            def lowest(r, g):
                v.tensor_tensor_reduce(prob[r % 2][:, g, :], s_ps[g % 2][:, 0:NPOS], mask[r % 2][:], 1.0, 3e38,
                                       ALU.add, ALU.min, low[:, r % 2, g:g + 1]).then_inc(masked, 1)

            def normalise(n, r, g):
                dve.wait_ge(summed, n)
                p = prob[r % 2][:, g, :]
                v.tensor_scalar(p, p, rinv[:, r % 2, g:g + 1], None, ALU.mult).then_inc(normed, 1)

            def keys_rest(n, rn, g):
                dve.wait_ge(keys_high, G * n + g + 1)
                v.tensor_tensor(kd[:, g, :, 1], kt[rn % 2][:, :, g], kd[:, g, :, 0].bitcast(F32), ALU.subtract)\
                    .then_inc(keys_split, 1)

            def q_rest(pair, u):
                dve.wait_ge(q_high, pair + 1)
                v.tensor_tensor(qd[:, :, 1, :], qn[u][:].rearrange("p (h d) -> p h d", h=H),
                                qd[:, :, 0, :].bitcast(F32), ALU.subtract).then_inc(q_split, 1)

            def q_copy(pair, u, step):
                dve.wait_ge(q_mm, 4 * pair + step + 1)
                h = 4 * (step // 2)
                v.tensor_copy(qs[u][:, step % 2, :, h:h + 4, :],
                              m_ps[:].rearrange("p (h b t) -> p b h t", h=4, b=2)).then_inc(q_out, 1)

            def x3_add(pair, u, uses):
                dve.wait_ge(wo_mm, pair)
                dve.wait_ge(x2_in[u], 16 * uses)
                v.tensor_tensor(x3[:], m_ps[:].rearrange("p (k n) -> p k n", k=KC), x2[u][:], ALU.add)\
                    .then_inc(x3_sum, 1)

            def x3_rest(pair):
                dve.wait_ge(x3_high, pair)
                v.tensor_tensor(x3l[:], x3[:], x3h[:].bitcast(F32), ALU.subtract).then_inc(x3_low, 1)

            def body(i, first, last):
                for r in range(QUAD):
                    b, pair, u = QUAD * i + r, 2 * i + r // 2, r // 2
                    before, after = not (first and r == 0), not (last and r == QUAD - 1)
                    tail = r % 2 == 1 and not (first and u == 0)
                    for g in range(G):
                        if before and g % 2 == 0:
                            probs_copy(b, g)
                        prev = (G * b + g, r, g - 1) if g > 0 else (G * b, r - 1, G - 1)
                        dve.wait_ge(scores_mm, G * b + g + 1)
                        if g == 0:
                            dve.wait_ge(mask_step, b + 1)
                        if g > 0 or before:
                            inverse(*prev)
                        lowest(r, g)
                        if g > 0 or before:
                            normalise(*prev)
                        if g < 2 and after:
                            keys_rest(b + 1, r + 1, g + 2)
                        elif g >= 2 and not (last and r >= QUAD - 2):
                            keys_rest(b + 2, r + 2, g - 2)
                        if not (last and u == 1):
                            if r % 2 == 0 and g == 1:
                                q_rest(pair + 1, (u + 1) % 2)
                            elif g >= 2:
                                q_copy(pair + 1, (u + 1) % 2, 2 * (r % 2) + g - 2)
                        if tail and g == 1:
                            x3_add(pair, (u + 1) % 2, i + u)
                        if tail and g == 3:
                            x3_rest(pair)
                        if after and g == 3:
                            mask_far(b + 1, r + 1)

            mask_far(0, 0)
            for g in range(G):
                keys_rest(0, 0, g)
            q_rest(0, 0)
            for g in range(2):
                keys_rest(1, 1, g)
            for step in range(4):
                q_copy(0, 0, step)
            quads(dve, body)
            inverse(G * B, QUAD - 1, G - 1)
            normalise(G * B, QUAD - 1, G - 1)
            for g in (0, 2):
                probs_copy(B, g)
            x3_add(PAIRS, 1, QUADS)
            x3_rest(PAIRS)


def kernel(**inputs):
    import concourse.bacc as bacc
    from concourse.bass_utils import run_bass_kernel_spmd

    a = {k: np.asarray(v) for k, v in inputs.items()}

    def chunks(m):
        return m.reshape(KC, 128, m.shape[1]).transpose(1, 0, 2)

    def quarters(m):
        return m.transpose(0, 2, 1, 3).reshape(NCACHE * 4, ROW)

    def rows(m):
        return np.broadcast_to(m, (128,) + m.shape)

    conds, kv = (a["itok_B_1_198"], a["itok_B_0_3"], a["itok_B_0_6"]), a["itok_B_37_3939"]
    qk = [a["L2_cond_q_norm_scale"], a["L2_cond_k_norm_scale"]]
    hh = HD // 2
    p = np.arange(128)
    entry = np.arange(NE)
    order = (entry % B) * WR + entry // B
    inv = (np.float32(1) / np.float32(10000.0) ** (np.arange(hh, dtype=np.float32) / np.float32(hh))).astype(np.float32)
    ang = np.arange(MAXPOS, dtype=np.float32)[:, None] * inv
    cos, sin = np.cos(ang), np.sin(ang)
    o4, j, q = np.meshgrid(np.arange(4), np.arange(RD), np.arange(4), indexing="ij")
    laid = {
        "x_pairs": a["x"].reshape(PAIRS, 128, D),
        "l0w": a["L0_cond_weights"].reshape(CONDS * T, T),
        "wbt": chunks(a["L1_cond_W_base"].T), "wt": chunks(a["L1_cond_Wt"]), "wpt": chunks(a["L1_cond_Wp"].T),
        "at": chunks(a["L1_cond_A"].reshape(E1 * R, D).T),
        "bt": chunks(a["L1_cond_B_w"].transpose(1, 0, 2).reshape(D, E1 * R)),
        "wqt": chunks(a["L2_cond_Wq"].T),
        "wkvt": chunks(np.concatenate([a["L2_cond_Wk"].T, a["L2_cond_Wv"].T], axis=1)),
        "wot": a["L2_cond_Wo"].T.reshape(2, 2, 2, HD, D).transpose(1, 3, 0, 2, 4).reshape(128, KC, D),
        "w3t": chunks(a["L3_cond_W"].T),
        "a3t": chunks(a["L3_cond_A"].reshape(E3 * R, D).T),
        "b3": a["L3_cond_Bm"].transpose(0, 2, 1).reshape(E3 * R, D),
        "normscale": rows(np.stack([np.stack([m, np.concatenate([m[hh:], m[:hh]])]) for m in qk])),
        "k_rows": quarters(a["L2_cond_k_blocks"]),
        "v_rows": quarters(a["L2_cond_v_blocks"]),
        "kv_col": np.concatenate([kv, kv])[:, None],
        "table": np.concatenate([a["itok_Bx257_0_4111"]] * 2),
        "ints": rows(np.stack([kv, *conds])),
        "sc1": np.tile(np.repeat(a["L1_cond_scaling"], R), 2)[:, None],
        "sc3": np.repeat(a["L3_cond_scalings"], R)[:, None],
        "cols": np.stack([p % B, p % (E1 * R) // R, p // R, p // B], 1).astype(np.float32),
        "rows": rows(np.arange(512, dtype=np.float32)),
        "later": (np.arange(B)[:, None, None] * WR + np.arange(WR)[None, :, None] > order).astype(np.float32),
        "ident": np.eye(128, dtype=np.float32),
        "pcol": rows((16 * j + 4 * q + o4).reshape(-1).astype(np.float32)),
        "rope": np.concatenate([cos, cos, sin, sin], axis=1).astype(np.float32),
    }
    nc = bacc.Bacc("TRN2", target_bir_lowering=False, num_devices=1)
    arrays, t = {}, {}
    for name, m in laid.items():
        arrays[f"in_{name}"] = np.ascontiguousarray(m)
        t[name] = nc.dram_tensor(f"in_{name}", m.shape, mybir.dt.from_np(m.dtype), kind="ExternalInput").ap()
    t["out_pairs"] = nc.dram_tensor("out", (PAIRS, 128, D), F32, kind="ExternalOutput").ap()
    program(nc, t)
    r = run_bass_kernel_spmd(nc, [arrays], core_ids=[0])
    return r.results[0]["out"].reshape(B, T, D)
```

```python
from contextlib import ExitStack

import numpy as np
import concourse.bass as bass
from concourse import mybir

F32, F32R, I32 = mybir.dt.float32, mybir.dt.float32r, mybir.dt.int32
ALU, ACT, AX = mybir.AluOpType, mybir.ActivationFunctionType, mybir.AxisListType

B, T, D = 64, 64, 512
PAIRS = B // 2
KC = D // 128
H, G, HD = 8, 4, 64
NBLK, BLOCK, WINDOW = 257, 16, 256
NCACHE = 16 * NBLK
MAXPOS = NBLK * BLOCK
CONDS = 200
R = 16
E1, E3 = 4, 8
WR = T // BLOCK + 1
RD = 21
NE = WR * B
JQ = RD * 4
OQ = BLOCK // 4
ROW = OQ * G * HD
NPOS = RD * BLOCK
SKIP = float(1 << 20)
MASKED = 1e30
KEY = 1024
EPS = 1e-6
SCALE = 256.0 ** -0.5


def program(nc, t):
    with ExitStack() as whole:
        pk = nc.dram_tensor("patched_k", (NE * 4, ROW), F32).ap()
        pv = nc.dram_tensor("patched_v", (NE * 4, ROW), F32).ap()
        q_dram = nc.dram_tensor("q_rows", (PAIRS, 128, H * HD), F32).ap()
        x2_dram = nc.dram_tensor("x2_t", (PAIRS, 128, KC * 128), F32).ap()

        def keep(name, shape, dt=F32):
            return whole.enter_context(nc.sbuf_tensor(name, shape, dt))

        s = {
            "ident": keep("ident", [128, 128]),
            "wo": keep("wo", [128, KC, D]),
            "w3h": keep("w3h", [128, KC, D], F32R), "w3l": keep("w3l", [128, KC, D], F32R),
            "a3": keep("a3", [128, KC, E3 * R]),
            "b3": keep("b3", [128, D]),
            "mask1": keep("mask1", [128, B]), "mask3": keep("mask3", [128, B]),
            "pair_idx": keep("pair_idx", [128, PAIRS, 3], I32),
            "row_idx": keep("row_idx", [JQ, B, 2], I32),
            "centre": keep("minus_centre", [128, B]), "half": keep("half", [128, B]),
            "pcol": keep("pcol", [128, NPOS]),
        }
        with ExitStack() as early:
            def early_t(name, shape, dt=F32):
                return early.enter_context(nc.sbuf_tensor(name, shape, dt))
            w = {
                "wbh": early_t("wbh", [128, KC, D], F32R), "wbl": early_t("wbl", [128, KC, D], F32R),
                "wqh": early_t("wqh", [128, KC, D], F32R), "wql": early_t("wql", [128, KC, D], F32R),
                "wkvh": early_t("wkvh", [128, KC, D], F32R), "wkvl": early_t("wkvl", [128, KC, D], F32R),
                "awh": early_t("awh", [128, KC, 128], F32R), "awl": early_t("awl", [128, KC, 128], F32R),
                "pbh": early_t("pbh", [128, D], F32R), "pbl": early_t("pbl", [128, D], F32R),
                "normscale": early_t("normscale", [128, 2, 2, HD]),
            }
            with ExitStack() as c:
                prepare(nc, c, t, s, w, pk, pv)
            with ExitStack() as c:
                project(nc, c, t, s, w, pk, pv, q_dram, x2_dram)
        with ExitStack() as c:
            attend(nc, c, t, s, pk, pv, q_dram, x2_dram)


def prepare(nc, ctx, t, s, w, pk, pv):
    def sb(name, shape, dt=F32):
        return ctx.enter_context(nc.sbuf_tensor(f"prep_{name}", shape, dt))

    def sem(name):
        return ctx.enter_context(nc.semaphore(f"prep_{name}"))

    stage = [sb(f"stage{i}", [128, KC, D]) for i in range(2)]
    wt, wpt = sb("wt", [128, KC, D]), sb("wpt", [128, KC, D])
    at, bt = sb("at", [128, KC, E1 * R]), sb("bt", [128, KC, E1 * R])
    sc1, sc3 = sb("sc1", [128, 1]), sb("sc3", [128, 1])
    cols = sb("cols", [128, 4])
    rows = sb("rows", [128, 512])
    later = sb("later", [B, WR, NE])
    kv_col, table = sb("kv_col", [128, 1], I32), sb("table", [128, NBLK], I32)
    ints = sb("ints", [128, 4, B], I32)
    k_it, w_it = sb("k_it", [128, 4], I32), sb("w_it", [128, 3, B], I32)
    fcol = sb("fcol", [128, 4])
    frow = sb("frow", [128, 8, B])
    tablef, picked = sb("tablef", [128, NBLK]), sb("picked", [128, NBLK])
    slots, blocks = sb("slots", [128, RD + WR]), sb("blocks", [128, RD + WR])
    diag, ones = sb("diag", [B, WR, B]), sb("ones", [B, 128])
    xrow, key = sb("xrow", [128, NE]), sb("key", [128, NE])
    keyed = sb("keyed", [128, RD + WR])
    dist = sb("dist", [128, RD + WR, NE])
    first = sb("first", [128, RD + WR])
    found, cached, patched = sb("found", [128, RD]), sb("cached", [128, RD]), sb("patched", [128, RD])
    quarter = sb("quarter", [B, 2, JQ])
    over = sb("over", [B, WR, NE])
    valid = sb("valid", [B, WR, BLOCK])
    dest = sb("dest", [B, WR * BLOCK])
    onehot = sb("onehot", [B, BLOCK])
    move = sb("move", [B, 2, T])
    init_idx = sb("init_idx", [128, WR, 2], I32)
    initf = sb("initf", [128, WR, 2])
    blkbuf = [sb(f"blkbuf{i}", [128, ROW]) for i in range(4)]
    ps = [ctx.enter_context(nc.psum_tensor(f"prep_ps{i}", [128, 512], F32)) for i in range(4)]

    small_in, later_in, lora_in, keep_in = sem("small_in"), sem("later_in"), sem("lora_in"), sem("keep_in")
    stage_in = [sem(f"stage_in{i}") for i in range(2)]
    stage_free, wsplit_h = sem("stage_free"), sem("wsplit_h")
    step, pe_step, dist_ready = sem("step"), sem("pe_step"), sem("dist_ready")
    blk_in = [sem(f"blk_in{i}") for i in range(4)]
    blk_out = [sem(f"blk_out{i}") for i in range(4)]
    split_w = [("wbt", "wbh", "wbl", True), ("wqt", "wqh", "wql", False),
               ("wkvt", "wkvh", "wkvl", False), ("w3t", "w3h", "w3l", True)]
    smalls = [(cols, "cols"), (rows, "rows"), (kv_col, "kv_col"), (table, "table"),
              (sc1, "sc1"), (sc3, "sc3"), (ints, "ints"), (s["ident"], "ident"), (s["pcol"], "pcol")]
    marks = {}
    with nc.Block() as block:

        @block.vector
        def _(dve):
            n = [0]

            def link(ins, mark=None):
                n[0] += 1
                ins.then_inc(step, 1)
                dve.wait_ge(step, n[0])
                if mark:
                    marks[mark] = n[0]

            v = nc.vector
            dve.wait_ge(small_in, 16 * len(smalls))
            link(v.tensor_scalar(k_it[:, 0:1], kv_col[:], 4, None, ALU.arith_shift_right))
            link(v.tensor_scalar(k_it[:, 1:2], kv_col[:], 15, None, ALU.bitwise_and))
            link(v.tensor_scalar(k_it[:, 3:4], kv_col[:], float(WINDOW - 1), None, ALU.subtract))
            link(v.tensor_scalar(k_it[:, 2:3], k_it[:, 3:4], 4, None, ALU.arith_shift_right))
            link(v.tensor_copy(fcol[:, 0:3], k_it[:, 0:3]))
            link(v.tensor_copy(tablef[:], table[:]))
            link(v.tensor_scalar(slots[:, 0:RD], rows[:, 0:RD], fcol[:, 2:3], 0.0, ALU.add, ALU.max))
            link(v.tensor_scalar(slots[:, RD:], rows[:, 0:WR], fcol[:, 0:1], 0.0, ALU.add, ALU.max))
            link(v.tensor_scalar(slots[:], slots[:], float(NBLK - 1), None, ALU.min))
            for j in range(RD + WR):
                link(v.scalar_tensor_tensor(picked[:], rows[:, 0:NBLK], slots[:, j:j + 1], tablef[:],
                                            ALU.is_equal, ALU.mult, accum_out=blocks[:, j:j + 1]))
            for half in range(2):
                link(v.tensor_scalar(initf[:, :, half], blocks[:, RD:], 4.0, 2.0 * half, ALU.mult, ALU.add))
            link(v.tensor_scalar(initf[:], initf[:], cols[:, 3:4], None, ALU.add))
            link(v.tensor_copy(init_idx[:], initf[:]), "init_idx")
            link(v.memset(ones[:], 1.0))
            for j in range(WR):
                link(v.tensor_scalar(diag[:, j, :], s["ident"][0:B, 0:B], blocks[0:B, RD + j:RD + j + 1], None,
                                     ALU.mult), "diag" if j == WR - 1 else None)
            dve.wait_ge(pe_step, 3)
            link(v.tensor_copy(xrow[:], ps[2][:, 0:NE]))
            link(v.scalar_tensor_tensor(key[:], xrow[:], float(KEY), rows[:, 0:NE], ALU.mult, ALU.add))
            link(v.tensor_scalar(keyed[:], blocks[:], -float(KEY), None, ALU.mult), "keyed")
            dve.wait_ge(dist_ready, RD + WR)
            link(v.tensor_reduce(first[:], dist[:], AX.X, ALU.min))
            dve.wait_ge(later_in, 16)
            for j in range(WR):
                link(v.scalar_tensor_tensor(over[:, j, :], xrow[0:B, :], blocks[0:B, RD + j:RD + j + 1],
                                            later[:, j, :], ALU.is_equal, ALU.mult))
            link(v.memset(valid[:], 1.0))
            link(v.tensor_scalar(valid[:, 0, :], rows[0:B, 0:BLOCK], fcol[0:B, 1:2], None, ALU.is_ge))
            link(v.tensor_scalar(valid[:, WR - 1, :], rows[0:B, 0:BLOCK], fcol[0:B, 1:2], None, ALU.is_lt), "over")
            link(v.tensor_scalar(found[:], first[:, 0:RD], NE - 0.5, SKIP, ALU.is_lt, ALU.mult))
            link(v.tensor_tensor(cached[:], blocks[:, 0:RD], found[:], ALU.add))
            link(v.tensor_scalar(found[:], first[:, 0:RD], NE - 0.5, SKIP, ALU.is_gt, ALU.mult))
            link(v.tensor_scalar(patched[:], first[:, 0:RD], float(NE), None, ALU.min))
            link(v.tensor_tensor(patched[:], patched[:], found[:], ALU.add))
            for c, src in enumerate((cached, patched)):
                for q in range(4):
                    link(v.tensor_scalar(quarter[:, c, :].rearrange("b (j q) -> b j q", q=4)[:, :, q], src[0:B, :],
                                         4.0, float(q), ALU.mult, ALU.add),
                         "quarter" if (c, q) == (1, 3) else None)
            dve.wait_ge(pe_step, 4)
            d3 = dest[:].rearrange("b (j o) -> b j o", j=WR)
            link(v.tensor_scalar(dest[:], ps[3][0:B, 0:WR * BLOCK], 0.5, SKIP, ALU.is_gt, ALU.mult))
            for j in range(WR):
                link(v.scalar_tensor_tensor(d3[:, j, :], rows[0:B, 0:BLOCK], 1.0, d3[:, j, :], ALU.mult, ALU.add))
                link(v.tensor_scalar(keyed[0:B, j:j + 1], first[0:B, RD + j:RD + j + 1], float(BLOCK), None, ALU.mult))
                link(v.tensor_scalar(d3[:, j, :], d3[:, j, :], keyed[0:B, j:j + 1], None, ALU.add))
            link(v.tensor_scalar(onehot[:], rows[0:B, 0:BLOCK], fcol[0:B, 1:2], None, ALU.is_equal))
            link(v.tensor_scalar(move[:, 0, :], dest[:, 0:T], onehot[:, 0:1], None, ALU.mult))
            for o in range(1, BLOCK):
                link(v.scalar_tensor_tensor(move[:, 0, :], dest[:, o:o + T], onehot[:, o:o + 1], move[:, 0, :],
                                            ALU.mult, ALU.add))
            link(v.tensor_copy(move[:, 1, :], move[:, 0, :]), "move")
            dve.wait_ge(pe_step, 5)
            for c in range(2):
                link(v.tensor_copy(s["row_idx"][:, :, c], ps[2][0:JQ, c * B:c * B + B]))
            link(v.tensor_copy(frow[:, 0:4, :], ints[:]))
            p2 = frow[:].rearrange("p k (i two) -> p k i two", two=2)
            for half, rng in ((0, slice(0, 64)), (1, slice(64, 128))):
                link(v.tensor_scalar(frow[rng, 4, 0:PAIRS], p2[rng, 1, :, half], 64.0, cols[rng, 0:1],
                                     ALU.mult, ALU.add))
                link(v.tensor_scalar(frow[rng, 4, PAIRS:B], p2[rng, 0, :, half], cols[rng, 0:1], float(MAXPOS - 1),
                                     ALU.add, ALU.min))
            link(v.tensor_copy(s["pair_idx"][:, :, 0], frow[:, 4, 0:PAIRS]))
            link(v.tensor_copy(s["pair_idx"][:, :, 1], frow[:, 4, PAIRS:B]))
            dve.wait_ge(pe_step, 6)
            m2 = ps[3][:, 128:128 + B].rearrange("p (i two) -> p i two", two=2)
            for half, rng in ((0, slice(0, 64)), (1, slice(64, 128))):
                link(v.tensor_copy(s["pair_idx"][rng, :, 2], m2[rng, :, half]))
            link(v.tensor_scalar(w_it[:, 0, :], ints[:, 0, :], 1.0, None, ALU.add))
            link(v.tensor_scalar(w_it[:, 0, :], w_it[:, 0, :], 15, None, ALU.bitwise_and))
            link(v.tensor_scalar(w_it[:, 1, :], ints[:, 0, :], float(WINDOW - 1), None, ALU.subtract))
            link(v.tensor_scalar(w_it[:, 2, :], w_it[:, 1, :], 4, None, ALU.arith_shift_right))
            link(v.tensor_copy(frow[:, 5, :], w_it[:, 0, :]))
            link(v.tensor_copy(frow[:, 6, :], w_it[:, 2, :]))
            link(v.tensor_scalar(frow[:, 5, :], frow[:, 5, :], cols[:, 0:1], None, ALU.add))
            link(v.tensor_scalar(frow[:, 6, :], frow[:, 6, :], -16.0, 0.0, ALU.mult, ALU.max))
            link(v.tensor_tensor(frow[:, 6, :], frow[:, 6, :], frow[:, 5, :], ALU.max))
            link(v.tensor_scalar(frow[:, 5, :], frow[:, 5, :], float(WINDOW - 1), 0.5, ALU.add, ALU.mult))
            link(v.scalar_tensor_tensor(s["centre"][:], frow[:, 6, :], 0.5, frow[:, 5, :], ALU.mult, ALU.add))
            link(v.tensor_scalar(s["centre"][:], s["centre"][:], -1.0, None, ALU.mult))
            link(v.scalar_tensor_tensor(frow[:, 7, :], frow[:, 6, :], -0.5, frow[:, 5, :], ALU.mult, ALU.add))
            link(v.tensor_scalar(s["half"][:], frow[:, 7, :], 0.25, None, ALU.add))
            link(v.tensor_scalar(s["mask1"][:], frow[:, 2, :], cols[:, 1:2], sc1[:, 0:1], ALU.is_equal, ALU.mult))
            link(v.tensor_scalar(s["mask3"][:], frow[:, 3, :], cols[:, 2:3], sc3[:, 0:1], ALU.is_equal, ALU.mult))
            dve.wait_ge(keep_in, 64)
            dve.wait_ge(pe_step, 2)
            aw = ps[0][:, 0:KC * 64].rearrange("p (k m) -> p k m", k=KC)
            for d in range(2):
                link(v.tensor_copy(w["awh"][:, :, 64 * d:64 * d + 64], aw))
                link(v.tensor_tensor(w["awl"][:, :, 64 * d:64 * d + 64], aw,
                                     w["awh"][:, :, 64 * d:64 * d + 64].bitcast(F32), ALU.subtract))
            link(v.tensor_copy(w["pbh"][:], ps[1][:]))
            link(v.tensor_tensor(w["pbl"][:], ps[1][:], w["pbh"][:].bitcast(F32), ALU.subtract))
            link(v.tensor_scalar(w["normscale"][:], w["normscale"][:], 1.0, None, ALU.add))
            minus = w["normscale"][:, :, 1, 0:HD // 2]
            link(v.tensor_scalar(minus, minus, -1.0, None, ALU.mult))
            link(v.tensor_scalar(w["normscale"][:, 0], w["normscale"][:, 0], -SCALE, None, ALU.mult))
            both = {**s, **w}
            for i, (_, h, lo, eye) in enumerate(split_w):
                dve.wait_ge(stage_in[i % 2], 16 * (i // 2) + 16)
                for k in range(KC if eye else 0):
                    link(v.tensor_tensor(stage[i % 2][:, k, k * 128:k * 128 + 128],
                                         stage[i % 2][:, k, k * 128:k * 128 + 128], s["ident"][:], ALU.add))
                link(v.tensor_copy(both[h][:], stage[i % 2][:]))
                link(v.tensor_tensor(both[lo][:], stage[i % 2][:], both[h][:].bitcast(F32), ALU.subtract))
                dve.sem_inc(stage_free, 1)

        @block.sync
        def _(sp):
            for dst, name in smalls:
                sp.dma_start(dst[:], t[name]).then_inc(small_in, 16)
            sp.dma_start(later[:], t["later"]).then_inc(later_in, 16)
            for dst, name in ((wt, "wt"), (at, "at"), (bt, "bt"), (wpt, "wpt")):
                sp.dma_start(dst[:], t[name]).then_inc(lora_in, 16)
            for dst, name in ((s["wo"], "wot"), (s["a3"], "a3t"), (s["b3"], "b3"), (w["normscale"], "normscale")):
                sp.dma_start(dst[:], t[name]).then_inc(keep_in, 16)
            sp.wait_ge(keep_in, 64)
            for n in range(2 * WR * 2):
                table_out = (pk, pv)[n % 2].rearrange("(j b q) f -> j q b f", j=WR, q=4)
                j, half = divmod(n // 2, 2)
                sp.wait_ge(blk_in[n % 4], 16 * (n // 4) + 16)
                for q2 in range(2):
                    sp.dma_start(table_out[j, 2 * half + q2], blkbuf[n % 4][64 * q2:64 * q2 + 64, :])\
                        .then_inc(blk_out[n % 4], 16)
            for i in range(4):
                sp.wait_ge(blk_out[i], 32 * 5)

        @block.scalar
        def _(act):
            for n, (name, h, _, _) in enumerate(split_w[0:2]):
                act.dma_start(stage[n][:], t[name]).then_inc(stage_in[n], 16)
            act.wait_ge(step, marks["keyed"])
            for j in range(RD + WR):
                nc.scalar.activation(dist[:, j, :], key[:], ACT.Abs, bias=keyed[:, j:j + 1]).then_inc(dist_ready, 1)
            for n, (name, h, _, _) in enumerate(split_w):
                if n < 2:
                    continue
                act.wait_ge(stage_free, n - 1)
                act.dma_start(stage[n % 2][:], t[name]).then_inc(stage_in[n % 2], 16)

        @block.gpsimd
        def _(pool):
            pool.wait_ge(step, marks["init_idx"])
            for n in range(2 * WR * 2):
                j, half = divmod(n // 2, 2)
                if n >= 4:
                    pool.wait_ge(blk_out[n % 4], 32 * (n // 4))
                src = t["k_rows"] if n % 2 == 0 else t["v_rows"]
                pool.indirect_dma_start(blkbuf[n % 4][:], None, src,
                                        bass.IndirectOffsetOnAxis(ap=init_idx[:, j, half:half + 1], axis=0),
                                        bounds_check=NCACHE * 4 - 1, oob_is_err=False).then_inc(blk_in[n % 4], 16)

        @block.tensor
        def _(pe):
            pe.wait_ge(lora_in, 64)
            for m in range(KC):
                for k in range(KC):
                    mm = pe.matmul(ps[0][:, m * 64:m * 64 + 64], wt[:, k, m * 128:m * 128 + 128], at[:, k, :],
                                   start=(k == 0), stop=(k == KC - 1))
            mm.then_inc(pe_step, 1)
            for d in range(2):
                for k in range(KC):
                    mm = pe.matmul(ps[1][64 * d:64 * d + 64, :], bt[:, k, :], wpt[:, k, :],
                                   start=(k == 0), stop=(k == KC - 1))
            mm.then_inc(pe_step, 1)
            pe.wait_ge(step, marks["diag"])
            for j in range(WR):
                mm = pe.matmul(ps[2][:, j * B:j * B + B], ones[:, :], diag[:, j, :], start=True, stop=True)
            mm.then_inc(pe_step, 1)
            pe.wait_ge(step, marks["over"])
            for j in range(WR):
                for j2 in range(WR):
                    mm = pe.matmul(ps[3][0:B, j * BLOCK:j * BLOCK + BLOCK], over[:, j2, j * B:j * B + B],
                                   valid[:, j2, :], start=(j2 == 0), stop=(j2 == WR - 1))
            mm.then_inc(pe_step, 1)
            pe.wait_ge(step, marks["quarter"])
            for c in range(2):
                mm = pe.transpose(ps[2][0:JQ, c * B:c * B + B], quarter[:, c, :], s["ident"][0:B, 0:B])
            mm.then_inc(pe_step, 1)
            pe.wait_ge(step, marks["move"])
            pe.transpose(ps[3][:, 128:128 + B], move[:].rearrange("b a t -> b (a t)"),
                         s["ident"][0:B, 0:B]).then_inc(pe_step, 1)


def project(nc, ctx, t, s, w, pk, pv, q_dram, x2_dram):
    GP = 4
    TURNS = PAIRS // GP
    N = GP * 128

    def sb(name, shape, dt=F32):
        return ctx.enter_context(nc.sbuf_tensor(f"proj_{name}", shape, dt))

    def sem(name):
        return ctx.enter_context(nc.semaphore(f"proj_{name}"))

    xn = [sb(f"xn{p}", [128, D]) for p in range(GP)]
    cw = [sb(f"cw{p}", [128, T]) for p in range(GP)]
    mix = [sb(f"mix{p}", [128, 128]) for p in range(GP)]
    idx = [sb(f"idx{c}", [128, GP], I32) for c in range(3)]
    rope = [sb(f"rope{p}", [128, 2, HD]) for p in range(GP)]
    turn = sb("turn", [128, 2, 2, HD])
    x1h, x1l = sb("x1h", [128, KC, N], F32R), sb("x1l", [128, KC, N], F32R)
    zm, zs = sb("zm", [128, N]), sb("zs", [128, N], F32R)
    x2r, x2h, x2l = sb("x2r", [128, KC, N]), sb("x2h", [128, KC, N], F32R), sb("x2l", [128, KC, N], F32R)
    NH = H + G
    sq, y, t1, t2 = (sb(n, [128, NH, HD]) for n in ("sq", "y", "t1", "t2"))
    ss, ms, rs = (sb(n, [128, NH]) for n in ("ss", "ms", "rs"))
    q_out = [sb(f"q_out{i}", [128, H, HD]) for i in range(2)]
    kv_out = [sb(f"kv_out{p}", [128, 2, G, HD]) for p in range(GP)]

    x1_ps = [ctx.enter_context(nc.psum_tensor(f"x1_ps{i}", [128, KC, 128], F32)) for i in range(2)]
    x2_ps = [ctx.enter_context(nc.psum_tensor(f"x2_ps{i}", [128, N], F32)) for i in range(3)]
    z_ps = ctx.enter_context(nc.psum_tensor("z_ps", [128, N], F32))
    q_bank = ctx.enter_context(nc.psum_tensor("q_bank", [128, N], F32))
    kv_bank = ctx.enter_context(nc.psum_tensor("kv_bank", [128, N], F32))
    x2_at = x2_ps + [q_bank]
    q_ps = [m[:].rearrange("p (h d) -> p h d", h=H) for m in (q_bank, x2_ps[1])]
    kv_ps = [m[:].rearrange("p (v g d) -> p v g d", v=2, g=G) for m in (kv_bank, x2_ps[2])]

    x_in = [sem(f"x_in{p}") for p in range(GP)]
    cw_in, rope_in = [sem(f"cw_in{p}") for p in range(GP)], [sem(f"rope_in{p}") for p in range(GP)]
    begun = sem("begun")
    idx_ready, mix_zero, mix_ready = [sem(f"idx_ready{c}") for c in range(3)], sem("mix_zero"), sem("mix_ready")
    x1_mm, x1_high, x1_low = sem("x1_mm"), sem("x1_high"), sem("x1_low")
    z_mm, z_masked, z_high, z_low = sem("z_mm"), sem("z_masked"), sem("z_high"), sem("z_low")
    x2_mm, x2_raw, x2_high, x2_low = sem("x2_mm"), sem("x2_raw"), sem("x2_high"), sem("x2_low")
    x2_stored = sem("x2_stored")
    qkv_mm, squared = sem("qkv_mm"), sem("squared")
    averaged, rooted = sem("averaged"), sem("rooted")
    turn_ready, chain, scaled, turned = sem("turn_ready"), sem("chain"), sem("scaled"), sem("turned")
    q_stored = [sem(f"q_stored{i}") for i in range(2)]
    kv_scattered = [sem(f"kv_scattered{p}") for p in range(GP)]
    positions = [m.rearrange("r (o f) -> (r o) f", o=OQ) for m in (pk, pv)]

    def turns(engine, body):
        body(0, 2)
        with engine.Fori(1, TURNS - 2) as i:
            body(i, 2)
        body(TURNS - 2, 1)
        body(TURNS - 1, 0)

    def wait(engine, semaphore, value):
        if not isinstance(value, int) or value > 0:
            engine.wait_ge(semaphore, value)

    def some(x, n=1):
        return slice(x, x + n) if isinstance(x, int) else bass.ds(x, n)

    with nc.Block() as block:

        @block.sync
        def _(sp):
            def load(n, p, before):
                wait(sp, x1_mm, before)
                sp.dma_start(xn[p][:], t["x_pairs"][some(n)].rearrange("a p n -> p (a n)")).then_inc(x_in[p], 16)

            def body(i, follow):
                if follow:
                    for p in range(GP):
                        load(GP * i + GP + p, p, GP * i + p + 1)
                sp.wait_ge(x2_raw, KC * i + KC)
                for p in range(GP):
                    sp.dma_start(x2_dram[some(GP * i + p)].rearrange("a p (k n) -> p (a k) n", k=KC),
                                 x2r[:, :, p * 128:p * 128 + 128]).then_inc(x2_stored, 16)
                for p in range(GP):
                    sp.wait_ge(turned, GP * i + p + 1)
                    sp.dma_start(q_dram[some(GP * i + p)].rearrange("a p n -> p (a n)"),
                                 q_out[p % 2][:].rearrange("p h d -> p (h d)")).then_inc(q_stored[p % 2], 16)

            for p in range(GP):
                load(p, p, 0)
            turns(sp, body)
            sp.wait_ge(x2_stored, 16 * PAIRS)
            for i in range(2):
                sp.wait_ge(q_stored[i], 16 * PAIRS // 2)

        @block.gpsimd
        def _(pool):
            def columns(c, i):
                for p in range(GP):
                    wait(pool, (cw_in, rope_in, kv_scattered)[c][p], (32 if c == 2 else 16) * i)
                pool.sem_inc(begun, 1)
                pool.tensor_copy(idx[c][:], s["pair_idx"][:, some(GP * i, GP), c]).then_inc(idx_ready[c], 1)
                pool.wait_ge(idx_ready[c], i + 1)

            def weights(n, p):
                wait(pool, mix_ready, n - GP + 1)
                pool.sem_inc(begun, 1)
                pool.indirect_dma_start(cw[p][:], None, t["l0w"],
                                        bass.IndirectOffsetOnAxis(ap=idx[0][:, p:p + 1], axis=0),
                                        bounds_check=CONDS * T - 1, oob_is_err=False).then_inc(cw_in[p], 16)

            def angles(n, p):
                wait(pool, turn_ready, n - GP + 1)
                pool.sem_inc(begun, 1)
                pool.indirect_dma_start(rope[p][:].rearrange("p a d -> p (a d)"), None, t["rope"],
                                        bass.IndirectOffsetOnAxis(ap=idx[1][:, p:p + 1], axis=0),
                                        bounds_check=MAXPOS - 1, oob_is_err=False).then_inc(rope_in[p], 16)

            def body(i, follow):
                columns(2, i)
                if follow > 0:
                    columns(1, i + 1)
                if follow > 1:
                    columns(0, i + 2)
                for p in range(GP):
                    n = GP * i + p
                    pool.wait_ge(turned, n + 1)
                    pool.wait_ge(squared, n + 1)
                    pool.sem_inc(begun, 1)
                    for kv in range(2):
                        pool.indirect_dma_start(positions[kv],
                                                bass.IndirectOffsetOnAxis(ap=idx[2][:, p:p + 1], axis=0),
                                                kv_out[p][:, kv].rearrange("p g d -> p (g d)"), None,
                                                bounds_check=NE * BLOCK - 1, oob_is_err=False)\
                            .then_inc(kv_scattered[p], 16)
                    if follow > 0:
                        angles(n + GP, p)
                    if follow > 1:
                        weights(n + 2 * GP, p)

            for p in range(GP):
                pool.memset(mix[p][:], 0.0).then_inc(mix_zero, 1)
            columns(0, 0)
            for p in range(GP):
                weights(p, p)
            columns(1, 0)
            for p in range(GP):
                angles(p, p)
            columns(0, 1)
            for p in range(GP):
                weights(GP + p, p)
            turns(pool, body)
            for p in range(GP):
                pool.wait_ge(kv_scattered[p], 32 * TURNS)

        @block.tensor
        def _(pe):
            def mix_tokens(i, n, p):
                pe.wait_ge(x_in[p], 16 * i + 16)
                pe.wait_ge(mix_ready, n + 1)
                wait(pe, x1_low, n - 1)
                for k in range(KC):
                    mm = pe.matmul(x1_ps[p % 2][:, k, :], xn[p][:, k * 128:k * 128 + 128], mix[p][:],
                                   start=True, stop=True)
                mm.then_inc(x1_mm, 1)

            def base(i, o):
                oc = slice(o * 128, o * 128 + 128)
                if o == 0:
                    wait(pe, x2_high, KC * i)
                elif o == 1:
                    wait(pe, scaled, GP * i)
                    wait(pe, squared, GP * i)
                for k in range(KC):
                    for m, (wa, xa) in enumerate((("wbh", x1h), ("wbh", x1l), ("wbl", x1h))):
                        pe.matmul(x2_at[o][:], w[wa][:, k, oc], xa[:, k, :],
                                  start=(k == 0 and m == 0), stop=False)

            def lora(o):
                oc = slice(o * 128, o * 128 + 128)
                pe.matmul(x2_at[o][:], w["pbh"][:, oc], zs[:], start=False, stop=False)
                pe.matmul(x2_at[o][:], w["pbl"][:, oc], zs[:], start=False, stop=True).then_inc(x2_mm, 1)

            def body(i, follow):
                pe.wait_ge(x1_low, GP * i + GP)
                wait(pe, z_masked, i)
                for k in range(KC):
                    for m, (wa, xa) in enumerate((("awh", x1h), ("awh", x1l), ("awl", x1h))):
                        mm = pe.matmul(z_ps[:], w[wa][:, k, :], xa[:, k, :],
                                       start=(k == 0 and m == 0), stop=(k == KC - 1 and m == 2))
                mm.then_inc(z_mm, 1)
                base(i, 0)
                base(i, 1)
                base(i, 2)
                pe.wait_ge(z_low, i + 1)
                lora(0)
                lora(1)
                base(i, 3)
                lora(2)
                lora(3)
                if follow:
                    mix_tokens(i + 1, GP * i + GP, 0)
                for p in range(GP):
                    n = GP * i + p
                    if follow and p < GP - 1:
                        mix_tokens(i + 1, n + GP + 1, p + 1)
                    if p == 0:
                        pe.wait_ge(x2_low, KC * i + KC)
                    wait(pe, scaled, n - 1)
                    wait(pe, squared, n - 1)
                    tok = slice(p * 128, p * 128 + 128)
                    for out, wh, wl in ((q_ps[p % 2].rearrange("p a b -> p (a b)"), "wqh", "wql"),
                                        (kv_ps[p % 2].rearrange("p a b c -> p (a b c)"), "wkvh", "wkvl")):
                        for k in range(KC):
                            for m, (xa, wa) in enumerate(((x2h, wh), (x2l, wh), (x2h, wl))):
                                mm = pe.matmul(out, xa[:, k, tok], w[wa][:, k, :],
                                               start=(k == 0 and m == 0), stop=(k == KC - 1 and m == 2))
                    mm.then_inc(qkv_mm, 1)

            for p in range(GP):
                mix_tokens(0, p, p)
            turns(pe, body)

        @block.scalar
        def _(act):
            sc = nc.scalar

            def x1_part(n, p):
                act.wait_ge(x1_mm, n + 1)
                sc.copy(x1h[:, :, p * 128:p * 128 + 128], x1_ps[p % 2][:]).then_inc(x1_high, 1)

            def body(i, follow):
                act.wait_ge(z_masked, i + 1)
                sc.copy(zs[:], zm[:]).then_inc(z_high, 1)
                for o in range(KC):
                    act.wait_ge(x2_mm, KC * i + o + 1)
                    if o == 0:
                        wait(act, x2_stored, 16 * GP * i)
                    sc.copy(x2r[:, o, :], x2_at[o][:]).then_inc(x2_raw, 1)
                    sc.copy(x2h[:, o, :], x2_at[o][:]).then_inc(x2_high, 1)
                if follow:
                    x1_part(GP * i + GP, 0)
                for p in range(GP):
                    if follow and p < GP - 1:
                        x1_part(GP * i + GP + p + 1, p + 1)
                    act.wait_ge(qkv_mm, GP * i + p + 1)
                    wait(act, scaled, GP * i + p)
                    sc.activation(sq[:, 0:H, :], q_ps[p % 2], ACT.Square)
                    sc.activation(sq[:, H:NH, :], kv_ps[p % 2][:, 0], ACT.Square)
                    wait(act, kv_scattered[p], 32 * i)
                    sc.copy(kv_out[p][:, 1], kv_ps[p % 2][:, 1]).then_inc(squared, 1)
                    act.wait_ge(averaged, GP * i + p + 1)
                    sc.activation(rs[:], ms[:], ACT.Sqrt).then_inc(rooted, 1)

            for p in range(GP):
                x1_part(p, p)
            turns(act, body)

        @block.vector
        def _(dve):
            v = nc.vector

            def mixer(i, n, p):
                dve.wait_ge(cw_in[p], 16 * i + 16)
                wait(dve, x1_mm, n - GP + 1)
                for r in (slice(0, 64), slice(64, 128)):
                    ins = v.tensor_tensor(mix[p][r, r], cw[p][r, :], s["ident"][r, r], ALU.add)
                ins.then_inc(mix_ready, 1)

            def x1_rest(n, p):
                dve.wait_ge(x1_high, n + 1)
                tok = slice(p * 128, p * 128 + 128)
                v.tensor_tensor(x1l[:, :, tok], x1_ps[p % 2][:], x1h[:, :, tok].bitcast(F32), ALU.subtract)\
                    .then_inc(x1_low, 1)

            def norm_and_turn(i, n, p):
                dve.wait_ge(rope_in[p], 16 * i + 16)
                v.tensor_tensor(turn[:], rope[p][:].unsqueeze(1).broadcast_to([128, 2, 2, HD]),
                                w["normscale"][:], ALU.mult).then_inc(turn_ready, 1)
                dve.wait_ge(squared, n + 1)
                v.tensor_reduce(ss[:], sq[:], AX.X, ALU.add).then_inc(chain, 1)
                dve.wait_ge(chain, 3 * n + 1)
                v.tensor_scalar(ms[:], ss[:], 1.0 / HD, EPS, ALU.mult, ALU.add).then_inc(averaged, 1)
                dve.wait_ge(rooted, n + 1)
                v.reciprocal(ss[:], rs[:]).then_inc(chain, 1)
                dve.wait_ge(chain, 3 * n + 2)
                v.tensor_tensor(y[:, 0:H, :], q_ps[p % 2], ss[:, 0:H].unsqueeze(2).broadcast_to([128, H, HD]), ALU.mult)
                v.tensor_tensor(y[:, H:NH, :], kv_ps[p % 2][:, 0], ss[:, H:NH].unsqueeze(2).broadcast_to([128, G, HD]),
                                ALU.mult).then_inc(scaled, 1)
                dve.wait_ge(scaled, n + 1)
                dve.wait_ge(turn_ready, n + 1)
                hh = HD // 2
                for k, (a, b) in enumerate(((0, H), (H, NH))):
                    m = b - a
                    v.tensor_tensor(t1[:, a:b, :], y[:, a:b, :],
                                    turn[:, k, 0, :].unsqueeze(1).broadcast_to([128, m, HD]), ALU.mult)
                    for u in range(2):
                        ins = v.tensor_tensor(t2[:, a:b, u * hh:u * hh + hh], y[:, a:b, hh - u * hh:HD - u * hh],
                                              turn[:, k, 1, u * hh:u * hh + hh].unsqueeze(1)
                                              .broadcast_to([128, m, hh]), ALU.mult)
                ins.then_inc(chain, 1)
                dve.wait_ge(chain, 3 * n + 3)
                wait(dve, q_stored[p % 2], 16 * (2 * i + p // 2))
                v.tensor_tensor(q_out[p % 2][:], t1[:, 0:H, :], t2[:, 0:H, :], ALU.add)
                wait(dve, kv_scattered[p], 32 * i)
                v.tensor_tensor(kv_out[p][:, 0], t1[:, H:NH, :], t2[:, H:NH, :], ALU.add).then_inc(turned, 1)

            def body(i, follow):
                dve.wait_ge(z_mm, i + 1)
                v.tensor_tensor(zm[:].rearrange("p (b t) -> p b t", t=T), z_ps[:].rearrange("p (b t) -> p b t", t=T),
                                s["mask1"][:, some(2 * GP * i, 2 * GP)].unsqueeze(2).broadcast_to([128, 2 * GP, T]),
                                ALU.mult).then_inc(z_masked, 1)
                dve.wait_ge(z_high, i + 1)
                v.tensor_tensor(zs[64:128, :], zm[64:128, :], zs[64:128, :].bitcast(F32), ALU.subtract)\
                    .then_inc(z_low, 1)
                if follow:
                    for p in range(GP):
                        mixer(i + 1, GP * i + GP + p, p)
                for o in range(KC):
                    dve.wait_ge(x2_high, KC * i + o + 1)
                    v.tensor_tensor(x2l[:, o, :], x2r[:, o, :], x2h[:, o, :].bitcast(F32), ALU.subtract)\
                        .then_inc(x2_low, 1)
                if follow:
                    x1_rest(GP * i + GP, 0)
                for p in range(GP):
                    if follow and p < GP - 1:
                        x1_rest(GP * i + GP + p + 1, p + 1)
                    norm_and_turn(i, GP * i + p, p)

            dve.wait_ge(mix_zero, GP)
            for p in range(GP):
                mixer(0, p, p)
            for p in range(GP):
                x1_rest(p, p)
            turns(dve, body)


def attend(nc, ctx, t, s, pk, pv, q_dram, x2_dram):
    QUAD = 4

    def sb(name, shape, dt=F32):
        return ctx.enter_context(nc.sbuf_tensor(f"attn_{name}", shape, dt))

    def sem(name):
        return ctx.enter_context(nc.semaphore(f"attn_{name}"))

    ridx = [sb(f"ridx{i}", [JQ, 2], I32) for i in range(QUAD)]
    kt = [sb(f"kt{i}", [JQ, OQ, G, HD]) for i in range(2)]
    vt = [sb(f"vt{i}", [JQ, OQ, G, HD]) for i in range(QUAD)]
    ks = [sb(f"ks{i}", [128, G, NPOS], F32R) for i in range(2)]
    qn = [sb(f"qn{i}", [128, H, 2, HD]) for i in range(2)]
    qs = [sb(f"qs{i}", [128, 2, 2, H, T], F32R) for i in range(2)]
    mask = [sb(f"mask{i}", [128, NPOS]) for i in range(2)]
    prob = [sb(f"prob{i}", [128, G, NPOS]) for i in range(2)]
    low, rsum, rinv = (sb(n, [128, 2, G]) for n in ("low", "rsum", "rinv"))
    pt = [sb(f"pt{g}", [JQ, 4, 128]) for g in range(G)]
    x2 = [sb(f"x2_{i}", [128, KC, 128]) for i in range(2)]
    ot = sb("ot", [128, 2, KC, T])
    x3, x3h, x3l = sb("x3", [128, KC, 128]), sb("x3h", [128, KC, 128], F32R), sb("x3l", [128, KC, 128], F32R)
    z3 = sb("z3", [128, 128])
    outs = [sb(f"outs{i}", [128, D]) for i in range(2)]

    def pb(name):
        return ctx.enter_context(nc.psum_tensor(name, [128, 512], F32))

    kt_ps, s_ps, pt_ps = ([pb(f"{n}{i}") for i in range(2)] for n in ("kt_ps", "s_ps", "pt_ps"))
    o_ps, m_ps = pb("o_ps"), pb("m_ps")
    z_ps = kt_ps[1][:, 384:512]

    begun = sem("begun")
    idx_ready = sem("idx_ready")
    k_base, k_in = [sem(f"k_base{i}") for i in range(2)], [sem(f"k_in{i}") for i in range(2)]
    v_base, v_in = [sem(f"v_base{i}") for i in range(QUAD)], [sem(f"v_in{i}") for i in range(QUAD)]
    q_in, x2_in = [sem(f"q_in{i}") for i in range(2)], [sem(f"x2_in{i}") for i in range(2)]
    keys_mm, keys_high, keys_out = (sem(n) for n in ("keys_mm", "keys_high", "keys_out"))
    q_mm, q_high, q_out = (sem(n) for n in ("q_mm", "q_high", "q_out"))
    scores_mm, masked, exped, summed, normed, mask_step = (sem(n) for n in (
        "scores_mm", "masked", "exped", "summed", "normed", "mask_step"))
    distances = sem("distances")
    probs_mm, probs_out = sem("probs_mm"), [sem(f"probs_out{i}") for i in range(2)]
    values_mm, o_out = sem("values_mm"), sem("o_out")
    wo_mm, x3_sum, x3_high, x3_low = sem("wo_mm"), sem("x3_sum"), sem("x3_high"), sem("x3_low")
    z3_mm, z3_out, l3_mm, out_ready = sem("z3_mm"), sem("z3_out"), sem("l3_mm"), sem("out_ready")
    out_stored = [sem(f"out_stored{i}") for i in range(2)]
    QUADS = B // QUAD

    def quads(engine, body):
        body(0, True, False)
        with engine.Fori(1, QUADS - 1) as i:
            body(i, False, False)
        body(QUADS - 1, False, True)

    def wait(engine, semaphore, value):
        if not isinstance(value, int) or value > 0:
            engine.wait_ge(semaphore, value)

    def one(x):
        return slice(x, x + 1) if isinstance(x, int) else bass.ds(x, 1)

    def at_most(value, limit):
        return min(value, limit) if isinstance(value, int) else value

    with nc.Block() as block:

        @block.sync
        def _(sp):
            def load_q(pair, u, before):
                wait(sp, q_mm, 2 * before)
                for a in range(2):
                    sp.dma_start(qn[u][:, :, a, :], q_dram[one(pair)].rearrange("a p (h d) -> p (a h) d", h=H))\
                        .then_inc(q_in[u], 16)

            def store(pair, u):
                sp.wait_ge(out_ready, pair + 1)
                sp.dma_start(t["out_pairs"][one(pair)].rearrange("a p n -> p (a n)"), outs[u][:])\
                    .then_inc(out_stored[u], 16)

            def body(i, first, last):
                for u in range(2):
                    pair = 2 * i + u
                    if not (last and u == 1):
                        load_q(pair + 1, (u + 1) % 2, pair)
                    wait(sp, x3_sum, pair - 1)
                    sp.dma_start(x2[u][:].rearrange("p k n -> p (k n)"),
                                 x2_dram[one(pair)].rearrange("a p n -> p (a n)")).then_inc(x2_in[u], 16)
                    if not first:
                        store(pair - 2, u)

            load_q(0, 0, 0)
            quads(sp, body)
            for u in range(2):
                store(PAIRS - 2 + u, u)
            for u in range(2):
                sp.wait_ge(out_stored[u], 16 * PAIRS // 2 + 16)

        @block.gpsimd
        def _(pool):
            def gather(dst, table, col, bound, done):
                pool.sem_inc(begun, 1)
                pool.indirect_dma_start(dst[:].rearrange("p o g d -> p (o g d)"), None, table, bass.IndirectOffsetOnAxis(ap=col, axis=0),
                                        bounds_check=bound, oob_is_err=False).then_inc(done, 16)

            def columns(row, r, turns):
                wait(pool, v_in[r], 16 * turns)
                pool.sem_inc(begun, 1)
                pool.tensor_copy(ridx[r][:], s["row_idx"][:, one(row), :].rearrange("p a k -> p (a k)"))\
                    .then_inc(idx_ready, 1)
                pool.wait_ge(idx_ready, row + 1)

            def keys(row, r):
                wait(pool, keys_mm, 2 * (row - 1))
                gather(kt[r % 2], t["k_rows"], ridx[r][:, 0:1], NCACHE * 4 - 1, k_base[r % 2])

            def keys_written(row, r, uses):
                pool.wait_ge(k_base[r % 2], 16 * uses)
                gather(kt[r % 2], pk, ridx[r][:, 1:2], NE * 4 - 1, k_in[r % 2])

            def values(row, r):
                wait(pool, values_mm, 2 * (row - 3))
                gather(vt[r], t["v_rows"], ridx[r][:, 0:1], NCACHE * 4 - 1, v_base[r])

            def values_written(r, turns):
                pool.wait_ge(v_base[r], 16 * turns)
                gather(vt[r], pv, ridx[r][:, 1:2], NE * 4 - 1, v_in[r])

            def body(i, first, last):
                for r in range(QUAD):
                    b = QUAD * i + r
                    n, m = (r + 1) % QUAD, (r + 2) % QUAD
                    if not (last and r >= QUAD - 2):
                        columns(b + 2, m, i + (r + 2) // QUAD)
                        keys(b + 2, m)
                    if not (last and r == QUAD - 1):
                        values(b + 1, n)
                    if not (last and r >= QUAD - 2):
                        keys_written(b + 2, m, 2 * i + (r + 2) // 2 + 1)
                    if not (last and r == QUAD - 1):
                        values_written(n, i + 1 + (r + 1) // QUAD)

            for r in range(2):
                columns(r, r, 0)
                keys(r, r)
                keys_written(r, r, 1)
            values(0, 0)
            values_written(0, 1)
            quads(pool, body)

        @block.tensor
        def _(pe):
            def turn_probs(b, r, g):
                pe.wait_ge(normed, G * (b - 1) + g + 1)
                wait(pe, probs_out[g % 2], 2 * (b - 1) + g // 2)
                for o in range(4):
                    mm = pe.transpose(pt_ps[g % 2][0:JQ, o * 128:o * 128 + 128],
                                      prob[(r - 1) % 2][:, g, o * JQ:o * JQ + JQ], s["ident"][:])
                mm.then_inc(probs_mm, 1)

            def scores(b, r, g, pair):
                pe.wait_ge(keys_out, G * b + g + 1)
                if r % 2 == 0:
                    pe.wait_ge(q_out, 2 * pair + g // 2 + 1)
                wait(pe, masked, G * b + g - 1)
                for m in range(2):
                    mm = pe.matmul(s_ps[g % 2][:, 0:NPOS],
                                   qs[r // 2][:, m, r % 2, 2 * g:2 * g + 2, :].rearrange("p h t -> p (h t)"),
                                   ks[r % 2][:, g, :], start=(m == 0), stop=(m == 1))
                mm.then_inc(scores_mm, 1)

            def turn_keys(n, rn, c, uses):
                if c == 0:
                    pe.wait_ge(k_in[rn % 2], 16 * uses)
                wait(pe, keys_out, G * (n - 1) + 2 * c + 2)
                for o in range(OQ):
                    mm = pe.transpose(kt_ps[c][:, o * JQ:o * JQ + JQ],
                                      kt[rn % 2][:, o, 2 * c:2 * c + 2].rearrange("p g d -> p (g d)"),
                                      s["ident"][0:JQ, 0:JQ])
                mm.then_inc(keys_mm, 1)

            def turn_q(pair, u, step, uses):
                if step == 0:
                    pe.wait_ge(q_in[u], 32 * uses)
                    wait(pe, out_ready, pair - 2)
                else:
                    wait(pe, x3_sum, pair - 1)
                wait(pe, q_out, 2 * pair + step)
                for h in range(4):
                    mm = pe.transpose(m_ps[:, h * 128:h * 128 + 128],
                                      qn[u][:, 4 * step + h].rearrange("p a d -> p (a d)"), s["ident"][:])
                mm.then_inc(q_mm, 1)

            def sums(row, r, c, turns, pair):
                for j in range(2):
                    pe.wait_ge(probs_out[j], 2 * row + c + 1)
                if c == 0:
                    pe.wait_ge(v_in[r], 16 * turns)
                    if r % 2 == 0:
                        wait(pe, o_out, pair)
                at = (r % 2) * 256 + c * 128
                for o in range(OQ):
                    for g2 in range(2):
                        mm = pe.matmul(o_ps[64 * g2:64 * g2 + 64, at:at + 128], vt[r][:, o, 2 * c + g2, :],
                                       pt[2 * c + g2][:, o, :], start=(o == 0), stop=(o == OQ - 1))
                mm.then_inc(values_mm, 1)

            def wo(pair, half):
                if half == 0:
                    pe.wait_ge(o_out, pair)
                    wait(pe, out_ready, pair - 1)
                    pe.wait_ge(q_out, at_most(2 * pair + 3, 2 * PAIRS))
                for m in (2 * half, 2 * half + 1):
                    for k in range(KC):
                        mm = pe.matmul(m_ps[:, m * 128:m * 128 + 128], s["wo"][:, k, m * 128:m * 128 + 128],
                                       ot[:, :, k, :], start=(k == 0), stop=(k == KC - 1))
                if half == 1:
                    mm.then_inc(wo_mm, 1)

            def lora3(pair):
                pe.wait_ge(x3_sum, pair)
                pe.wait_ge(keys_out, at_most(8 * pair + 12, G * B))
                wait(pe, z3_out, pair - 1)
                for k in range(KC):
                    mm = pe.matmul(z_ps, s["a3"][:, k, :], x3[:, k, :], start=(k == 0), stop=(k == KC - 1))
                mm.then_inc(z3_mm, 1)

            def out3(pair, half):
                if half == 0:
                    pe.wait_ge(x3_low, pair)
                    pe.wait_ge(x3_sum, pair)
                    pe.wait_ge(q_out, at_most(2 * pair + 4, 2 * PAIRS))
                for k in (2 * half, 2 * half + 1):
                    for m, (xa, wa) in enumerate(((x3h, "w3h"), (x3l, "w3h"), (x3h, "w3l"))):
                        pe.matmul(m_ps[:], xa[:, k, :], s[wa][:, k, :], start=(k == 0 and m == 0), stop=False)

            def adapters3(pair):
                pe.wait_ge(z3_out, pair)
                pe.matmul(m_ps[:], z3[:], s["b3"][:], start=False, stop=True).then_inc(l3_mm, 1)

            def body(i, first, last):
                for r in range(QUAD):
                    b, pair, u = QUAD * i + r, 2 * i + r // 2, r // 2
                    before, after = not (first and r == 0), not (last and r == QUAD - 1)
                    tail = r % 2 == 1 and not (first and u == 0)
                    for g in range(G):
                        scores(b, r, g, pair)
                        if before:
                            turn_probs(b, r, g)
                        if g == 0 and not (first and r < 2):
                            sums(b - 2, (r + 2) % QUAD, 1, 0, 0)
                        if r % 2 == 0 and not first and g in (1, 2):
                            out3(pair - 1, g - 1)
                            if g == 1:
                                lora3(pair - 1)
                        if tail and g in (1, 2):
                            wo(pair, g - 1)
                        if after and g % 2 == 0:
                            if g == 2 and r % 2 == 0:
                                wait(pe, z3_out, pair - 1)
                            turn_keys(b + 1, r + 1, g // 2, 2 * i + (r + 1) // 2 + 1)
                        if r % 2 == 0 and not first and g == 2:
                            adapters3(pair - 1)
                        if g == 3:
                            if r % 2 == 1 and not (last and u == 1):
                                turn_q(pair + 1, (u + 1) % 2, r % 2, i + 1 + u)
                            if before:
                                sums(b - 1, (r - 1) % QUAD, 0, i + (r > 0), pair)
                            if r % 2 == 0 and not (last and u == 1):
                                turn_q(pair + 1, (u + 1) % 2, r % 2, i + 1 + u)

            for c in range(2):
                turn_keys(0, 0, c, 1)
            for step in range(2):
                turn_q(0, 0, step, 1)
            quads(pe, body)
            turn_probs(B, 0, 0)
            sums(B - 2, QUAD - 2, 1, 0, 0)
            turn_probs(B, 0, 1)
            out3(PAIRS - 1, 0)
            lora3(PAIRS - 1)
            turn_probs(B, 0, 2)
            out3(PAIRS - 1, 1)
            adapters3(PAIRS - 1)
            turn_probs(B, 0, 3)
            for c in range(2):
                sums(B - 1, QUAD - 1, c, QUADS, PAIRS)
            for half in range(2):
                wo(PAIRS, half)
            lora3(PAIRS)
            for half in range(2):
                out3(PAIRS, half)
            adapters3(PAIRS)

        @block.scalar
        def _(act):
            sc = nc.scalar

            def probs_copy(b, g):
                act.wait_ge(probs_mm, G * (b - 1) + g + 1)
                wait(act, values_mm, 2 * (b - 2) + g // 2 + 1)
                sc.copy(pt[g][:].rearrange("p o c -> p (o c)"), pt_ps[1][0:JQ, :]).then_inc(probs_out[1], 1)

            def mask_distance(row, r):
                wait(act, masked, G * (row - 1))
                sc.activation(mask[r % 2][:], s["pcol"][:], ACT.Abs, bias=s["centre"][:, one(row)])\
                    .then_inc(distances, 1)

            def exponents(b, r, g):
                act.wait_ge(masked, G * b + g + 1)
                p = prob[r % 2][:, g, :]
                sc.activation(p, p, ACT.Exp, bias=low[:, r % 2, g:g + 1], scale=-1.0,
                              accum_out=rsum[:, r % 2, g:g + 1]).then_inc(exped, 1)

            def keys_part(n, rn, g):
                act.wait_ge(keys_mm, 2 * n + g // 2 + 1)
                at = slice(64 * (g % 2), 64 * (g % 2) + 64)
                sc.copy(ks[rn % 2][at, g, :], kt_ps[g // 2][at, 0:NPOS]).then_inc(keys_high, 1)

            def q_part(pair, u, step):
                act.wait_ge(q_mm, 2 * pair + step + 1)
                sc.copy(qs[u][:, 0, :, 4 * step:4 * step + 4, :],
                        m_ps[:].rearrange("p (h b t) -> p b h t", h=4, b=2)).then_inc(q_high, 1)

            def o_copy(pair):
                act.wait_ge(values_mm, 4 * pair)
                wait(act, wo_mm, pair - 1)
                sc.copy(ot[:].rearrange("p b k t -> p (b k t)"), o_ps[:]).then_inc(o_out, 1)

            def x3_copy(pair):
                act.wait_ge(x3_sum, pair)
                wait(act, l3_mm, pair - 1)
                sc.copy(x3h[:], x3[:]).then_inc(x3_high, 1)

            def z3_mask(pair):
                act.wait_ge(z3_mm, pair)
                for u in range(2):
                    col = 2 * pair - 2 + u
                    ins = sc.mul(z3[:, T * u:T * u + T], z_ps[:, T * u:T * u + T], s["mask3"][:, one(col)])
                ins.then_inc(z3_out, 1)

            def out_copy(pair, u, uses):
                act.wait_ge(l3_mm, pair)
                act.wait_ge(out_stored[u], 16 * uses + 16)
                sc.copy(outs[u][:], m_ps[:]).then_inc(out_ready, 1)

            def body(i, first, last):
                for r in range(QUAD):
                    b, pair, u = QUAD * i + r, 2 * i + r // 2, r // 2
                    before, after = not (first and r == 0), not (last and r == QUAD - 1)
                    tail = r % 2 == 1 and not (first and u == 0)
                    for g in range(G):
                        if r % 2 == 0 and not first and g == 2:
                            z3_mask(pair - 1)
                        if r % 2 == 0 and not first and g == 3:
                            out_copy(pair - 1, u, i - 1)
                        if g == 0 and (r > 0 or not first) and not (last and r == QUAD - 1):
                            q_part(pair + r % 2, (u + r % 2) % 2, (r + 1) % 2)
                        exponents(b, r, g)
                        if tail and g == 0:
                            o_copy(pair)
                        if before and g % 2 == 1:
                            probs_copy(b, g)
                        if after:
                            keys_part(b + 1, r + 1, g)
                        if after and g == 1:
                            mask_distance(b + 1, r + 1)
                        if tail and g == 3:
                            x3_copy(pair)

            for i in range(2):
                act.sem_inc(out_stored[i], 16)
            mask_distance(0, 0)
            for g in range(G):
                keys_part(0, 0, g)
            for step in range(2):
                q_part(0, 0, step)
            quads(act, body)
            z3_mask(PAIRS - 1)
            probs_copy(B, 1)
            out_copy(PAIRS - 1, 0, QUADS - 1)
            probs_copy(B, 3)
            o_copy(PAIRS)
            x3_copy(PAIRS)
            z3_mask(PAIRS)
            out_copy(PAIRS, 1, QUADS - 1)

        @block.vector
        def _(dve):
            v = nc.vector

            def mask_far(row, r):
                dve.wait_ge(distances, row + 1)
                v.tensor_scalar(mask[r % 2][:], mask[r % 2][:], s["half"][:, one(row)], MASKED,
                                ALU.is_gt, ALU.mult).then_inc(mask_step, 1)

            def probs_copy(b, g):
                dve.wait_ge(probs_mm, G * (b - 1) + g + 1)
                wait(dve, values_mm, 2 * (b - 2) + g // 2 + 1)
                v.tensor_copy(pt[g][:].rearrange("p o c -> p (o c)"), pt_ps[0][0:JQ, :]).then_inc(probs_out[0], 1)

            def inverse(n, r, g):
                dve.wait_ge(exped, n)
                v.reciprocal(rinv[:, r % 2, g:g + 1], rsum[:, r % 2, g:g + 1]).then_inc(summed, 1)

            def lowest(r, g):
                v.tensor_tensor_reduce(prob[r % 2][:, g, :], s_ps[g % 2][:, 0:NPOS], mask[r % 2][:], 1.0, 3e38,
                                       ALU.add, ALU.min, low[:, r % 2, g:g + 1]).then_inc(masked, 1)

            def normalise(n, r, g):
                dve.wait_ge(summed, n)
                p = prob[r % 2][:, g, :]
                v.tensor_scalar(p, p, rinv[:, r % 2, g:g + 1], None, ALU.mult).then_inc(normed, 1)

            def keys_rest(n, rn, g):
                dve.wait_ge(keys_high, G * n + g + 1)
                at = slice(64 * (g % 2), 64 * (g % 2) + 64)
                other = slice(64 - 64 * (g % 2), 128 - 64 * (g % 2))
                v.tensor_tensor(ks[rn % 2][other, g, :], kt_ps[g // 2][at, 0:NPOS],
                                ks[rn % 2][at, g, :].bitcast(F32), ALU.subtract).then_inc(keys_out, 1)

            def q_rest(pair, u, step):
                dve.wait_ge(q_high, 2 * pair + step + 1)
                h = 4 * step
                v.tensor_tensor(qs[u][:, 1, :, h:h + 4, :], m_ps[:].rearrange("p (h b t) -> p b h t", h=4, b=2),
                                qs[u][:, 0, :, h:h + 4, :].bitcast(F32), ALU.subtract).then_inc(q_out, 1)

            def x3_add(pair, u, uses):
                dve.wait_ge(wo_mm, pair)
                dve.wait_ge(x2_in[u], 16 * uses)
                v.tensor_tensor(x3[:], m_ps[:].rearrange("p (k n) -> p k n", k=KC), x2[u][:], ALU.add)\
                    .then_inc(x3_sum, 1)

            def x3_rest(pair):
                dve.wait_ge(x3_high, pair)
                v.tensor_tensor(x3l[:], x3[:], x3h[:].bitcast(F32), ALU.subtract).then_inc(x3_low, 1)

            def body(i, first, last):
                for r in range(QUAD):
                    b, pair, u = QUAD * i + r, 2 * i + r // 2, r // 2
                    before, after = not (first and r == 0), not (last and r == QUAD - 1)
                    tail = r % 2 == 1 and not (first and u == 0)
                    for g in range(G):
                        if g == 0 and (r > 0 or not first) and not (last and r == QUAD - 1):
                            q_rest(pair + r % 2, (u + r % 2) % 2, (r + 1) % 2)
                        if before and g % 2 == 0:
                            probs_copy(b, g)
                        prev = (G * b + g, r, g - 1) if g > 0 else (G * b, r - 1, G - 1)
                        dve.wait_ge(scores_mm, G * b + g + 1)
                        if g == 0:
                            dve.wait_ge(mask_step, b + 1)
                        if g > 0 or before:
                            inverse(*prev)
                        lowest(r, g)
                        if g > 0 or before:
                            normalise(*prev)
                        if g == 0:
                            keys_rest(b, r, 3)
                        elif after:
                            keys_rest(b + 1, r + 1, g - 1)
                        if tail and g == 2:
                            x3_add(pair, (u + 1) % 2, i + u)
                        if tail and g == 3:
                            x3_rest(pair)
                        if after and g == 3:
                            mask_far(b + 1, r + 1)

            mask_far(0, 0)
            for g in range(3):
                keys_rest(0, 0, g)
            for step in range(2):
                q_rest(0, 0, step)
            quads(dve, body)
            inverse(G * B, QUAD - 1, G - 1)
            normalise(G * B, QUAD - 1, G - 1)
            for g in (0, 2):
                probs_copy(B, g)
            x3_add(PAIRS, 1, QUADS)
            x3_rest(PAIRS)


def kernel(**inputs):
    import concourse.bacc as bacc
    from concourse.bass_utils import run_bass_kernel_spmd

    a = {k: np.asarray(v) for k, v in inputs.items()}

    def chunks(m):
        return m.reshape(KC, 128, m.shape[1]).transpose(1, 0, 2)

    def quarters(m):
        return m.transpose(0, 2, 1, 3).reshape(NCACHE * 4, ROW)

    def rows(m):
        return np.broadcast_to(m, (128,) + m.shape)

    conds, kv = (a["itok_B_1_198"], a["itok_B_0_3"], a["itok_B_0_6"]), a["itok_B_37_3939"]
    qk = [a["L2_cond_q_norm_scale"], a["L2_cond_k_norm_scale"]]
    hh = HD // 2
    p = np.arange(128)
    entry = np.arange(NE)
    order = (entry % B) * WR + entry // B
    inv = (np.float32(1) / np.float32(10000.0) ** (np.arange(hh, dtype=np.float32) / np.float32(hh))).astype(np.float32)
    ang = np.arange(MAXPOS, dtype=np.float32)[:, None] * inv
    cos, sin = np.cos(ang), np.sin(ang)
    o4, j, q = np.meshgrid(np.arange(4), np.arange(RD), np.arange(4), indexing="ij")
    laid = {
        "x_pairs": a["x"].reshape(PAIRS, 128, D),
        "l0w": a["L0_cond_weights"].reshape(CONDS * T, T),
        "wbt": chunks(a["L1_cond_W_base"].T), "wt": chunks(a["L1_cond_Wt"]), "wpt": chunks(a["L1_cond_Wp"].T),
        "at": chunks(a["L1_cond_A"].reshape(E1 * R, D).T),
        "bt": chunks(a["L1_cond_B_w"].transpose(1, 0, 2).reshape(D, E1 * R)),
        "wqt": chunks(a["L2_cond_Wq"].T),
        "wkvt": chunks(np.concatenate([a["L2_cond_Wk"].T, a["L2_cond_Wv"].T], axis=1)),
        "wot": a["L2_cond_Wo"].T.reshape(2, 2, 2, HD, D).transpose(1, 3, 0, 2, 4).reshape(128, KC, D),
        "w3t": chunks(a["L3_cond_W"].T),
        "a3t": chunks(a["L3_cond_A"].reshape(E3 * R, D).T),
        "b3": a["L3_cond_Bm"].transpose(0, 2, 1).reshape(E3 * R, D),
        "normscale": rows(np.stack([np.stack([m, np.concatenate([m[hh:], m[:hh]])]) for m in qk])),
        "k_rows": quarters(a["L2_cond_k_blocks"]),
        "v_rows": quarters(a["L2_cond_v_blocks"]),
        "kv_col": np.concatenate([kv, kv])[:, None],
        "table": np.concatenate([a["itok_Bx257_0_4111"]] * 2),
        "ints": rows(np.stack([kv, *conds])),
        "sc1": np.tile(np.repeat(a["L1_cond_scaling"], R), 2)[:, None],
        "sc3": np.repeat(a["L3_cond_scalings"], R)[:, None],
        "cols": np.stack([p % B, p % (E1 * R) // R, p // R, p // B], 1).astype(np.float32),
        "rows": rows(np.arange(512, dtype=np.float32)),
        "later": (np.arange(B)[:, None, None] * WR + np.arange(WR)[None, :, None] > order).astype(np.float32),
        "ident": np.eye(128, dtype=np.float32),
        "pcol": rows((16 * j + 4 * q + o4).reshape(-1).astype(np.float32)),
        "rope": np.concatenate([cos, cos, sin, sin], axis=1).astype(np.float32),
    }
    nc = bacc.Bacc("TRN2", target_bir_lowering=False, num_devices=1)
    arrays, t = {}, {}
    for name, m in laid.items():
        arrays[f"in_{name}"] = np.ascontiguousarray(m)
        t[name] = nc.dram_tensor(f"in_{name}", m.shape, mybir.dt.from_np(m.dtype), kind="ExternalInput").ap()
    t["out_pairs"] = nc.dram_tensor("out", (PAIRS, 128, D), F32, kind="ExternalOutput").ap()
    program(nc, t)
    r = run_bass_kernel_spmd(nc, [arrays], core_ids=[0])
    return r.results[0]["out"].reshape(B, T, D)
```
